# Optimizing a Trainium2 kernel written in Bass

```python
import numpy as np
import jax
import jax.numpy as jnp

def _softmax(x, axis=-1):
    return jax.nn.softmax(x, axis=axis)

def _gelu(x):
    return jax.nn.gelu(x, approximate=True)

def _silu(x):
    return jax.nn.silu(x)

def _sigmoid(x):
    return jax.nn.sigmoid(x)

def _layernorm(x, axis=-1, eps=1e-05):
    m = jnp.mean(x, axis=axis, keepdims=True)
    v = jnp.var(x, axis=axis, keepdims=True)
    return (x - m) / jnp.sqrt(v + eps)

def _scatter_add(tgt, idx, src, axis=0):
    return tgt.at[idx].add(src)

def _segment_sum(src, seg, n):
    return jax.ops.segment_sum(src, seg, n)
kernel_name = 'mk_hybrid_d1_jaxref_r8_bd9ab5'

def setup_inputs(seed: int=0):
    np.random.seed(seed)
    _w = jnp.asarray

    def _L0_attn_a_setup():
        import jax, jax.numpy as jnp
        import numpy as np
        D_MODEL = 256
        NUM_HEADS = 16
        D_KV = D_MODEL // NUM_HEADS
        THETA = 10000.0
        N_LORA = 4
        RANK = 16
        BATCH = 2
        SEQ = 256

        def _adapter_ids(starts, batch):
            ids = jnp.searchsorted(starts, jnp.arange(batch), side='right') - 1
            return jnp.clip(ids, 0, starts.shape[0] - 1)

        def _multilora(x, ids, W, A, B):
            base = jnp.einsum('bsd,od->bso', x, W)
            Ai, Bi = (A[ids], B[ids])
            low = jnp.einsum('bsd,brd->bsr', x, Ai)
            return base + jnp.einsum('bsr,bor->bso', low, Bi)

        def _rope(x):
            d = x.shape[-1]
            pos = jnp.arange(x.shape[-2], dtype=jnp.float32)
            inv_freq = THETA ** (-jnp.arange(0, d, 2, dtype=jnp.float32) / d)
            ang = pos[:, None] * inv_freq[None, :]
            cos, sin = (jnp.cos(ang), jnp.sin(ang))
            x1, x2 = (x[..., 0::2], x[..., 1::2])
            o1 = x1 * cos - x2 * sin
            o2 = x1 * sin + x2 * cos
            return jnp.stack([o1, o2], axis=-1).reshape(x.shape)
        key = jax.random.key(seed)
        ks = jax.random.split(key, 16)
        s = 0.02
        inp = {'x': jax.random.normal(ks[0], (BATCH, SEQ, D_MODEL), jnp.float32), 'lora_start_indices': jnp.sort(jax.random.randint(ks[1], (N_LORA,), 0, BATCH)), 'Wq': jax.random.normal(ks[2], (D_MODEL, D_MODEL), jnp.float32) * s, 'Aq': jax.random.normal(ks[3], (N_LORA, RANK, D_MODEL), jnp.float32) * s, 'Bq': jax.random.normal(ks[4], (N_LORA, D_MODEL, RANK), jnp.float32) * s, 'Wk': jax.random.normal(ks[5], (D_MODEL, D_MODEL), jnp.float32) * s, 'Ak': jax.random.normal(ks[6], (N_LORA, RANK, D_MODEL), jnp.float32) * s, 'Bk': jax.random.normal(ks[7], (N_LORA, D_MODEL, RANK), jnp.float32) * s, 'Wv': jax.random.normal(ks[8], (D_MODEL, D_MODEL), jnp.float32) * s, 'Av': jax.random.normal(ks[9], (N_LORA, RANK, D_MODEL), jnp.float32) * s, 'Bv': jax.random.normal(ks[10], (N_LORA, D_MODEL, RANK), jnp.float32) * s, 'Wo': jax.random.normal(ks[11], (D_MODEL, D_MODEL), jnp.float32) * s, 'Ao': jax.random.normal(ks[12], (N_LORA, RANK, D_MODEL), jnp.float32) * s, 'Bo': jax.random.normal(ks[13], (N_LORA, D_MODEL, RANK), jnp.float32) * s}
        return inp
    _L0_attn_a_in = _L0_attn_a_setup()

    def _L0_attn_b_setup():
        import jax, jax.numpy as jnp
        import numpy as np
        D_MODEL = 256
        D_STATE = 128
        HEADDIM = 64
        EXPAND = 2
        D_CONV = 4
        NGROUPS = 1
        CHUNK = 32
        EPS = 1e-05
        D_INNER = EXPAND * D_MODEL
        NHEADS = D_INNER // HEADDIM
        CONV_DIM = D_INNER + 2 * NGROUPS * D_STATE
        D_IN_PROJ = 2 * D_INNER + 2 * NGROUPS * D_STATE + NHEADS

        def _segsum(a):
            T = a.shape[-1]
            cs = jnp.cumsum(a, axis=-1)
            d = cs[..., :, None] - cs[..., None, :]
            mask = jnp.tril(jnp.ones((T, T), dtype=bool))
            return jnp.where(mask, d, -jnp.inf)

        def _ssd(X, A, Bm, Cm):
            b, l, h, p = X.shape
            n = Bm.shape[-1]
            c = l // CHUNK
            X = X.reshape(b, c, CHUNK, h, p)
            A = A.reshape(b, c, CHUNK, h).transpose(0, 3, 1, 2)
            Bm = Bm.reshape(b, c, CHUNK, n)
            Cm = Cm.reshape(b, c, CHUNK, n)
            A_cs = jnp.cumsum(A, axis=-1)
            Lmat = jnp.exp(_segsum(A))
            Y_diag = jnp.einsum('bcln,bcsn,bhcls,bcshp->bclhp', Cm, Bm, Lmat, X)
            decay_states = jnp.exp(A_cs[..., -1:] - A_cs)
            states = jnp.einsum('bcln,bhcl,bclhp->bchpn', Bm, decay_states, X)
            A_last = jnp.pad(A_cs[..., -1], ((0, 0), (0, 0), (1, 0)))
            decay_chunk = jnp.exp(_segsum(A_last))
            states = jnp.concatenate([jnp.zeros_like(states[:, :1]), states], axis=1)
            states = jnp.einsum('bhzc,bchpn->bzhpn', decay_chunk, states)[:, :-1]
            Y_off = jnp.einsum('bchpn,bcln,bhcl->bclhp', states, Cm, jnp.exp(A_cs))
            return (Y_diag + Y_off).reshape(b, l, h, p)

        def _mamba2(x, w_in, conv_w, conv_b, dt_bias, A_log, D, norm_w, w_out):
            B, L, _ = x.shape
            zxbcdt = jnp.einsum('bld,de->ble', x, w_in)
            z = zxbcdt[..., :D_INNER]
            xBC = zxbcdt[..., D_INNER:D_INNER + CONV_DIM]
            dt = zxbcdt[..., D_INNER + CONV_DIM:]
            dt = jax.nn.softplus(dt + dt_bias)
            xp = jnp.pad(xBC, ((0, 0), (D_CONV - 1, 0), (0, 0)))
            acc = conv_b
            xBC = sum((conv_w[:, k] * xp[:, k:k + L, :] for k in range(D_CONV))) + conv_b
            xBC = jax.nn.silu(xBC)
            xh = xBC[..., :D_INNER].reshape(B, L, NHEADS, HEADDIM)
            Bm = xBC[..., D_INNER:D_INNER + NGROUPS * D_STATE]
            Cm = xBC[..., D_INNER + NGROUPS * D_STATE:]
            A = -jnp.exp(A_log)
            y = _ssd(xh * dt[..., None], dt * A, Bm, Cm)
            y = y + xh * D[None, None, :, None]
            y = y.reshape(B, L, D_INNER)
            y = y * jax.nn.silu(z)
            y = y * jax.lax.rsqrt(jnp.mean(y * y, axis=-1, keepdims=True) + EPS) * norm_w
            return jnp.einsum('ble,ed->bld', y, w_out)
        key = jax.random.key(seed)
        ks = jax.random.split(key, 9)
        B, L = (2, 256)
        x = jax.random.normal(ks[0], (B, L, D_MODEL), jnp.float32)
        w_in = jax.random.normal(ks[1], (D_MODEL, D_IN_PROJ), jnp.float32) * D_MODEL ** (-0.5)
        conv_w = jax.random.normal(ks[2], (CONV_DIM, D_CONV), jnp.float32) * 0.2
        conv_b = jnp.zeros((CONV_DIM,), jnp.float32)
        dt_bias = jax.random.uniform(ks[3], (NHEADS,), jnp.float32, -4.0, -1.0)
        A_log = jnp.log(jax.random.uniform(ks[4], (NHEADS,), jnp.float32, 1.0, 16.0))
        D = jnp.ones((NHEADS,), jnp.float32)
        norm_w = jnp.ones((D_INNER,), jnp.float32)
        w_out = jax.random.normal(ks[5], (D_INNER, D_MODEL), jnp.float32) * D_INNER ** (-0.5)
        return {'x': x, 'w_in': w_in, 'conv_w': conv_w, 'conv_b': conv_b, 'dt_bias': dt_bias, 'A_log': A_log, 'D': D, 'norm_w': norm_w, 'w_out': w_out}
    _L0_attn_b_in = _L0_attn_b_setup()

    def _L0_ffn_setup():
        import jax, jax.numpy as jnp
        import numpy as np
        D_MODEL = 256
        D_FF = 1024
        N_EXPERTS = 4
        B, S = (2, 256)
        key = jax.random.key(seed)
        ks = jax.random.split(key, 6)
        scale = 0.02
        return {'hidden_states': jax.random.normal(ks[0], (B, S, D_MODEL), dtype=jnp.float32), 'Wr': jax.random.normal(ks[1], (D_MODEL, N_EXPERTS), dtype=jnp.float32) * scale, 'br': jnp.zeros((N_EXPERTS,), dtype=jnp.float32), 'Wg': jax.random.normal(ks[2], (N_EXPERTS, D_MODEL, D_FF), dtype=jnp.float32) * scale, 'Wu': jax.random.normal(ks[3], (N_EXPERTS, D_MODEL, D_FF), dtype=jnp.float32) * scale, 'Wd': jax.random.normal(ks[4], (N_EXPERTS, D_FF, D_MODEL), dtype=jnp.float32) * scale}
    _L0_ffn_in = _L0_ffn_setup()
    _d = {'L0_attn_a_x': _L0_attn_a_in['x'], 'L0_attn_a_lora_start_indices': _L0_attn_a_in['lora_start_indices'], 'L0_attn_a_Wq': _L0_attn_a_in['Wq'], 'L0_attn_a_Aq': _L0_attn_a_in['Aq'], 'L0_attn_a_Bq': _L0_attn_a_in['Bq'], 'L0_attn_a_Wk': _L0_attn_a_in['Wk'], 'L0_attn_a_Ak': _L0_attn_a_in['Ak'], 'L0_attn_a_Bk': _L0_attn_a_in['Bk'], 'L0_attn_a_Wv': _L0_attn_a_in['Wv'], 'L0_attn_a_Av': _L0_attn_a_in['Av'], 'L0_attn_a_Bv': _L0_attn_a_in['Bv'], 'L0_attn_a_Wo': _L0_attn_a_in['Wo'], 'L0_attn_a_Ao': _L0_attn_a_in['Ao'], 'L0_attn_a_Bo': _L0_attn_a_in['Bo'], 'L0_attn_b_w_in': _L0_attn_b_in['w_in'], 'L0_attn_b_conv_w': _L0_attn_b_in['conv_w'], 'L0_attn_b_conv_b': _L0_attn_b_in['conv_b'], 'L0_attn_b_dt_bias': _L0_attn_b_in['dt_bias'], 'L0_attn_b_A_log': _L0_attn_b_in['A_log'], 'L0_attn_b_D': _L0_attn_b_in['D'], 'L0_attn_b_norm_w': _L0_attn_b_in['norm_w'], 'L0_attn_b_w_out': _L0_attn_b_in['w_out'], 'L0_ffn_Wr': _L0_ffn_in['Wr'], 'L0_ffn_br': _L0_ffn_in['br'], 'L0_ffn_Wg': _L0_ffn_in['Wg'], 'L0_ffn_Wu': _L0_ffn_in['Wu'], 'L0_ffn_Wd': _L0_ffn_in['Wd']}
    _x0 = _d['L0_attn_a_x']
    _d['L0_attn_a_x'] = jax.random.normal(jax.random.fold_in(jax.random.key(seed), 1), (4, 1024, 256), dtype=_x0.dtype)
    del _x0
    return _d

def reference(L0_attn_a_x, L0_attn_a_lora_start_indices, L0_attn_a_Wq, L0_attn_a_Aq, L0_attn_a_Bq, L0_attn_a_Wk, L0_attn_a_Ak, L0_attn_a_Bk, L0_attn_a_Wv, L0_attn_a_Av, L0_attn_a_Bv, L0_attn_a_Wo, L0_attn_a_Ao, L0_attn_a_Bo, L0_attn_b_w_in, L0_attn_b_conv_w, L0_attn_b_conv_b, L0_attn_b_dt_bias, L0_attn_b_A_log, L0_attn_b_D, L0_attn_b_norm_w, L0_attn_b_w_out, L0_ffn_Wr, L0_ffn_br, L0_ffn_Wg, L0_ffn_Wu, L0_ffn_Wd):

    def _L0_attn_a_ref(x, lora_start_indices, Wq, Aq, Bq, Wk, Ak, Bk, Wv, Av, Bv, Wo, Ao, Bo):
        import jax, jax.numpy as jnp
        import numpy as np
        D_MODEL = 256
        NUM_HEADS = 16
        D_KV = D_MODEL // NUM_HEADS
        THETA = 10000.0
        N_LORA = 4
        RANK = 16
        BATCH = 2
        SEQ = 256

        def _adapter_ids(starts, batch):
            ids = jnp.searchsorted(starts, jnp.arange(batch), side='right') - 1
            return jnp.clip(ids, 0, starts.shape[0] - 1)

        def _multilora(x, ids, W, A, B):
            base = jnp.einsum('bsd,od->bso', x, W)
            Ai, Bi = (A[ids], B[ids])
            low = jnp.einsum('bsd,brd->bsr', x, Ai)
            return base + jnp.einsum('bsr,bor->bso', low, Bi)

        def _rope(x):
            d = x.shape[-1]
            pos = jnp.arange(x.shape[-2], dtype=jnp.float32)
            inv_freq = THETA ** (-jnp.arange(0, d, 2, dtype=jnp.float32) / d)
            ang = pos[:, None] * inv_freq[None, :]
            cos, sin = (jnp.cos(ang), jnp.sin(ang))
            x1, x2 = (x[..., 0::2], x[..., 1::2])
            o1 = x1 * cos - x2 * sin
            o2 = x1 * sin + x2 * cos
            return jnp.stack([o1, o2], axis=-1).reshape(x.shape)
        b, s, _ = x.shape
        ids = _adapter_ids(lora_start_indices, b)
        Q = _multilora(x, ids, Wq, Aq, Bq)
        K = _multilora(x, ids, Wk, Ak, Bk)
        V = _multilora(x, ids, Wv, Av, Bv)
        split = lambda t: t.reshape(b, s, NUM_HEADS, D_KV).transpose(0, 2, 1, 3)
        Q, K, V = (split(Q), split(K), split(V))
        Q, K = (_rope(Q), _rope(K))
        scores = jnp.einsum('bhqd,bhkd->bhqk', Q, K) / jnp.sqrt(jnp.asarray(D_KV, x.dtype))
        causal = jnp.tril(jnp.ones((s, s), bool))
        scores = jnp.where(causal, scores, jnp.asarray(-jnp.inf, scores.dtype))
        attn = jax.nn.softmax(scores, axis=-1)
        out = jnp.einsum('bhqk,bhkd->bhqd', attn, V)
        out = out.transpose(0, 2, 1, 3).reshape(b, s, D_MODEL)
        return _multilora(out, ids, Wo, Ao, Bo)

    def _L0_attn_b_ref(x, w_in, conv_w, conv_b, dt_bias, A_log, D, norm_w, w_out):
        import jax, jax.numpy as jnp
        import numpy as np
        D_MODEL = 256
        D_STATE = 128
        HEADDIM = 64
        EXPAND = 2
        D_CONV = 4
        NGROUPS = 1
        CHUNK = 32
        EPS = 1e-05
        D_INNER = EXPAND * D_MODEL
        NHEADS = D_INNER // HEADDIM
        CONV_DIM = D_INNER + 2 * NGROUPS * D_STATE
        D_IN_PROJ = 2 * D_INNER + 2 * NGROUPS * D_STATE + NHEADS

        def _segsum(a):
            T = a.shape[-1]
            cs = jnp.cumsum(a, axis=-1)
            d = cs[..., :, None] - cs[..., None, :]
            mask = jnp.tril(jnp.ones((T, T), dtype=bool))
            return jnp.where(mask, d, -jnp.inf)

        def _ssd(X, A, Bm, Cm):
            b, l, h, p = X.shape
            n = Bm.shape[-1]
            c = l // CHUNK
            X = X.reshape(b, c, CHUNK, h, p)
            A = A.reshape(b, c, CHUNK, h).transpose(0, 3, 1, 2)
            Bm = Bm.reshape(b, c, CHUNK, n)
            Cm = Cm.reshape(b, c, CHUNK, n)
            A_cs = jnp.cumsum(A, axis=-1)
            Lmat = jnp.exp(_segsum(A))
            Y_diag = jnp.einsum('bcln,bcsn,bhcls,bcshp->bclhp', Cm, Bm, Lmat, X)
            decay_states = jnp.exp(A_cs[..., -1:] - A_cs)
            states = jnp.einsum('bcln,bhcl,bclhp->bchpn', Bm, decay_states, X)
            A_last = jnp.pad(A_cs[..., -1], ((0, 0), (0, 0), (1, 0)))
            decay_chunk = jnp.exp(_segsum(A_last))
            states = jnp.concatenate([jnp.zeros_like(states[:, :1]), states], axis=1)
            states = jnp.einsum('bhzc,bchpn->bzhpn', decay_chunk, states)[:, :-1]
            Y_off = jnp.einsum('bchpn,bcln,bhcl->bclhp', states, Cm, jnp.exp(A_cs))
            return (Y_diag + Y_off).reshape(b, l, h, p)

        def _mamba2(x, w_in, conv_w, conv_b, dt_bias, A_log, D, norm_w, w_out):
            B, L, _ = x.shape
            zxbcdt = jnp.einsum('bld,de->ble', x, w_in)
            z = zxbcdt[..., :D_INNER]
            xBC = zxbcdt[..., D_INNER:D_INNER + CONV_DIM]
            dt = zxbcdt[..., D_INNER + CONV_DIM:]
            dt = jax.nn.softplus(dt + dt_bias)
            xp = jnp.pad(xBC, ((0, 0), (D_CONV - 1, 0), (0, 0)))
            acc = conv_b
            xBC = sum((conv_w[:, k] * xp[:, k:k + L, :] for k in range(D_CONV))) + conv_b
            xBC = jax.nn.silu(xBC)
            xh = xBC[..., :D_INNER].reshape(B, L, NHEADS, HEADDIM)
            Bm = xBC[..., D_INNER:D_INNER + NGROUPS * D_STATE]
            Cm = xBC[..., D_INNER + NGROUPS * D_STATE:]
            A = -jnp.exp(A_log)
            y = _ssd(xh * dt[..., None], dt * A, Bm, Cm)
            y = y + xh * D[None, None, :, None]
            y = y.reshape(B, L, D_INNER)
            y = y * jax.nn.silu(z)
            y = y * jax.lax.rsqrt(jnp.mean(y * y, axis=-1, keepdims=True) + EPS) * norm_w
            return jnp.einsum('ble,ed->bld', y, w_out)
        return x + _mamba2(x, w_in, conv_w, conv_b, dt_bias, A_log, D, norm_w, w_out)

    def _L0_ffn_ref(hidden_states, Wr, br, Wg, Wu, Wd):
        import jax, jax.numpy as jnp
        import numpy as np
        D_MODEL = 256
        D_FF = 1024
        N_EXPERTS = 4
        B, S = (2, 256)
        b, s, d = hidden_states.shape
        x = hidden_states.reshape(-1, d)
        logits = x @ Wr + br
        probs = jax.nn.softmax(logits, axis=-1)
        top_w, top_idx = jax.lax.top_k(probs, 1)
        g = jnp.einsum('td,edf->tef', x, Wg)
        u = jnp.einsum('td,edf->tef', x, Wu)
        h = jax.nn.silu(g) * u
        y = jnp.einsum('tef,efd->ted', h, Wd)
        sel = jnp.take_along_axis(y, top_idx[:, :, None], axis=1)[:, 0]
        out = sel * top_w
        return out.reshape(b, s, d)
    x = L0_attn_a_x
    x = x + _L0_attn_a_ref(_layernorm(x, axis=-1), L0_attn_a_lora_start_indices, L0_attn_a_Wq, L0_attn_a_Aq, L0_attn_a_Bq, L0_attn_a_Wk, L0_attn_a_Ak, L0_attn_a_Bk, L0_attn_a_Wv, L0_attn_a_Av, L0_attn_a_Bv, L0_attn_a_Wo, L0_attn_a_Ao, L0_attn_a_Bo)
    x = x + _L0_ffn_ref(_layernorm(x, axis=-1), L0_ffn_Wr, L0_ffn_br, L0_ffn_Wg, L0_ffn_Wu, L0_ffn_Wd)
    x = x + _L0_attn_b_ref(_layernorm(x, axis=-1), L0_attn_b_w_in, L0_attn_b_conv_w, L0_attn_b_conv_b, L0_attn_b_dt_bias, L0_attn_b_A_log, L0_attn_b_D, L0_attn_b_norm_w, L0_attn_b_w_out)
    x = x + _L0_ffn_ref(_layernorm(x, axis=-1), L0_ffn_Wr, L0_ffn_br, L0_ffn_Wg, L0_ffn_Wu, L0_ffn_Wd)
    return x

_drawn_inputs = setup_inputs


def setup_inputs(seed=0):
    import zlib

    import numpy as np

    out = dict(_drawn_inputs(seed))
    spreads = {'L0_attn_b_conv_b': (0.0, 0.1),
     'L0_attn_b_D': (1.0, 0.2),
     'L0_attn_b_norm_w': (1.0, 0.2),
     'L0_ffn_br': (0.0, 0.8)}
    factors = {'L0_attn_a_Wq': 8.0,
     'L0_attn_a_Aq': 8.0,
     'L0_attn_a_Bq': 8.0,
     'L0_attn_a_Wk': 8.0,
     'L0_attn_a_Ak': 8.0,
     'L0_attn_a_Bk': 8.0,
     'L0_attn_a_Wv': 5.7,
     'L0_attn_a_Av': 8.0,
     'L0_attn_a_Bv': 8.0,
     'L0_attn_a_Wo': 5.645,
     'L0_attn_a_Ao': 8.0,
     'L0_attn_a_Bo': 8.0,
     'L0_ffn_Wr': 4.087,
     'L0_ffn_Wg': 3.426,
     'L0_ffn_Wu': 3.386,
     'L0_ffn_Wd': 3.381}
    for name, (base, spread) in spreads.items():
        noise = np.random.default_rng([zlib.crc32(name.encode()), seed]).standard_normal(out[name].shape)
        drawn = base * np.exp(spread * noise) if base else spread * noise
        out[name] = jnp.asarray(drawn.astype(out[name].dtype))
    for name, factor in factors.items():
        out[name] = (out[name] * factor).astype(out[name].dtype)
    return out
```

```python
from contextlib import ExitStack

import numpy as np

import concourse.bass as bass
from concourse import mybir

F32 = mybir.dt.float32
F32R = mybir.dt.float32r
BF16 = mybir.dt.bfloat16
I32 = mybir.dt.int32
U32 = mybir.dt.uint32
ALU = mybir.AluOpType
ACT = mybir.ActivationFunctionType
AX = mybir.AxisListType.X

P = 128
BATCH, SEQ, D = 4, 1024, 256
DT = D // P
T = SEQ // P
NT = BATCH * T
HEADS, DH = 16, 16
GROUP = 4
GROUPS = HEADS // GROUP
ADAPTERS, RANK = 4, 16
EXPERTS, FF = 4, 1024
SLOTS = NT + EXPERTS - 1
LN_EPS = 1e-5
MASKED = -1e30
STATE, INNER, CONV, TAPS, MHEADS, HDIM = 128, 512, 768, 4, 8, 64
CT = CONV // P
IN_PROJ = 2 * INNER + 2 * STATE + MHEADS


class Semaphores:

    def __init__(self, nc, ctx):
        self.nc, self.ctx, self.held = nc, ctx, {}

    def __call__(self, name):
        if name not in self.held:
            self.held[name] = self.ctx.enter_context(self.nc.semaphore(name))
        return self.held[name]

    def clear(self, prefix):
        with self.nc.Block() as block:
            @block.sync
            def _(sp):
                for name, held in self.held.items():
                    if name.startswith(prefix):
                        sp.sem_clear(held)


class Steps:

    def __init__(self, eng, sem, base=0):
        self.eng, self.sem, self.base, self.n = eng, sem, base, 0

    def __call__(self, ins, wait=True):
        ins.then_inc(self.sem, 1)
        self.n += 1
        if wait:
            self.eng.wait_ge(self.sem, self.base + self.n)


def row_stats(nc, step, tiles, stats, mean_var, var_eps, done):
    for t, x in enumerate(tiles):
        step(nc.vector.bn_stats(stats[:, t], x), wait=t + 1 == len(tiles))
    step(nc.vector.memset(var_eps, 0.0), wait=False)
    for t in range(len(tiles)):
        step(nc.vector.bn_aggr(mean_var[:, t], stats[:, t]), wait=t + 1 == len(tiles))
    nc.vector.tensor_scalar(var_eps, mean_var[:, :, 1], LN_EPS, None, ALU.add).then_inc(done, 1)


def inverse_root(nc, out, x, C):
    return nc.gpsimd.tensor_tensor(out, x, C["minus_half"].to_broadcast(list(out.shape)), ALU.pow)


def attention(nc, X, C, A):
    STACK = 64
    PAIRS = HEADS // 2
    RING = 8
    CHUNKS = sum(1 + (i >= T // 2) for i in range(T)) * GROUP
    UNITS = T * GROUP
    with ExitStack() as ctx:
        def sb(name, shape, dt=F32):
            return ctx.enter_context(nc.sbuf_tensor("a_" + name, shape, dt))

        def sem(name):
            return C["sems"]("a_" + name)

        ps_e = ctx.enter_context(nc.psum_tensor("a_ps_e", [P, 2, 2, 512], F32))
        ps_m = ctx.enter_context(nc.psum_tensor("a_ps_m", [P, 2, 512], F32))
        ps_a = ctx.enter_context(nc.psum_tensor("a_ps_a", [P, 2, 512], F32))

        probs = sb("probs", [P, RING, SEQ])
        spare = probs[:].rearrange("p r q -> p (r q)")
        w_nat = spare[:, 0:2048].rearrange("p (m t d) -> p m t d", m=4, t=2)
        b_nat = spare[:, 2048:2560].rearrange("p (m t e r) -> p m t e r", m=4, t=2, e=ADAPTERS)
        k_tok = spare[:, 3072:5120].bitcast(F32R).rearrange("p (a h c) -> p a h c", a=2, h=HEADS)
        rot = spare[:, 5120:6144].rearrange("p (a b d) -> p a b d", a=2, b=2)
        rope_a, rope_b = spare[:, 6144:6656], spare[:, 6656:7168]
        xn = spare[:, 7168:7680].rearrange("p (a d) -> p a d", a=2)
        xn_t = spare[:, 7680:8192].rearrange("p (a d) -> p a d", a=2)
        acc = probs[:, RING - 1, :]
        a_cat = sb("a_cat", [64, 4, D])
        w_t = sb("w_t", [P, 4, DT, D])
        b_t = sb("b_t", [64, 4, D])
        w_eff = sb("w_eff", [P, DT, 4, D])
        starts_i = sb("starts_i", [64, ADAPTERS], I32)
        starts = sb("starts", [64, ADAPTERS])
        picked = sb("picked", [64, 4, BATCH])
        ident_b = sb("ident_b", [P, P], BF16)
        mask_b = sb("mask_b", [P, 2, P], BF16)
        rope = sb("rope", [P, T, 2, DH])
        stats = sb("stats", [P, T, 6])
        mean_var = sb("mean_var", [P, T, 2])
        var_eps = sb("var_eps", [P, T])
        rstd = sb("rstd", [P, T])
        q_tok = sb("q_tok", [P, T, HEADS, STACK], F32R)
        q_st = sb("q_st", [P, PAIRS, SEQ], F32R)
        k_st = sb("k_st", [P, PAIRS, SEQ], F32R)
        vals = sb("vals", [P, T, (HEADS + 1) * 17])
        peak = sb("peak", [P, GROUP, T, 2])
        recip = sb("recip", [P, T * GROUP])
        heads_out = sb("heads_out", [P, T, D])
        ho_t = sb("ho_t", [P, D])
        a_sel = heads_out[0:64].rearrange("p (m t) d -> p m (t d)", m=4)[:, :, 0:D]

        loaded, fixed, folded, cast, w_ready = (sem(n) for n in ("loaded", "fixed", "folded", "cast", "w_ready"))
        dve_step, wt_ps, wt_sb, sel_ready, wl_ps, wl_used = (
            sem(n) for n in ("dve_step", "wt_ps", "wt_sb", "sel_ready", "wl_ps", "wl_used"))
        xn_ready, xt_ps, xt_sb, qkv_ps, rot_ready, v_copied = (
            sem(n) for n in ("xn_ready", "xt_ps", "xt_sb", "qkv_ps", "rot_ready", "v_copied"))
        hi_ready, lo_ready, ks_ps, ks_sb, qs_ps, qs_sb = (
            sem(n) for n in ("hi_ready", "lo_ready", "ks_ps", "ks_sb", "qs_ps", "qs_sb"))
        score_ps, chunk_max, max_ready, again_ps, again_sb = (
            sem(n) for n in ("score_ps", "chunk_max", "max_ready", "again_ps", "again_sb"))
        shifted_ps, exp_done, pv_done, acc_sb, acc_t, normed = (
            sem(n) for n in ("shifted_ps", "exp_done", "pv_done", "acc_sb", "acc_t", "normed"))
        stats_ready, rstd_ready = sem("stats_ready"), sem("rstd_ready")
        ot_ps, ot_sb, proj_ps, x_added, half_turned = (
            sem(n) for n in ("ot_ps", "ot_sb", "proj_ps", "x_added", "half_turned"))

        LOADS = 4 * 3 + 2
        block = ctx.enter_context(nc.Block())

        @block.sync
        def _(sp):
            for m, name in enumerate("qkvo"):
                sp.dma_start(w_nat[:, m], A["W" + name].rearrange("(t p) d -> p t d", p=P)).then_inc(loaded, 16)
                for t in range(2):
                    sp.dma_start(b_nat[:, m, t], A["B" + name][:, t * P:(t + 1) * P, :].rearrange("e p r -> p e r")
                                 ).then_inc(loaded, 16)
                sp.dma_start(a_cat[:, m], A["A" + name].rearrange("e r d -> (e r) d")).then_inc(loaded, 16)
            sp.dma_start(starts_i[:], A["starts"].rearrange("(a n) -> a n", a=1).to_broadcast([64, ADAPTERS])
                         ).then_inc(loaded, 16)
            sp.dma_start(rope[:], A["rope"].rearrange("(t p) a f -> p t a f", p=P)).then_inc(loaded, 16)
            sp.wait_ge(loaded, 16 * (LOADS + 4))

        @block.vector
        def _(dve):
            dve.wait_ge(loaded, 16 * (LOADS + 4))
            step = Steps(dve, fixed)
            step(nc.vector.tensor_copy(ident_b[:], C["ident"]))
            step(nc.vector.tensor_copy(mask_b[:], C["neg"]))
            step(nc.vector.memset(q_tok[:].bitcast(F32), 0.0))
            step(nc.vector.memset(vals[:], 1.0))
            step(nc.vector.tensor_copy(starts[:], starts_i[:]))
            for b in range(BATCH):
                step(nc.vector.tensor_scalar(picked[:, 0, :], starts[:], float(b), None, ALU.is_le))
                step(nc.vector.tensor_reduce(picked[:, 1, 0:1], picked[:, 0, :], AX, ALU.add))
                step(nc.vector.tensor_scalar(picked[:, 2, 0:1], picked[:, 1, 0:1], -1.0, 0.0, ALU.add, ALU.max))
                step(nc.vector.tensor_scalar(picked[:, 3, b:b + 1], picked[:, 2, 0:1], C["adapter"][0:64, :], None,
                                             ALU.is_equal))
            for m in range(4):
                dve.wait_ge(wt_ps, m + 1)
                nc.vector.tensor_copy(w_t[:, m], ps_e[:, m // 2, m % 2, :]).then_inc(wt_sb, 1)
            for m in range(4):
                dve.wait_ge(wt_ps, 5 + m)
                nc.vector.tensor_copy(b_t[:, m], ps_e[0:64, m // 2, m % 2, 0:D]).then_inc(wt_sb, 1)
            dve.wait_ge(wt_sb, 8)
            dve.sem_inc(chunk_max, 2)
            dve.sem_inc(rot_ready, 1)
            dve.sem_inc(x_added, 1)
            dve.sem_inc(normed, 1)
            dve.sem_inc(qs_sb, 1)
            NSTEP = 2 * T + 1 + 2 * T + 3 + GROUPS * 3
            with dve.Fori(0, BATCH) as b:
                step = Steps(dve, dve_step, b * NSTEP)
                for m in range(4):
                    if m == 0:
                        dve.wait_ge(x_added, b * T + 1)
                    nc.vector.tensor_scalar(a_sel[:, m], a_cat[:, m], picked[:, 3, bass.ds(b, 1)], None,
                                            ALU.mult).then_inc(sel_ready, 1)
                for m in range(4):
                    dve.wait_ge(wl_ps, b * 4 + m + 1)
                    nc.vector.tensor_tensor(w_eff[:, :, m, :], w_t[:, m],
                                            ps_e[:, m // 2, m % 2, :].rearrange("p (t o) -> p t o", t=DT),
                                            ALU.add).then_inc(wl_used, 1)
                row_stats(nc, step, [X[:, bass.ds(b * T + t, 1), :].rearrange("p a d -> p (a d)") for t in range(T)],
                          stats, mean_var, var_eps[:], stats_ready)
                step(nc.vector.memset(q_tok[:, :, :, 32:34].bitcast(F32), 0.0))
                step(nc.vector.memset(k_tok.bitcast(F32), 0.0))
                step(nc.vector.memset(k_tok[:, :, :, 32:34].bitcast(F32), 1.0))

                def norm(t):
                    if t >= 2:
                        dve.wait_ge(xt_ps, b * T + t - 1)
                    if t == 0:
                        dve.wait_ge(rstd_ready, b + 1)
                    nc.vector.tensor_scalar(xn[:, t % 2], X[:, bass.ds(b * T + t, 1), :].rearrange("p a d -> p (a d)"),
                                            mean_var[:, t, 0:1], rstd[:, t:t + 1], ALU.subtract, ALU.mult
                                            ).then_inc(xn_ready, 1)

                def rotate(t):
                    dve.wait_ge(qkv_ps, b * T + t + 1)
                    qk = ps_e[:, 0, 0, :]
                    cos = rope[:, t, 0:1, :].to_broadcast([P, 2 * HEADS, DH])
                    sin = rope[:, t, 1, :].rearrange("p (i two) -> p two i", two=2)
                    step(nc.vector.tensor_tensor(rope_a.rearrange("p (h d) -> p h d", d=DH),
                                                 qk.rearrange("p (h d) -> p h d", d=DH), cos, ALU.mult))
                    pair = qk.rearrange("p (h i two) -> p two h i", two=2, i=DH // 2)
                    out = rope_b.rearrange("p (h i two) -> p two h i", two=2, i=DH // 2)
                    for odd in range(2):
                        last = nc.vector.tensor_tensor(
                            out[:, odd], pair[:, 1 - odd],
                            sin[:, odd:odd + 1, :].to_broadcast([P, 2 * HEADS, DH // 2]), ALU.mult)
                        if odd == 0:
                            last.then_inc(half_turned, 1)
                    step(last)
                    dve.wait_ge(half_turned, b * T + t + 1)
                    if t >= 2:
                        dve.wait_ge(lo_ready, b * T + t - 1)
                    nc.vector.tensor_tensor(rot[:, t % 2].rearrange("p a d -> p (a d)"), rope_a, rope_b,
                                            ALU.add).then_inc(rot_ready, 1)

                def queries(t):
                    dve.wait_ge(qs_ps, b * T + t + 1)
                    nc.vector.tensor_copy(q_st[:, :, t * P:(t + 1) * P],
                                          ps_m[:].rearrange("p b (c q) -> p (b c) q", q=P)).then_inc(qs_sb, 1)

                norm(0)
                for t in range(T):
                    if t + 1 < T:
                        norm(t + 1)
                    rotate(t)
                    if t >= 1:
                        queries(t - 1)
                queries(T - 1)

                def maxima(g, i):
                    for u in range(GROUP):
                        for c in range(1 + (i >= T // 2)):
                            n = (sum(1 + (x >= T // 2) for x in range(i)) * GROUP + u * (1 + (i >= T // 2)) + c)
                            dve.wait_ge(score_ps, (b * GROUPS + g) * CHUNKS + n + 1)
                            w = min(512, (i + 1) * P - 512 * c)
                            nc.vector.tensor_reduce(peak[:, u, i, c:c + 1], ps_m[:, n % 2, 0:w], AX, ALU.max
                                                    ).then_inc(chunk_max, 1)
                def fold(g):
                    dve.wait_ge(chunk_max, (b * GROUPS + g + 1) * CHUNKS + 2)
                    h = T // 2
                    step(nc.vector.tensor_tensor(peak[:, :, h:, 0], peak[:, :, h:, 0], peak[:, :, h:, 1], ALU.max))
                    to = q_tok[:, :, g * GROUP:(g + 1) * GROUP, :].rearrange("p t u c -> p u t c")
                    step(nc.vector.tensor_scalar(to[:, :, :, 32], peak[:, :, :, 0], -1.0, None, ALU.mult))
                    nc.vector.scalar_tensor_tensor(to[:, :, :, 33], peak[:, :, :, 0], -1.0,
                                                   to[:, :, :, 32].bitcast(F32), ALU.mult, ALU.subtract
                                                   ).then_inc(max_ready, 1)

                def collect(g):
                    dve.wait_ge(acc_t, b * GROUPS + g + 1)
                    if g == 0:
                        dve.wait_ge(x_added, b * T + 1)
                    at = ps_a[:].rearrange("p b (c u f) -> p (b c u) f", u=GROUP, f=32)
                    step(nc.vector.reciprocal(recip[:], at[:, :, 16]))
                    nc.vector.tensor_tensor(
                        heads_out[:, :, g * GROUP * DH:(g + 1) * GROUP * DH].rearrange("p t (u f) -> p t u f", f=DH),
                        at[:, :, 0:DH].rearrange("p (t u) f -> p t u f", u=GROUP),
                        recip[:].rearrange("p (t u) -> p t u", u=GROUP).unsqueeze(3).to_broadcast([P, T, GROUP, DH]),
                        ALU.mult).then_inc(normed, 1)

                for i in range(T):
                    maxima(0, i)
                fold(0)
                for g in range(GROUPS):
                    for j in range(T):
                        if g + 1 < GROUPS:
                            maxima(g + 1, j)
                        if j == 0 and g >= 1:
                            collect(g - 1)
                    if g + 1 < GROUPS:
                        fold(g + 1)
                collect(GROUPS - 1)
                for t in range(T):
                    dve.wait_ge(proj_ps, b * T + t + 1)
                    x = X[:, bass.ds(b * T + t, 1), :].rearrange("p a d -> p (a d)")
                    nc.vector.tensor_tensor(x, x, ps_m[:, 1, 0:D], ALU.add).then_inc(x_added, 1)
                dve.wait_ge(x_added, b * T + T + 1)
                assert step.n == NSTEP, step.n

        @block.gpsimd
        def _(pool):
            with pool.Fori(0, BATCH) as b:
                pool.wait_ge(stats_ready, b + 1)
                inverse_root(nc, rstd[:], var_eps[:], C).then_inc(rstd_ready, 1)
                for t in range(T):
                    r = rot[:, t % 2].rearrange("p a (h d) -> p a h d", d=DH)
                    pool.wait_ge(hi_ready, b * T + t + 1)
                    q, k = q_tok[:, t], k_tok[:, t % 2]
                    nc.gpsimd.tensor_tensor(q[:, :, 48:64], r[:, 0], q[:, :, 0:16].bitcast(F32), ALU.subtract)
                    nc.gpsimd.tensor_tensor(k[:, :, 16:32], r[:, 1], k[:, :, 0:16].bitcast(F32), ALU.subtract)
                    nc.gpsimd.tensor_copy(q[:, :, 16:32], q[:, :, 0:16].bitcast(F32))
                    nc.gpsimd.tensor_copy(k[:, :, 48:64], k[:, :, 0:16].bitcast(F32)).then_inc(lo_ready, 1)

        @block.scalar
        def _(act):
            act.sem_inc(exp_done, 2)
            act.sem_inc(xt_sb, 1)
            act.sem_inc(v_copied, 1)
            act.sem_inc(ks_sb, 1)
            act.sem_inc(ot_sb, 1)
            act.wait_ge(fixed, 4)
            with act.Fori(0, BATCH) as b:
                def high(t):
                    act.wait_ge(rot_ready, b * T + t + 2)
                    if t >= 2:
                        act.wait_ge(ks_ps, b * T + t - 1)
                    r = rot[:, t % 2].rearrange("p a (h d) -> p a h d", d=DH)
                    nc.scalar.copy(q_tok[:, t, :, 0:16], r[:, 0])
                    nc.scalar.copy(k_tok[:, t % 2, :, 0:16], r[:, 1]).then_inc(hi_ready, 1)

                def keys(t):
                    act.wait_ge(ks_ps, b * T + t + 1)
                    nc.scalar.copy(k_st[:, :, t * P:(t + 1) * P],
                                   ps_a[:].rearrange("p b (c k) -> p (b c) k", k=P)).then_inc(ks_sb, 1)

                for t in range(T):
                    act.wait_ge(xt_ps, b * T + t + 1)
                    nc.scalar.copy(xn_t[:, t % 2], ps_e[:, 1, 0, 0:D]).then_inc(xt_sb, 1)
                    if t >= 1:
                        high(t - 1)
                    act.wait_ge(qkv_ps, b * T + t + 1)
                    nc.scalar.copy(vals[:, t].rearrange("p (h c) -> p h c", c=17)[:, 0:HEADS, 0:DH], ps_e[:, 0, 1, 0:D].rearrange("p (h d) -> p h d", d=DH)
                                   ).then_inc(v_copied, 1)
                    if t >= 1:
                        keys(t - 1)
                high(T - 1)
                keys(T - 1)

                def again(g):
                    for n in range(4):
                        act.wait_ge(again_ps, (b * GROUPS + g) * 4 + n + 1)
                        nc.scalar.copy(q_st[:, 2 * g + n // 2, (n % 2) * 512:(n % 2) * 512 + 512], ps_m[:, n % 2, :]
                                       ).then_inc(again_sb, 1)

                again(0)
                for g in range(GROUPS):
                    for j in range(T):
                        for u in range(GROUP):
                            n = j * GROUP + u
                            at = (b * GROUPS + g) * UNITS + n
                            act.wait_ge(shifted_ps, at + 1)
                            k = n % RING
                            if g >= 1 and n == RING - 1:
                                act.wait_ge(acc_t, b * GROUPS + g)
                            if n >= RING:
                                act.wait_ge(pv_done, (b * GROUPS + g) * T + (n - RING) // GROUP + 1)
                            nc.scalar.activation(probs[:, k, j * P:],
                                                 ps_e[:, n % 2].rearrange("p b q -> p (b q)")[:, j * P:],
                                                 ACT.Exp, scale=DH ** -0.5).then_inc(exp_done, 1)
                    act.wait_ge(pv_done, (b * GROUPS + g) * T + T)
                    nc.scalar.copy(acc, ps_a[:].rearrange("p b q -> p (b q)")).then_inc(acc_sb, 1)
                    if g + 1 < GROUPS:
                        again(g + 1)
                for t in range(T):
                    act.wait_ge(ot_ps, b * T + t + 1)
                    nc.scalar.copy(ho_t[:], ps_m[:, 0, 0:D]).then_inc(ot_sb, 1)

        @block.tensor
        def _(pe):
            ident = C["ident"]
            pe.wait_ge(loaded, 16 * (LOADS + 4))
            for m in range(4):
                for d in range(DT):
                    for o in range(2):
                        last = nc.tensor.transpose(ps_e[:, m // 2, m % 2, d * D + o * P:d * D + o * P + P],
                                                   w_nat[:, m, o, d * P:(d + 1) * P], ident)
                last.then_inc(wt_ps, 1)
            for m in range(4):
                pe.wait_ge(wt_sb, m + 1)
                for o in range(2):
                    last = nc.tensor.transpose(ps_e[0:64, m // 2, m % 2, o * P:(o + 1) * P],
                                               b_nat[:, m, o].rearrange("p e r -> p (e r)"), ident)
                last.then_inc(wt_ps, 1)
            pe.wait_ge(fixed, 4)
            pe.wait_ge(wt_sb, 8)
            with pe.Fori(0, BATCH) as b:
                for m in range(4):
                    pe.wait_ge(sel_ready, b * 4 + m + 1)
                    if m == 0:
                        pe.wait_ge(exp_done, b * GROUPS * UNITS + 2)
                    for d in range(DT):
                        last = nc.tensor.matmul(ps_e[:, m // 2, m % 2, d * D:(d + 1) * D],
                                                a_sel[:, m, d * P:(d + 1) * P], b_t[:, m], start=(d == 0),
                                                stop=(d == DT - 1), skip_group_check=True)
                    last.then_inc(wl_ps, 1)
                pe.wait_ge(wl_used, b * 4 + 4)

                def turn(t):
                    pe.wait_ge(xn_ready, b * T + t + 1)
                    pe.wait_ge(xt_sb, b * T + t + 1)
                    for d in range(DT):
                        last = nc.tensor.transpose(ps_e[:, 1, 0, d * P:(d + 1) * P], xn[:, t % 2, d * P:(d + 1) * P],
                                                   ident)
                    last.then_inc(xt_ps, 1)

                def stacks(t):
                    pe.wait_ge(lo_ready, b * T + t + 1)
                    pe.wait_ge(ks_sb, b * T + t + 1)
                    for c in range(PAIRS):
                        last = nc.tensor.transpose(ps_a[:, c // 4, (c % 4) * P:(c % 4 + 1) * P],
                                                   k_tok[:, t % 2, 2 * c:2 * c + 2, :].bitcast(F32).rearrange(
                                                       "p h c -> p (h c)"), ident)
                    last.then_inc(ks_ps, 1)
                    pe.wait_ge(qs_sb, b * T + t + 1)
                    for c in range(PAIRS):
                        last = nc.tensor.transpose(ps_m[:, c // 4, (c % 4) * P:(c % 4 + 1) * P],
                                                   q_tok[:, t, 2 * c:2 * c + 2, :].bitcast(F32).rearrange(
                                                       "p h c -> p (h c)"), ident)
                    last.then_inc(qs_ps, 1)

                def project(t):
                    pe.wait_ge(xt_sb, b * T + t + 2)
                    pe.wait_ge(rot_ready, b * T + t + 1)
                    pe.wait_ge(v_copied, b * T + t + 1)
                    for d in range(DT):
                        nc.tensor.matmul(ps_e[:, 0, 0, :], xn_t[:, t % 2, d * P:(d + 1) * P],
                                         w_eff[:, d, 0:2].rearrange("p m o -> p (m o)"), start=(d == 0),
                                         stop=(d == DT - 1))
                    for d in range(DT):
                        last = nc.tensor.matmul(ps_e[:, 0, 1, 0:D], xn_t[:, t % 2, d * P:(d + 1) * P], w_eff[:, d, 2],
                                                start=(d == 0), stop=(d == DT - 1))
                    last.then_inc(qkv_ps, 1)

                for t in range(T):
                    turn(t)
                    project(t)
                    if t >= 1:
                        stacks(t - 1)
                stacks(T - 1)
                pe.wait_ge(ks_sb, b * T + T + 1)
                pe.wait_ge(qs_sb, b * T + T + 1)
                pe.wait_ge(v_copied, b * T + T + 1)

                def scores(g, i):
                    for u in range(GROUP):
                        h = g * GROUP + u
                        rows = slice(64 * (h % 2), 64 * (h % 2) + 64)
                        for c in range(1 + (i >= T // 2)):
                            n = (sum(1 + (x >= T // 2) for x in range(i)) * GROUP + u * (1 + (i >= T // 2)) + c)
                            w = min(512, (i + 1) * P - 512 * c)
                            diag = w < 512 or c == 1 or i == T // 2 - 1
                            pe.wait_ge(chunk_max, (b * GROUPS + g) * CHUNKS + n + 1)
                            last = nc.tensor.matmul(ps_m[:, n % 2, 0:w], q_st[rows, h // 2, i * P:(i + 1) * P],
                                                    k_st[rows, h // 2, 512 * c:512 * c + w], start=True,
                                                    stop=not diag)
                            if diag:
                                last = nc.tensor.matmul(ps_m[:, n % 2, w - P:w], ident_b[:], mask_b[:, 0], start=False,
                                                        stop=True)
                            last.then_inc(score_ps, 1)

                def again(g):
                    pe.wait_ge(max_ready, b * GROUPS + g + 1)
                    for n in range(4):
                        if n >= 2:
                            pe.wait_ge(again_sb, (b * GROUPS + g) * 4 + n - 1)
                        for k in range(4):
                            t = (n % 2) * 4 + k
                            last = nc.tensor.transpose(ps_m[:, n % 2, k * P:(k + 1) * P],
                                                       q_tok[:, t, 4 * g + 2 * (n // 2):4 * g + 2 * (n // 2) + 2, :]
                                                       .bitcast(F32).rearrange("p h c -> p (h c)"), ident)
                        last.then_inc(again_ps, 1)
                    pe.wait_ge(again_sb, (b * GROUPS + g) * 4 + 4)

                def shifted(g, j, u):
                    h, n = g * GROUP + u, j * GROUP + u
                    rows = slice(64 * (h % 2), 64 * (h % 2) + 64)
                    pe.wait_ge(exp_done, (b * GROUPS + g) * UNITS + n + 1)
                    for c in range((j * P) // 512, 2):
                        q0 = max(j * P, 512 * c)
                        diag = q0 == j * P
                        last = nc.tensor.matmul(ps_e[:, n % 2, c, q0 - 512 * c:512], k_st[rows, h // 2, j * P:(j + 1) * P],
                                                q_st[rows, h // 2, q0:512 * (c + 1)], start=True, stop=not diag)
                        if diag:
                            last = nc.tensor.matmul(ps_e[:, n % 2, c, q0 - 512 * c:q0 - 512 * c + P], ident_b[:],
                                                    mask_b[:, 1], start=False, stop=True)
                    last.then_inc(shifted_ps, 1)

                def weigh(g, j):
                    pe.wait_ge(exp_done, (b * GROUPS + g) * UNITS + (j + 1) * GROUP + 2)
                    if j == 0:
                        pe.wait_ge(normed, b * GROUPS + g + 1)
                    for c in range((j * P) // 512, 2):
                        q0 = max(j * P, 512 * c)
                        for u in range(GROUP):
                            last = nc.tensor.matmul(ps_a[32 * u:32 * u + 32, c, q0 - 512 * c:512],
                                                    vals[:, j, 17 * (g * GROUP + u):17 * (g * GROUP + u) + 32],
                                                    probs[:, (j * GROUP + u) % RING, q0:512 * (c + 1)],
                                                    start=(j == 0), stop=(j == 4 * c + 3), tile_position=(0, 32 * u))
                    last.then_inc(pv_done, 1)

                def turn_acc(g):
                    pe.wait_ge(acc_sb, b * GROUPS + g + 1)
                    for t in range(T):
                        last = nc.tensor.transpose(ps_a[:, t // 4, (t % 4) * P:(t % 4 + 1) * P],
                                                   acc[:, t * P:(t + 1) * P], ident)
                    last.then_inc(acc_t, 1)

                for i in range(T):
                    scores(0, i)
                again(0)
                for g in range(GROUPS):
                    for j in range(T):
                        for u in range(GROUP):
                            shifted(g, j, u)
                            if u == 1 and j >= 1:
                                weigh(g, j - 1)
                        if j == 0 and g >= 1:
                            turn_acc(g - 1)
                        if g + 1 < GROUPS:
                            scores(g + 1, j)
                    weigh(g, T - 1)
                    if g + 1 < GROUPS:
                        again(g + 1)
                turn_acc(GROUPS - 1)
                pe.wait_ge(normed, b * GROUPS + GROUPS + 1)
                for t in range(T):
                    pe.wait_ge(ot_sb, b * T + t + 1)
                    for d in range(DT):
                        last = nc.tensor.transpose(ps_m[:, 0, d * P:(d + 1) * P], heads_out[:, t, d * P:(d + 1) * P],
                                                   ident)
                    last.then_inc(ot_ps, 1)
                    pe.wait_ge(ot_sb, b * T + t + 2)
                    pe.wait_ge(x_added, b * T + t + 1)
                    for d in range(DT):
                        last = nc.tensor.matmul(ps_m[:, 1, 0:D], ho_t[:, d * P:(d + 1) * P], w_eff[:, d, 3],
                                                start=(d == 0), stop=(d == DT - 1))
                    last.then_inc(proj_ps, 1)
                pe.wait_ge(x_added, b * T + T + 1)


def routed_ffn(nc, X, C, F, name):
    FT = FF // P
    with ExitStack() as ctx:
        def sb(n, shape, dt=F32):
            return ctx.enter_context(nc.sbuf_tensor(name + n, shape, dt))

        def sem(n):
            return C["sems"]("f_" + n)

        ps_g = ctx.enter_context(nc.psum_tensor(name + "ps_g", [P, 2, 512], F32))
        ps_u = ctx.enter_context(nc.psum_tensor(name + "ps_u", [P, 2, 512], F32))
        ps_h = ctx.enter_context(nc.psum_tensor(name + "ps_h", [P, 2, 512], F32))
        ps_x = ctx.enter_context(nc.psum_tensor(name + "ps_x", [P, 512], F32))
        ps_y = ctx.enter_context(nc.psum_tensor(name + "ps_y", [P, 512], F32))

        w_gu = sb("w_gu", [P, EXPERTS, DT, 2, FF])
        w_d = sb("w_d", [P, EXPERTS, FT, D])
        w_r = sb("w_r", [P, DT, EXPERTS])
        b_r = sb("b_r", [P, EXPERTS])
        stats = sb("stats", [P, NT, 6])
        mean_var = sb("mean_var", [P, NT, 2])
        var_eps = sb("var_eps", [P, NT])
        rstd = sb("rstd", [P, NT])
        xn = sb("xn", [P, 4, D])
        xn_t = sb("xn_t", [P, 2, 2 * D])
        logits = sb("logits", [P, NT, EXPERTS])
        best = sb("best", [P, NT])
        expd = sb("expd", [P, NT, EXPERTS])
        top_w = sb("top_w", [P, NT])
        hot = sb("hot", [P, NT, EXPERTS])
        taken = sb("taken", [P, NT])
        hot_b = sb("hot_b", [P, NT, EXPERTS], BF16)
        before_b = sb("before_b", [P, P], BF16)
        ones_b = sb("ones_b", [P, P], BF16)
        ones = sb("ones", [P, NT])
        upto = sb("upto", [P, NT, EXPERTS])
        place = sb("place", [P, NT, EXPERTS])
        over = sb("over", [P, EXPERTS, NT])
        tiles = sb("tiles", [P, EXPERTS])
        first = sb("first", [P, EXPERTS])
        slot = sb("slot", [P, NT])
        slot_i = sb("slot_i", [P, NT], U32)
        owner = sb("owner", [P, 2, SLOTS])
        owner_i = sb("owner_i", [P, SLOTS], I32)
        xe = sb("xe", [P, D])
        xe_t = sb("xe_t", [P, D])
        gate = sb("gate", [P, FF])
        hid = sb("hid", [P, FF])
        hid_t = sb("hid_t", [P, FF])
        y = sb("y", [P, D])
        y_tok = sb("y_tok", [P, 4, D])
        warm = sb("warm", [P, 1])
        warmed = sem("warmed")

        loaded, w_loaded, step_done, stats_ready, rstd_ready = (
            sem(n) for n in ("loaded", "w_loaded", "step_done", "stats_ready", "rstd_ready"))
        xn_ready, xt_ps, xt_sb, logit_ps, pair_used, shifted, exp_ready = (
            sem(n) for n in ("xn_ready", "xt_ps", "xt_sb", "logit_ps", "pair_used", "shifted", "exp_ready"))
        hot_ready, rank_ps, slot_ready, owner_ready, again_ready = (
            sem(n) for n in ("hot_ready", "rank_ps", "slot_ready", "owner_ready", "again_ready"))
        sent = [C["sems"](f"{name}sent{k}") for k in range(4)]
        fetched = [C["sems"](f"{name}fetched{k}") for k in range(4)]
        xe_loaded, xe_ps, xe_sb, gate_ps, gate_sb, up_ps, hid_ready = (
            sem(n) for n in ("xe_loaded", "xe_ps", "xe_sb", "gate_ps", "gate_sb", "up_ps", "hid_ready"))
        ht_ps, ht_lo, ht_hi, y_ps, y_sb, y_stored, added, zeroed = (
            sem(n) for n in ("ht_ps", "ht_lo", "ht_hi", "y_ps", "y_sb", "y_stored", "added", "zeroed"))

        x_slots, y_slots = F["x_slots"], F["y_slots"]
        W_LOADS = 3 * EXPERTS
        block = ctx.enter_context(nc.Block())

        @block.sync
        def _(sp):
            sp.dma_start(w_r[:], F["Wr"].rearrange("(t p) e -> p t e", p=P)).then_inc(loaded, 16)
            sp.dma_start(b_r[:], F["br"].rearrange("(a e) -> a e", a=1).to_broadcast([P, EXPERTS])).then_inc(loaded, 16)
            sp.wait_ge(zeroed, 1)
            sp.dma_start(x_slots.rearrange("(t p) d -> p t d", p=P),
                         gate[:, 0:D].unsqueeze(1).to_broadcast([P, SLOTS, D])).then_inc(zeroed, 16)
            for e in range(EXPERTS):
                for k, w in enumerate(("Wg", "Wu")):
                    sp.dma_start(w_gu[:, e, :, k], F[w][e].rearrange("(t p) f -> p t f", p=P)).then_inc(w_loaded, 16)
                sp.dma_start(w_d[:, e], F["Wd"][e].rearrange("(t p) d -> p t d", p=P)).then_inc(w_loaded, 16)
            for k in range(4):
                sp.wait_ge(sent[k], 16 * (NT // 4))
            sp.sem_inc(y_stored, 16)
            sp.dma_start(xe[:], x_slots[0:P, :]).then_inc(xe_loaded, 16)
            with sp.Fori(1, SLOTS) as j:
                sp.wait_ge(xe_ps, j)
                sp.dma_start(xe[:], x_slots[bass.ds(j * P, P), :]).then_inc(xe_loaded, 16)
                sp.wait_ge(y_sb, j)
                sp.dma_start(y_slots[bass.ds(j * P - P, P), :], y[:]).then_inc(y_stored, 16)
            sp.wait_ge(y_sb, SLOTS)
            sp.dma_start(y_slots[(SLOTS - 1) * P:SLOTS * P, :], y[:]).then_inc(y_stored, 16)
            sp.wait_ge(y_stored, 16 * SLOTS + 16)

        def x_tile(t):
            return X[:, bass.ds(t, 1), :].rearrange("p a d -> p (a d)")

        @block.vector
        def _(dve):
            step = Steps(dve, step_done)
            nc.vector.memset(gate[:], 0.0).then_inc(zeroed, 1)
            step(nc.vector.memset(ones_b[:], 1.0))
            step(nc.vector.memset(ones[:], 1.0))
            step(nc.vector.tensor_copy(before_b[:], C["before"]))
            row_stats(nc, step, [X[:, t, :] for t in range(NT)], stats, mean_var, var_eps[:], stats_ready)
            dve.wait_ge(rstd_ready, 1)
            dve.wait_ge(loaded, 32)

            def norm(t):
                if t >= 4:
                    dve.wait_ge(xt_ps, t // 2 - 1)
                nc.vector.tensor_scalar(xn[:, t % 4], X[:, t, :], mean_var[:, t, 0:1], rstd[:, t:t + 1],
                                        ALU.subtract, ALU.mult).then_inc(xn_ready, 1)

            for t in range(NT):
                norm(t)
            dve.wait_ge(logit_ps, 1)
            step(nc.vector.tensor_tensor(logits[:], ps_y[:, 0:NT * EXPERTS].rearrange("p (t e) -> p t e", e=EXPERTS),
                                         b_r[:].unsqueeze(1).to_broadcast([P, NT, EXPERTS]), ALU.add))

            def all_experts(v):
                return v.unsqueeze(2).to_broadcast([P, NT, EXPERTS])

            step(nc.vector.tensor_reduce(best[:], logits[:], AX, ALU.max))
            nc.vector.tensor_tensor(logits[:], logits[:], all_experts(best[:]), ALU.subtract).then_inc(shifted, 1)
            dve.wait_ge(shifted, 1)
            step(nc.vector.tensor_scalar(hot[:], logits[:], 0.0, None, ALU.is_equal))
            step(nc.vector.tensor_copy(taken[:], hot[:, :, 0]))
            for e in range(1, EXPERTS):
                step(nc.vector.tensor_tensor(hot[:, :, e], hot[:, :, e], taken[:], ALU.is_gt))
                step(nc.vector.tensor_tensor(taken[:], hot[:, :, e], taken[:], ALU.add))
            nc.vector.tensor_copy(hot_b[:], hot[:]).then_inc(hot_ready, 1)
            dve.wait_ge(exp_ready, 1)
            step(nc.vector.tensor_reduce(best[:], expd[:], AX, ALU.add))
            step(nc.vector.reciprocal(top_w[:], best[:]))
            dve.wait_ge(rank_ps, 1)
            totals = ps_g[:, 1, 0:P].rearrange("p (t e) -> p t e", e=EXPERTS)
            for e in range(EXPERTS):
                step(nc.vector.tensor_tensor_scan(upto[:, :, e], ones[:], totals[:, :, e], 0.0, ALU.mult, ALU.add))
            step(nc.vector.tensor_tensor(place[:], upto[:], totals, ALU.subtract))
            step(nc.vector.tensor_tensor(place[:], place[:], ps_g[:, 0, 0:P].rearrange("p (t e) -> p t e", e=EXPERTS),
                                         ALU.add))
            step(nc.vector.tensor_tensor(over[:], upto[:, NT - 1, :].unsqueeze(2).to_broadcast([P, EXPERTS, NT]),
                                         C["tile_tokens"].unsqueeze(1).to_broadcast([P, EXPERTS, NT]), ALU.is_gt))
            step(nc.vector.tensor_reduce(tiles[:], over[:], AX, ALU.add))
            step(nc.vector.memset(first[:], 0.0))
            for e in range(1, EXPERTS):
                step(nc.vector.tensor_tensor(first[:, e:e + 1], first[:, e - 1:e], tiles[:, e - 1:e], ALU.add))
            for e in range(EXPERTS):
                step(nc.vector.tensor_scalar(over[:, e, 0:1], first[:, e:e + 1], float(P), None, ALU.mult))
                step(nc.vector.tensor_scalar(place[:, :, e], place[:, :, e], over[:, e, 0:1], None, ALU.add))
            step(nc.vector.tensor_tensor(place[:], place[:], hot[:], ALU.mult))
            step(nc.vector.tensor_reduce(slot[:], place[:], AX, ALU.add))
            nc.vector.tensor_copy(slot_i[:], slot[:]).then_inc(slot_ready, 1)
            step(nc.vector.tensor_scalar(owner[:, 0, :], C["slot_no"], first[:, 1:2], None, ALU.is_ge))
            for e in range(2, EXPERTS):
                step(nc.vector.tensor_scalar(owner[:, 1, :], C["slot_no"], first[:, e:e + 1], None, ALU.is_ge))
                step(nc.vector.tensor_tensor(owner[:, 0, :], owner[:, 0, :], owner[:, 1, :], ALU.add))
            nc.vector.tensor_copy(owner_i[:], owner[:, 0, :]).then_inc(owner_ready, 1)
            for t in range(NT):
                if t >= 4:
                    dve.wait_ge(sent[t % 4], 16 * (t // 4))
                nc.vector.tensor_scalar(xn[:, t % 4], X[:, t, :], mean_var[:, t, 0:1], rstd[:, t:t + 1],
                                        ALU.subtract, ALU.mult).then_inc(again_ready, 1)

            def take(j):
                dve.wait_ge(xe_ps, j + 1)
                nc.vector.tensor_copy(xe_t[:], ps_x[:, 0:D]).then_inc(xe_sb, 1)

            def combine(j):
                dve.wait_ge(up_ps, j + 1)
                dve.wait_ge(gate_sb, j + 1)
                nc.vector.tensor_tensor(hid[:], gate[:], ps_u[:].rearrange("p b f -> p (b f)"), ALU.mult
                                        ).then_inc(hid_ready, 1)

            def hidden(j):
                dve.wait_ge(ht_ps, j + 1)
                nc.vector.tensor_copy(hid_t[:, 0:512], ps_h[:, 0]).then_inc(ht_lo, 1)

            take(0)
            with dve.Fori(0, SLOTS - 1) as j:
                combine(j)
                take(j + 1)
                hidden(j)
            combine(SLOTS - 1)
            hidden(SLOTS - 1)
            for t in range(NT):
                dve.wait_ge(fetched[t % 4], 16 * (t // 4 + 1))
                nc.vector.scalar_tensor_tensor(X[:, t, :], y_tok[:, t % 4], top_w[:, t:t + 1], X[:, t, :], ALU.mult,
                                               ALU.add).then_inc(added, 1)
            dve.wait_ge(added, NT)

        @block.gpsimd
        def _(pool):
            pool.wait_ge(stats_ready, 1)
            inverse_root(nc, rstd[:], var_eps[:], C).then_inc(rstd_ready, 1)
            pool.wait_ge(zeroed, 17)
            pool.wait_ge(slot_ready, 1)
            for t in range(NT):
                pool.wait_ge(again_ready, t + 1)
                nc.gpsimd.indirect_dma_start(
                    out=x_slots, out_offset=bass.IndirectOffsetOnAxis(ap=slot_i[:, t:t + 1], axis=0),
                    in_=xn[:, t % 4], in_offset=None).then_inc(sent[t % 4], 16)
            pool.wait_ge(y_stored, 16 * SLOTS + 16)
            for t in range(NT):
                if t >= 4:
                    pool.wait_ge(added, t - 3)
                nc.gpsimd.indirect_dma_start(
                    out=y_tok[:, t % 4], out_offset=None, in_=y_slots,
                    in_offset=bass.IndirectOffsetOnAxis(ap=slot_i[:, t:t + 1], axis=0)).then_inc(fetched[t % 4], 16)
            for k in range(4):
                pool.wait_ge(fetched[k], 16 * (NT // 4))

        @block.scalar
        def _(act):
            for k in range(NT // 2):
                act.wait_ge(xt_ps, k + 1)
                if k >= 2:
                    act.wait_ge(pair_used, k - 1)
                nc.scalar.copy(xn_t[:, k % 2], ps_u[:, k % 2]).then_inc(xt_sb, 1)
            act.wait_ge(shifted, 1)
            nc.scalar.activation(expd[:], logits[:], ACT.Exp).then_inc(exp_ready, 1)

            def activate(j):
                act.wait_ge(gate_ps, j + 1)
                nc.scalar.activation(gate[:], ps_g[:].rearrange("p b f -> p (b f)"), ACT.Silu).then_inc(gate_sb, 1)

            def hidden(j):
                act.wait_ge(ht_ps, j + 1)
                nc.scalar.copy(hid_t[:, 512:1024], ps_h[:, 1]).then_inc(ht_hi, 1)

            def result(j):
                act.wait_ge(y_ps, j + 1)
                act.wait_ge(y_stored, j * 16 + 16)
                nc.scalar.copy(y[:], ps_y[:, 0:D]).then_inc(y_sb, 1)

            activate(0)
            hidden(0)
            with act.Fori(1, SLOTS) as j:
                nc.scalar.activation(warm[:], ones[:, 0:1], ACT.Silu).then_inc(warmed, 1)
                act.wait_ge(warmed, j)
                activate(j)
                result(j - 1)
                hidden(j)
            result(SLOTS - 1)

        @block.tensor
        def _(pe):
            ident = C["ident"]

            def turn_pair(k):
                pe.wait_ge(xn_ready, 2 * k + 2)
                if k >= 2:
                    pe.wait_ge(xt_sb, k - 1)
                for n in range(2 * DT):
                    last = nc.tensor.transpose(ps_u[:, k % 2, n * P:(n + 1) * P],
                                               xn[:, 2 * (k % 2) + n // DT, (n % DT) * P:(n % DT + 1) * P], ident)
                last.then_inc(xt_ps, 1)

            def route(k):
                pe.wait_ge(xt_sb, k + 1)
                for n in range(2 * DT):
                    t, d = 2 * k + n // DT, n % DT
                    last = nc.tensor.matmul(ps_y[:, t * EXPERTS:(t + 1) * EXPERTS], xn_t[:, k % 2, n * P:(n + 1) * P],
                                            w_r[:, d], start=(d == 0), stop=(d == DT - 1))
                last.then_inc(logit_ps if k == NT // 2 - 1 else pair_used, 1)

            turn_pair(0)
            for k in range(NT // 2):
                if k + 1 < NT // 2:
                    turn_pair(k + 1)
                route(k)
            pe.wait_ge(hot_ready, 1)
            oh = hot_b[:].rearrange("p t e -> p (t e)")
            nc.tensor.matmul(ps_g[:, 0, 0:P], before_b[:], oh, start=True, stop=True)
            nc.tensor.matmul(ps_g[:, 1, 0:P], ones_b[:], oh, start=True, stop=True).then_inc(rank_ps, 1)
            pe.wait_ge(owner_ready, 1)
            pe.wait_ge(w_loaded, 16 * W_LOADS)

            def turn(j):
                pe.wait_ge(xe_loaded, j * 16 + 16)
                for d in range(DT):
                    last = nc.tensor.transpose(ps_x[:, d * P:(d + 1) * P], xe[:, d * P:(d + 1) * P], ident)
                last.then_inc(xe_ps, 1)

            def up(j, e):
                pe.wait_ge(xe_sb, j + 1)
                for k, ps, done in ((0, ps_g, gate_ps), (1, ps_u, up_ps)):
                    for c in range(FF // 512):
                        for d in range(DT):
                            last = nc.tensor.matmul(
                                ps[:, c], xe_t[:, d * P:(d + 1) * P],
                                w_gu[:, bass.ds(e, 1), d, k, c * 512:(c + 1) * 512].rearrange("p a f -> p (a f)"),
                                start=(d == 0), stop=(d == DT - 1))
                    last.then_inc(done, 1)

            def down(j, e):
                pe.wait_ge(ht_lo, j + 1)
                pe.wait_ge(ht_hi, j + 1)
                for f in range(FT):
                    last = nc.tensor.matmul(ps_y[:, 0:D], hid_t[:, f * P:(f + 1) * P],
                                            w_d[:, bass.ds(e, 1), f].rearrange("p a d -> p (a d)"), start=(f == 0),
                                            stop=(f == FT - 1))
                last.then_inc(y_ps, 1)

            def turn_hidden(j):
                pe.wait_ge(hid_ready, j + 1)
                for f in range(FT):
                    last = nc.tensor.transpose(ps_h[:, f // 4, (f % 4) * P:(f % 4 + 1) * P], hid[:, f * P:(f + 1) * P],
                                               ident)
                last.then_inc(ht_ps, 1)

            def expert_of(j):
                return pe.value_load(owner_i[0:1, bass.ds(j, 1)], min_val=0, max_val=EXPERTS - 1)

            turn(0)
            up(0, expert_of(0))
            turn(1)
            turn_hidden(0)
            with pe.Fori(1, SLOTS - 1) as j:
                up(j, expert_of(j))
                down(j - 1, expert_of(j - 1))
                turn(j + 1)
                turn_hidden(j)
            up(SLOTS - 1, expert_of(SLOTS - 1))
            down(SLOTS - 2, expert_of(SLOTS - 2))
            turn_hidden(SLOTS - 1)
            down(SLOTS - 1, expert_of(SLOTS - 1))
            pe.wait_ge(y_sb, SLOTS)



def mamba(nc, X, C, M):
    ZT = INNER // P
    with ExitStack() as ctx:
        def sb(n, shape, dt=F32):
            return ctx.enter_context(nc.sbuf_tensor("m_" + n, shape, dt))

        def sem(n):
            return C["sems"]("m_" + n)

        def ps(n, banks=1):
            return ctx.enter_context(nc.psum_tensor("m_ps_" + n, [P, banks, 512], F32))

        ps_r, ps_t, ps_b, ps_y, ps_o, ps_s, ps_z = ps("r", 2), ps("t"), ps("b"), ps("y"), ps("o"), ps("s"), ps("z")

        w_in = sb("w_in", [P, DT, IN_PROJ])
        w_out = sb("w_out", [P, ZT, D])
        norm_w = sb("norm_w", [P, ZT])
        conv_w = sb("conv_w", [P, CT, TAPS])
        conv_b = sb("conv_b", [P, CT])
        dt_bias = sb("dt_bias", [P, MHEADS])
        a_neg = sb("a_neg", [P, 2, MHEADS])
        skip = sb("skip", [P, MHEADS])
        ident_b = sb("ident_b", [P, P], BF16)
        neg_b = sb("neg_b", [P, P], BF16)
        ones = sb("ones", [P, P])
        stats = sb("stats", [P, T, 6])
        mean_var = sb("mean_var", [P, T, 2])
        var_eps = sb("var_eps", [P, T])
        rstd = sb("rstd", [P, T])
        xn = sb("xn", [P, 2, D])
        xn_t = sb("xn_t", [P, DT, SEQ])
        pre = sb("pre", [P, 2, SEQ + TAPS - 1])
        conv = sb("conv", [P, 2, SEQ])
        xbc = sb("xbc", [P, CT, SEQ])
        z_act = sb("z_act", [P, T, INNER])
        dtv = sb("dtv", [P, 6, T, MHEADS])
        dt = sb("dt", [P, T, MHEADS])
        dta = sb("dta", [P, T, MHEADS])
        acs = sb("acs", [P, 2, T, MHEADS])
        neg_acs = sb("neg_acs", [P, T, MHEADS])
        e_acs = sb("e_acs", [P, T, MHEADS])
        e_rest = sb("e_rest", [P, T, MHEADS])
        e_all = sb("e_all", [P, T, MHEADS])
        decay = sb("decay", [P, MHEADS, P])
        mix = sb("mix", [P, MHEADS, P])
        b_tok = sb("b_tok", [P, P])
        xdt = sb("xdt", [P, MHEADS, HDIM])
        xskip = sb("xskip", [P, MHEADS, HDIM])
        xds = sb("xds", [P, MHEADS, HDIM])
        state = sb("state", [P, MHEADS, HDIM])
        y = sb("y", [P, 2, MHEADS, HDIM])
        y_t = sb("y_t", [P, INNER])
        square = sb("square", [P, INNER])
        sum_sq = sb("sum_sq", [P, 1])
        mean_sq = sb("mean_sq", [P, 1])
        rms = sb("rms", [P, 1])

        loaded, fixed, step_done, act_fixed, stats_ready, rstd_ready = (
            sem(n) for n in ("loaded", "fixed", "step_done", "act_fixed", "stats_ready", "rstd_ready"))
        xn_ready, xn_added, xt_ps, xt_sb, conv_ps, pre_ready, conv_ready, xbc_ready = (
            sem(n) for n in ("xn_ready", "xn_added", "xt_ps", "xt_sb", "conv_ps", "pre_ready", "conv_ready", "xbc_ready"))
        z_ps, z_ready, dt_ps, dt_step, dt_exp, dta_ready, sums_ps, sums_ready, exps_ready = (
            sem(n) for n in ("z_ps", "z_ready", "dt_ps", "dt_step", "dt_exp", "dta_ready", "sums_ps", "sums_ready",
                             "exps_ready"))
        turned_ps, gram_ps, decay_ps, b_ready, decay_ready, mix_ready, xdt_ready, xds_ready = (
            sem(n) for n in ("turned_ps", "gram_ps", "decay_ps", "b_ready", "decay_ready", "mix_ready", "xdt_ready",
                             "xds_ready"))
        diag_ps, off_ps, state_ps, state_ready, y_sum, gate_step, y_ready, sq_ready, mean_ready, rms_ready = (
            sem(n) for n in ("diag_ps", "off_ps", "state_ps", "state_ready", "y_sum", "gate_step", "y_ready",
                             "sq_ready", "mean_ready", "rms_ready"))
        yt_ps, yt_sb, out_ps, x_added = (sem(n) for n in ("yt_ps", "yt_sb", "out_ps", "x_added"))

        block = ctx.enter_context(nc.Block())

        def spread(v):
            return v.rearrange("(a h) -> a h", a=1).to_broadcast([P, MHEADS])

        @block.sync
        def _(sp):
            sp.dma_start(w_in[:], M["w_in"].rearrange("(t p) e -> p t e", p=P)).then_inc(loaded, 16)
            sp.dma_start(w_out[:], M["w_out"].rearrange("(t p) d -> p t d", p=P)).then_inc(loaded, 16)
            with nc.allow_non_contiguous_dma(reason="a few hundred words of parameters"):
                sp.dma_start(norm_w[:], M["norm_w"].rearrange("(t p) -> p t", p=P)).then_inc(loaded, 16)
                sp.dma_start(conv_b[:], M["conv_b"].rearrange("(t p) -> p t", p=P)).then_inc(loaded, 16)
                sp.dma_start(conv_w[:], M["conv_w"].rearrange("(t p) k -> p t k", p=P)).then_inc(loaded, 16)
            sp.dma_start(dt_bias[:], spread(M["dt_bias"])).then_inc(loaded, 16)
            sp.dma_start(a_neg[:, 0], spread(M["A_log"])).then_inc(loaded, 16)
            sp.dma_start(skip[:], spread(M["D"])).then_inc(loaded, 16)
            sp.wait_ge(loaded, 16 * 8)

        def heads(v):
            return v.unsqueeze(2).to_broadcast([P, MHEADS, HDIM])

        def by_head(v):
            return v.rearrange("p (h f) -> p h f", h=MHEADS)

        def x_tile(b, t):
            return X[:, bass.ds(b * T + t, 1), :].rearrange("p a d -> p (a d)")

        ORDER = [4, 5, 0, 1, 2, 3]

        @block.vector
        def _(dve):
            dve.wait_ge(loaded, 16 * 8)
            step = Steps(dve, fixed)
            step(nc.vector.tensor_copy(ident_b[:], C["ident"]))
            step(nc.vector.tensor_copy(neg_b[:], C["neg"][:, 1]))
            step(nc.vector.memset(ones[:], 1.0))
            step(nc.vector.memset(pre[:], 0.0))
            for k in range(ZT):
                step(nc.vector.tensor_scalar(w_out[:, k], w_out[:, k], norm_w[:, k:k + 1], None, ALU.mult))
            dve.wait_ge(act_fixed, 1)
            step(nc.vector.tensor_scalar(a_neg[:, 1], a_neg[:, 1], -1.0, None, ALU.mult))
            dve.sem_inc(x_added, 1)
            dve.sem_inc(y_sum, 1)
            NSTEP = 2 * T + 1 + CT * (TAPS - 1) + 7 + 2 + T * 2
            with dve.Fori(0, BATCH) as b:
                step = Steps(dve, step_done, b * NSTEP)
                row_stats(nc, step, [x_tile(b, t) for t in range(T)], stats, mean_var, var_eps[:], stats_ready)
                dve.wait_ge(rstd_ready, b + 1)
                for t in range(T):
                    if t >= 2:
                        dve.wait_ge(xt_ps, b * T + t - 1)
                        dve.wait_ge(xn_added, b * T + t - 1)
                    nc.vector.tensor_scalar(xn[:, t % 2], x_tile(b, t), mean_var[:, t, 0:1], rstd[:, t:t + 1],
                                            ALU.subtract, ALU.mult).then_inc(xn_ready, 1)
                for n, c in enumerate(ORDER):
                    dve.wait_ge(pre_ready, b * 2 * CT + 2 * n + 2)
                    if n >= 2:
                        dve.wait_ge(xbc_ready, b * CT + n - 1)
                    x, a = pre[:, n % 2], conv[:, n % 2]
                    step(nc.vector.tensor_scalar(a, x[:, 3:3 + SEQ], conv_w[:, c, 3:4], conv_b[:, c:c + 1], ALU.mult,
                                                 ALU.add))
                    for k in (2, 1):
                        step(nc.vector.scalar_tensor_tensor(a, x[:, k:k + SEQ], conv_w[:, c, k:k + 1], a, ALU.mult,
                                                            ALU.add))
                    nc.vector.scalar_tensor_tensor(a, x[:, 0:SEQ], conv_w[:, c, 0:1], a, ALU.mult, ALU.add
                                                   ).then_inc(conv_ready, 1)
                v, e, u, r, q = (dtv[:, k] for k in range(5))

                def flat(w):
                    return w.rearrange("p t h -> p (t h)")

                dve.wait_ge(dt_ps, b + 1)
                step(nc.vector.tensor_tensor(v, ps_b[:, 0, 0:T * MHEADS].rearrange("p (t h) -> p t h", h=MHEADS),
                                             dt_bias[:].unsqueeze(1).to_broadcast([P, T, MHEADS]), ALU.add))
                nc.vector.scalar_tensor_tensor(flat(e), flat(v), -1.0, flat(v), ALU.mult, ALU.max).then_inc(dt_step, 1)
                dve.wait_ge(dt_exp, b * 2 + 1)
                nc.vector.tensor_scalar(u, e, 1.0, None, ALU.add).then_inc(dt_step, 1)
                dve.wait_ge(dt_step, b * 2 + 2)
                step(nc.vector.tensor_scalar(r, u, -1.0, None, ALU.add))
                step(nc.vector.tensor_tensor(r, e, r, ALU.subtract))
                step(nc.vector.reciprocal(q, u))
                step(nc.vector.tensor_tensor(r, r, q, ALU.mult))
                dve.wait_ge(dt_exp, b * 2 + 2)
                step(nc.vector.tensor_tensor(r, r, dtv[:, 5], ALU.add))
                step(nc.vector.scalar_tensor_tensor(flat(dt[:]), flat(v), 0.0, flat(r), ALU.max, ALU.add))
                nc.vector.tensor_tensor(dta[:], dt[:], a_neg[:, 1].unsqueeze(1).to_broadcast([P, T, MHEADS]), ALU.mult
                                        ).then_inc(dta_ready, 1)
                dve.wait_ge(sums_ps, b + 1)
                two = ps_t[:, 0, 0:2 * T * MHEADS].rearrange("p (a t h) -> p a t h", a=2, t=T)
                step(nc.vector.tensor_copy(acs[:, 0], two[:, 0]))
                step(nc.vector.tensor_scalar(neg_acs[:], acs[:, 0], -1.0, None, ALU.mult))
                nc.vector.tensor_tensor(acs[:, 1], two[:, 1], acs[:, 0], ALU.subtract).then_inc(sums_ready, 1)
                nc.vector.memset(state[:], 0.0).then_inc(state_ready, 1)

                def front(t):
                    N = b * T + t
                    dve.wait_ge(turned_ps, N + 1)
                    nc.vector.tensor_tensor(xdt[:], by_head(ps_t[:, 0]), heads(dt[:, t]), ALU.mult
                                            ).then_inc(xdt_ready, 1)
                    nc.vector.tensor_tensor(xskip[:], by_head(ps_t[:, 0]), heads(skip[:]), ALU.mult
                                            ).then_inc(xdt_ready, 1)
                    dve.wait_ge(gram_ps, N + 1)
                    dve.wait_ge(decay_ready, N + 1)
                    nc.vector.tensor_tensor(mix[:], decay[:],
                                            ps_b[:, 0, 0:P].unsqueeze(1).to_broadcast([P, MHEADS, P]), ALU.mult
                                            ).then_inc(mix_ready, 1)

                def middle(t):
                    N = b * T + t
                    dve.wait_ge(off_ps, N + 1)
                    step(nc.vector.tensor_tensor(state[:], state[:], heads(e_all[:, t]), ALU.mult))
                    dve.wait_ge(state_ps, N + 1)
                    nc.vector.tensor_tensor(state[:], state[:], by_head(ps_s[:, 0]), ALU.add).then_inc(state_ready, 1)
                    if t >= 2:
                        dve.wait_ge(y_ready, N - 1)
                    step(nc.vector.tensor_tensor(y[:, t % 2], by_head(ps_o[:, 0]), heads(e_acs[:, t]), ALU.mult))
                    dve.wait_ge(diag_ps, N + 1)
                    nc.vector.tensor_tensor(y[:, t % 2], y[:, t % 2], by_head(ps_y[:, 0]), ALU.add).then_inc(y_sum, 1)

                def mean(t):
                    N = b * T + t
                    dve.wait_ge(sq_ready, N + 1)
                    nc.vector.tensor_scalar(mean_sq[:], sum_sq[:], 1.0 / INNER, LN_EPS, ALU.mult, ALU.add
                                            ).then_inc(mean_ready, 1)

                def last(t):
                    N = b * T + t
                    dve.wait_ge(out_ps, N + 1)
                    dve.wait_ge(rms_ready, N + 1)
                    dve.wait_ge(xn_added, N + 1)
                    nc.vector.scalar_tensor_tensor(x_tile(b, t), ps_z[:, 0, 0:D], rms[:], x_tile(b, t), ALU.mult,
                                                   ALU.add).then_inc(x_added, 1)

                dve.wait_ge(exps_ready, b + 1)
                dve.wait_ge(state_ready, b * (T + 1) + 1)
                front(0)
                for t in range(T):
                    middle(t)
                    if t + 1 < T:
                        dve.wait_ge(state_ps, b * T + t + 1)
                        dve.wait_ge(gate_step, b * T + t + 1)
                        front(t + 1)
                    mean(t)
                    last(t)
                dve.wait_ge(x_added, b * T + T + 1)
                assert step.n == NSTEP, (step.n, NSTEP)

        @block.gpsimd
        def _(pool):
            with pool.Fori(0, BATCH) as b:
                pool.wait_ge(stats_ready, b + 1)
                inverse_root(nc, rstd[:], var_eps[:], C).then_inc(rstd_ready, 1)
                for t in range(T):
                    pool.wait_ge(xn_ready, b * T + t + 1)
                    nc.gpsimd.tensor_tensor(x_tile(b, t), x_tile(b, t), xn[:, t % 2], ALU.add).then_inc(xn_added, 1)

                def weigh(t):
                    pool.wait_ge(xdt_ready, 2 * (b * T + t) + 1)
                    if t >= 1:
                        pool.wait_ge(state_ps, b * T + t)
                    nc.gpsimd.tensor_tensor(xds[:], xdt[:], heads(e_rest[:, t]), ALU.mult).then_inc(xds_ready, 1)

                pool.wait_ge(exps_ready, b + 1)
                pool.wait_ge(z_ready, b * T + T)
                weigh(0)
                for t in range(T):
                    N = b * T + t
                    pool.wait_ge(y_sum, N + 2)
                    pool.wait_ge(xdt_ready, 2 * N + 2)
                    nc.gpsimd.tensor_tensor(y[:, t % 2], y[:, t % 2], xskip[:], ALU.add).then_inc(gate_step, 1)
                    pool.wait_ge(gate_step, N + 1)
                    nc.gpsimd.tensor_tensor(y[:, t % 2], y[:, t % 2], by_head(z_act[:, t]), ALU.mult).then_inc(y_ready, 1)
                    if t + 1 < T:
                        weigh(t + 1)
                    pool.wait_ge(mean_ready, N + 1)
                    if t >= 1:
                        pool.wait_ge(x_added, N + 1)
                    inverse_root(nc, rms[:], mean_sq[:], C).then_inc(rms_ready, 1)

        @block.scalar
        def _(act):
            act.wait_ge(loaded, 16 * 8)
            nc.scalar.activation(a_neg[:, 1], a_neg[:, 0], ACT.Exp).then_inc(act_fixed, 1)
            act.sem_inc(xt_sb, 1)
            act.wait_ge(fixed, 4)
            with act.Fori(0, BATCH) as b:
                for t in range(T):
                    act.wait_ge(xt_ps, b * T + t + 1)
                    nc.scalar.copy(xn_t[:, :, t * P:(t + 1) * P], ps_z[:, 0, 0:D].rearrange("p (d k) -> p d k", d=DT)
                                   ).then_inc(xt_sb, 1)
                for n, c in enumerate(ORDER):
                    for k, bank in enumerate((ps_y, ps_o)):
                        act.wait_ge(conv_ps, b * 2 * CT + 2 * n + k + 1)
                        if n >= 2 and k == 0:
                            act.wait_ge(conv_ready, b * CT + n - 1)
                        nc.scalar.copy(pre[:, n % 2, 3 + 512 * k:3 + 512 * (k + 1)], bank[:, 0]).then_inc(pre_ready, 1)
                    if n >= 1:
                        act.wait_ge(conv_ready, b * CT + n)
                        nc.scalar.activation(xbc[:, ORDER[n - 1]], conv[:, (n - 1) % 2], ACT.Silu).then_inc(xbc_ready, 1)
                act.wait_ge(conv_ready, b * CT + CT)
                nc.scalar.activation(xbc[:, ORDER[-1]], conv[:, (CT - 1) % 2], ACT.Silu).then_inc(xbc_ready, 1)
                for t in range(T):
                    act.wait_ge(z_ps, b * T + t + 1)
                    nc.scalar.activation(z_act[:, t], ps_r[:, t % 2], ACT.Silu).then_inc(z_ready, 1)
                act.wait_ge(dt_step, b * 2 + 1)
                nc.scalar.activation(dtv[:, 1], dtv[:, 1], ACT.Exp, scale=-1.0).then_inc(dt_exp, 1)
                act.wait_ge(dt_step, b * 2 + 2)
                nc.scalar.activation(dtv[:, 5], dtv[:, 2], ACT.Ln).then_inc(dt_exp, 1)
                act.wait_ge(sums_ready, b + 1)
                nc.scalar.activation(e_acs[:], acs[:, 0], ACT.Exp)
                nc.scalar.activation(e_rest[:], acs[:, 1], ACT.Exp)
                nc.scalar.activation(e_all[:].rearrange("p t h -> p (t h)"), ps_t[:, 0, T * MHEADS:2 * T * MHEADS],
                                     ACT.Exp).then_inc(exps_ready, 1)

                def front(t):
                    N = b * T + t
                    act.wait_ge(turned_ps, N + 1)
                    if t >= 1:
                        act.wait_ge(state_ps, N)
                    nc.scalar.copy(b_tok[:], ps_b[:, 0, P:2 * P]).then_inc(b_ready, 1)
                    act.wait_ge(decay_ps, N + 1)
                    if t >= 1:
                        act.wait_ge(mix_ready, N)
                    for h in range(MHEADS):
                        last = nc.scalar.activation(decay[:, h], ps_r[:, h // 4, (h % 4) * P:(h % 4 + 1) * P], ACT.Exp,
                                                    bias=neg_acs[:, t, h:h + 1])
                    last.then_inc(decay_ready, 1)

                front(0)
                for t in range(T):
                    N = b * T + t
                    if t + 1 < T:
                        front(t + 1)
                    act.wait_ge(y_ready, N + 1)
                    if t >= 1:
                        act.wait_ge(mean_ready, N)
                    nc.scalar.activation(square[:], y[:, t % 2].rearrange("p h f -> p (h f)"), ACT.Square,
                                         accum_out=sum_sq[:]).then_inc(sq_ready, 1)
                    act.wait_ge(yt_ps, N + 1)
                    if t >= 1:
                        act.wait_ge(out_ps, N)
                    nc.scalar.copy(y_t[:], ps_y[:, 0]).then_inc(yt_sb, 1)

        @block.tensor
        def _(pe):
            ident = C["ident"]
            pe.wait_ge(loaded, 16 * 8)
            pe.wait_ge(fixed, 4 + ZT + 1)
            with pe.Fori(0, BATCH) as b:
                pe.wait_ge(x_added, b * T + 1)
                for t in range(T):
                    pe.wait_ge(xn_ready, b * T + t + 1)
                    pe.wait_ge(xt_sb, b * T + t + 1)
                    for d in range(DT):
                        last = nc.tensor.transpose(ps_z[:, 0, d * P:(d + 1) * P], xn[:, t % 2, d * P:(d + 1) * P], ident)
                    last.then_inc(xt_ps, 1)
                pe.wait_ge(xt_sb, b * T + T + 1)
                for n, c in enumerate(ORDER):
                    for k, bank in enumerate((ps_y, ps_o)):
                        if n >= 1:
                            pe.wait_ge(pre_ready, b * 2 * CT + 2 * n + k - 1)
                        for d in range(DT):
                            last = nc.tensor.matmul(bank[:, 0], w_in[:, d, INNER + c * P:INNER + (c + 1) * P],
                                                    xn_t[:, d, 512 * k:512 * (k + 1)], start=(d == 0),
                                                    stop=(d == DT - 1))
                        last.then_inc(conv_ps, 1)
                for t in range(T):
                    if t >= 2:
                        pe.wait_ge(z_ready, b * T + t - 1)
                    for d in range(DT):
                        last = nc.tensor.matmul(ps_r[:, t % 2], xn_t[:, d, t * P:(t + 1) * P], w_in[:, d, 0:INNER],
                                                start=(d == 0), stop=(d == DT - 1))
                    last.then_inc(z_ps, 1)
                for t in range(T):
                    for d in range(DT):
                        last = nc.tensor.matmul(ps_b[:, 0, t * MHEADS:(t + 1) * MHEADS], xn_t[:, d, t * P:(t + 1) * P],
                                                w_in[:, d, INNER + CONV:], start=(d == 0), stop=(d == DT - 1))
                last.then_inc(dt_ps, 1)
                pe.wait_ge(dta_ready, b + 1)
                flat = dta[:].rearrange("p t h -> p (t h)")
                nc.tensor.matmul(ps_t[:, 0, 0:T * MHEADS], C["upto"], flat, start=True, stop=True)
                nc.tensor.matmul(ps_t[:, 0, T * MHEADS:2 * T * MHEADS], ones[:], flat, start=True, stop=True
                                 ).then_inc(sums_ps, 1)
                pe.wait_ge(exps_ready, b + 1)
                pe.wait_ge(z_ready, b * T + T)
                pe.wait_ge(xbc_ready, b * CT + CT)

                def front(t):
                    N, s = b * T + t, slice(t * P, (t + 1) * P)
                    if t >= 1:
                        pe.wait_ge(xdt_ready, 2 * N)
                        pe.wait_ge(b_ready, N)
                        pe.wait_ge(mix_ready, N)
                    for k in range(ZT):
                        nc.tensor.transpose(ps_t[:, 0, k * P:(k + 1) * P], xbc[:, k, s], ident)
                    nc.tensor.transpose(ps_b[:, 0, P:2 * P], xbc[:, 4, s], ident).then_inc(turned_ps, 1)
                    for h in range(MHEADS):
                        nc.tensor.matmul(ps_r[:, h // 4, (h % 4) * P:(h % 4 + 1) * P],
                                         dta[:, t, h:h + 1].to_broadcast([P, P]), C["upto"], start=(h % 4 == 0),
                                         stop=False, skip_group_check=True)
                    for k in range(2):
                        last = nc.tensor.matmul(ps_r[:, k].rearrange("p (h l) -> p h l", l=P), ident_b[:],
                                                neg_b[:].unsqueeze(1).to_broadcast([P, 4, P]), start=False, stop=True,
                                                skip_group_check=True)
                    last.then_inc(decay_ps, 1)
                    pe.wait_ge(b_ready, N + 1)
                    nc.tensor.matmul(ps_b[:, 0, 0:P], xbc[:, 4, s], xbc[:, 5, s], start=True, stop=True
                                     ).then_inc(gram_ps, 1)

                front(0)
                for t in range(T):
                    N, s = b * T + t, slice(t * P, (t + 1) * P)
                    pe.wait_ge(y_sum, N + 1)
                    pe.wait_ge(state_ready, b * (T + 1) + t + 1)
                    nc.tensor.matmul(ps_o[:, 0], xbc[:, 5, s], state[:].rearrange("p h f -> p (h f)"), start=True,
                                     stop=True).then_inc(off_ps, 1)
                    pe.wait_ge(mix_ready, N + 1)
                    if t >= 1:
                        pe.wait_ge(yt_sb, N)
                    for h in range(MHEADS):
                        last = nc.tensor.matmul(ps_y[:, 0, h * HDIM:(h + 1) * HDIM], mix[:, h], xdt[:, h],
                                                start=(h == 0), stop=True, skip_group_check=True)
                    last.then_inc(diag_ps, 1)
                    pe.wait_ge(xds_ready, N + 1)
                    nc.tensor.matmul(ps_s[:, 0], b_tok[:], xds[:].rearrange("p h f -> p (h f)"), start=True, stop=True
                                     ).then_inc(state_ps, 1)
                    if t + 1 < T:
                        front(t + 1)
                    pe.wait_ge(y_ready, N + 1)
                    flat_y = y[:, t % 2].rearrange("p h f -> p (h f)")
                    for k in range(ZT):
                        last = nc.tensor.transpose(ps_y[:, 0, k * P:(k + 1) * P], flat_y[:, k * P:(k + 1) * P], ident)
                    last.then_inc(yt_ps, 1)
                    pe.wait_ge(yt_sb, N + 1)
                    pe.wait_ge(x_added, N + 1)
                    for k in range(ZT):
                        last = nc.tensor.matmul(ps_z[:, 0, 0:D], y_t[:, k * P:(k + 1) * P], w_out[:, k], start=(k == 0),
                                                stop=(k == ZT - 1))
                    last.then_inc(out_ps, 1)



def constants():
    i = np.arange(P)
    inv = (10000.0 ** (-np.arange(0, DH, 2) / DH)).astype(np.float32)
    ang = (np.arange(SEQ, dtype=np.float32)[:, None] * inv[None, :]).astype(np.float32)
    cos, sin = np.cos(ang), np.sin(ang)
    rope = np.stack([np.repeat(cos, 2, 1), np.stack([-sin, sin], -1).reshape(SEQ, DH)], 1).astype(np.float32)
    neg = np.stack([np.where(i[None, :] > i[:, None], MASKED, 0.0), np.where(i[None, :] < i[:, None], MASKED, 0.0)], 1)
    table = np.zeros((P, CONSTS), np.float32)
    table[:, 0:P] = np.eye(P)
    table[:, P:3 * P] = neg.reshape(P, 2 * P)
    table[:, 3 * P:4 * P] = (i[:, None] < i[None, :])
    table[:, 4 * P:5 * P] = (i[:, None] <= i[None, :])
    table[:, 5 * P] = i // RANK
    table[:, 5 * P + 1:5 * P + 1 + SLOTS] = np.arange(SLOTS)
    table[:, 5 * P + 1 + SLOTS:5 * P + 1 + SLOTS + NT] = P * np.arange(NT)
    table[:, CONSTS - 1] = -0.5
    return {"const_table": table, "const_rope": rope}


CONSTS = 5 * P + 1 + SLOTS + NT + 1


def program(nc, I, out, phases):
    with ExitStack() as ctx:
        X = ctx.enter_context(nc.sbuf_tensor("x_res", [P, NT, D], F32))
        table = ctx.enter_context(nc.sbuf_tensor("table", [P, CONSTS], F32))
        C = {
            "ident": table[:, 0:P],
            "neg": table[:, P:3 * P].rearrange("p (a k) -> p a k", a=2),
            "before": table[:, 3 * P:4 * P],
            "upto": table[:, 4 * P:5 * P],
            "minus_half": table[:, CONSTS - 1:CONSTS],
            "adapter": table[:, 5 * P:5 * P + 1],
            "slot_no": table[:, 5 * P + 1:5 * P + 1 + SLOTS],
            "tile_tokens": table[:, 5 * P + 1 + SLOTS:CONSTS - 1],
        }
        C["sems"] = Semaphores(nc, ctx)
        begun = ctx.enter_context(nc.semaphore("begun"))
        with nc.Block() as block:
            @block.sync
            def _(sp):
                sp.dma_start(table[:], I["const_table"]).then_inc(begun, 16)
                x = I["L0_attn_a_x"].rearrange("b (t p) d -> p (b t) d", p=P)
                for b in range(BATCH):
                    sp.dma_start(X[:, b * T:(b + 1) * T], x[:, b * T:(b + 1) * T]).then_inc(begun, 16)
                sp.wait_ge(begun, 16 * (BATCH + 1))
        for phase in phases:
            phase(nc, X, C, I)
        stored = ctx.enter_context(nc.semaphore("stored"))
        with nc.Block() as block:
            @block.sync
            def _(sp):
                y = out.rearrange("b (t p) d -> p (b t) d", p=P)
                for b in range(BATCH):
                    sp.dma_start(y[:, b * T:(b + 1) * T], X[:, b * T:(b + 1) * T]).then_inc(stored, 16)
                sp.wait_ge(stored, 16 * BATCH)


def phase_attention(nc, X, C, I):
    A = {k: I["L0_attn_a_" + k] for k in ("Wq", "Wk", "Wv", "Wo", "Aq", "Ak", "Av", "Ao", "Bq", "Bk", "Bv", "Bo")}
    A["starts"], A["rope"] = I["L0_attn_a_lora_start_indices"], I["const_rope"]
    attention(nc, X, C, A)


def phase_ffn(which):
    def phase(nc, X, C, I):
        C["sems"].clear("f_")
        F = {k: I["L0_ffn_" + k] for k in ("Wr", "br", "Wg", "Wu", "Wd")}
        F["x_slots"] = nc.dram_tensor(which + "x_slots", (SLOTS * P, D), F32, kind="Internal").ap()
        F["y_slots"] = nc.dram_tensor(which + "y_slots", (SLOTS * P, D), F32, kind="Internal").ap()
        routed_ffn(nc, X, C, F, which)
    return phase


def phase_mamba(nc, X, C, I):
    mamba(nc, X, C, {k: I["L0_attn_b_" + k]
                     for k in ("w_in", "conv_w", "conv_b", "dt_bias", "A_log", "D", "norm_w", "w_out")})


PHASES = [phase_attention, phase_ffn("g1_"), phase_mamba, phase_ffn("g2_")]


def kernel(**inputs):
    import concourse.bacc as bacc
    from concourse.bass_utils import run_bass_kernel_spmd

    nc = bacc.Bacc("TRN2", target_bir_lowering=False, num_devices=1)
    arrays = {k: np.ascontiguousarray(v) for k, v in {**inputs, **constants()}.items()}
    I = {k: nc.dram_tensor(k, a.shape, mybir.dt.from_np(a.dtype), kind="ExternalInput").ap()
         for k, a in arrays.items()}
    out = nc.dram_tensor("out", (BATCH, SEQ, D), F32, kind="ExternalOutput").ap()
    program(nc, I, out, PHASES)
    return run_bass_kernel_spmd(nc, [arrays], core_ids=[0]).results[0]["out"]
```

```python
from contextlib import ExitStack

import numpy as np

import concourse.bass as bass
from concourse import mybir

F32 = mybir.dt.float32
F32R = mybir.dt.float32r
BF16 = mybir.dt.bfloat16
I32 = mybir.dt.int32
U32 = mybir.dt.uint32
ALU = mybir.AluOpType
ACT = mybir.ActivationFunctionType
AX = mybir.AxisListType.X

P = 128
BATCH, SEQ, D = 4, 1024, 256
DT = D // P
T = SEQ // P
NT = BATCH * T
HEADS, DH = 16, 16
GROUP = 4
GROUPS = HEADS // GROUP
ADAPTERS, RANK = 4, 16
EXPERTS, FF = 4, 1024
SLOTS = NT + EXPERTS - 1
LN_EPS = 1e-5
MASKED = -1e30
STATE, INNER, CONV, TAPS, MHEADS, HDIM = 128, 512, 768, 4, 8, 64
CT = CONV // P
IN_PROJ = 2 * INNER + 2 * STATE + MHEADS


class Semaphores:

    def __init__(self, nc, ctx):
        self.nc, self.ctx, self.held = nc, ctx, {}

    def __call__(self, name):
        if name not in self.held:
            self.held[name] = self.ctx.enter_context(self.nc.semaphore(name))
        return self.held[name]

    def clear(self, prefix):
        with self.nc.Block() as block:
            @block.sync
            def _(sp):
                for name, held in self.held.items():
                    if name.startswith(prefix):
                        sp.sem_clear(held)


class Steps:

    def __init__(self, eng, sem, base=0):
        self.eng, self.sem, self.base, self.n = eng, sem, base, 0

    def __call__(self, ins, wait=True):
        ins.then_inc(self.sem, 1)
        self.n += 1
        if wait:
            self.eng.wait_ge(self.sem, self.base + self.n)


def row_stats(nc, step, tiles, stats, mean_var, var_eps, done):
    for t, x in enumerate(tiles):
        step(nc.vector.bn_stats(stats[:, t], x), wait=t + 1 == len(tiles))
    step(nc.vector.memset(var_eps, 0.0), wait=False)
    for t in range(len(tiles)):
        step(nc.vector.bn_aggr(mean_var[:, t], stats[:, t]), wait=t + 1 == len(tiles))
    nc.vector.tensor_scalar(var_eps, mean_var[:, :, 1], LN_EPS, None, ALU.add).then_inc(done, 1)


def inverse_root(nc, out, x, C):
    return nc.gpsimd.tensor_tensor(out, x, C["minus_half"].to_broadcast(list(out.shape)), ALU.pow)


def attention(nc, X, C, A):
    STACK = 64
    PAIRS = HEADS // 2
    RING = 8
    UNITS = T * GROUP
    HALF = T // 2
    rising = [(i, u, c) for i in range(T) for u in range(GROUP) for c in range(1 + i // HALF)]
    falling = [(i, u, c) for i in reversed(range(T)) for u in range(GROUP) for c in range(1 + i // HALF)]
    CHUNKS = len(rising)
    FIRST, LAST, SLACK = 1, 6 * GROUP, 650
    issued, pe_at, dve_at = [0] * (FIRST + 1), 0., 0.
    for n in range(FIRST, UNITS):
        wide, before = P * (T - n // GROUP), P * (T - (n // GROUP - 1) % T)
        pe_at += max(wide * 0.42 + 60 + before * 0.42, wide * 0.85 + (250 if n < GROUP else 50))
        k = issued[-1]
        while k < CHUNKS and (n == LAST or dve_at - pe_at < SLACK):
            w = min(512, (falling[k][0] + 1) * P - 512 * falling[k][2])
            pe_at += w * 0.42 + 30
            dve_at = max(dve_at, pe_at) + w * 1.04 + 66
            k += 1
        issued.append(k)
    with ExitStack() as ctx:
        def sb(name, shape, dt=F32):
            return ctx.enter_context(nc.sbuf_tensor("a_" + name, shape, dt))

        def sem(name):
            return C["sems"]("a_" + name)

        ps_e = ctx.enter_context(nc.psum_tensor("a_ps_e", [P, 2, 2, 512], F32))
        ps_m = ctx.enter_context(nc.psum_tensor("a_ps_m", [P, 2, 512], F32))
        ps_a = ctx.enter_context(nc.psum_tensor("a_ps_a", [P, 2, 512], F32))

        probs = sb("probs", [P, RING, SEQ])
        spare = probs[:].rearrange("p r q -> p (r q)")
        w_nat = spare[:, 0:2048].rearrange("p (m t d) -> p m t d", m=4, t=2)
        b_nat = spare[:, 2048:2560].rearrange("p (m t e r) -> p m t e r", m=4, t=2, e=ADAPTERS)
        k_tok = spare[:, 3072:5120].bitcast(F32R).rearrange("p (a h c) -> p a h c", a=2, h=HEADS)
        rot = spare[:, 5120:6144].rearrange("p (a b d) -> p a b d", a=2, b=2)
        rope_a, rope_b = spare[:, 6144:6656], spare[:, 6656:7168]
        xn = spare[:, 7168:7680].rearrange("p (a d) -> p a d", a=2)
        xn_t = spare[:, 7680:8192].rearrange("p (a d) -> p a d", a=2)
        acc = probs[:, RING - 1, :]
        a_cat = sb("a_cat", [64, 4, D])
        w_t = sb("w_t", [P, 4, DT, D])
        b_t = sb("b_t", [64, 4, D])
        w_eff = sb("w_eff", [P, DT, 4, D])
        starts_i = sb("starts_i", [64, ADAPTERS], I32)
        starts = sb("starts", [64, ADAPTERS])
        picked = sb("picked", [64, 4, BATCH])
        ident_b = sb("ident_b", [P, P], BF16)
        mask_b = sb("mask_b", [P, 2, P], BF16)
        rope = sb("rope", [P, T, 2, DH])
        mean_var = sb("mean_var", [P, NT, 2])
        var_eps = sb("var_eps", [P, NT])
        rstd = sb("rstd", [P, NT])
        q_tok = sb("q_tok", [P, T, HEADS, STACK], F32R)
        q_st = sb("q_st", [P, PAIRS, SEQ], F32R)
        k_st = sb("k_st", [P, PAIRS, SEQ], F32R)
        vals = sb("vals", [P, T, (HEADS + 1) * 17])
        peak = sb("peak", [P, GROUP, T, 2])
        recip = sb("recip", [P, T * GROUP])
        heads_out = sb("heads_out", [P, T, D])
        ho_t = spare[:, 0:512].rearrange("p (a d) -> p a d", a=2)
        stats = heads_out[:, 0, 0:NT * 6].rearrange("p (t s) -> p t s", s=6)
        a_sel = heads_out[0:64].rearrange("p (m t) d -> p m (t d)", m=4)[:, :, 0:D]

        loaded, fixed, folded, cast, w_ready = (sem(n) for n in ("loaded", "fixed", "folded", "cast", "w_ready"))
        dve_step, wt_ps, wt_sb, sel_ready, wl_ps, wl_used = (
            sem(n) for n in ("dve_step", "wt_ps", "wt_sb", "sel_ready", "wl_ps", "wl_used"))
        xn_ready, xt_ps, xt_sb, qk_ps, rot_ready, v_copied = (
            sem(n) for n in ("xn_ready", "xt_ps", "xt_sb", "qk_ps", "rot_ready", "v_copied"))
        hi_ready, lo_ready, stack_ps, stack_sb, v_ps, again_dve = (
            sem(n) for n in ("hi_ready", "lo_ready", "stack_ps", "stack_sb", "v_ps", "again_dve"))
        score_ps, chunk_max, max_ready, again_ps, again_act = (
            sem(n) for n in ("score_ps", "chunk_max", "max_ready", "again_ps", "again_act"))
        shifted_ps, exp_done, pv_done, acc_sb, acc_t, normed = (
            sem(n) for n in ("shifted_ps", "exp_done", "pv_done", "acc_sb", "acc_t", "normed"))
        stats_ready, rstd_ready = sem("stats_ready"), sem("rstd_ready")
        ot_ps, ot_sb, proj_ps, x_added, half_turned = (
            sem(n) for n in ("ot_ps", "ot_sb", "proj_ps", "x_added", "half_turned"))

        LOADS = 4 * 3 + 2
        block = ctx.enter_context(nc.Block())

        @block.sync
        def _(sp):
            for m, name in enumerate("qkvo"):
                sp.dma_start(w_nat[:, m], A["W" + name].rearrange("(t p) d -> p t d", p=P)).then_inc(loaded, 16)
                for t in range(2):
                    sp.dma_start(b_nat[:, m, t], A["B" + name][:, t * P:(t + 1) * P, :].rearrange("e p r -> p e r")
                                 ).then_inc(loaded, 16)
                sp.dma_start(a_cat[:, m], A["A" + name].rearrange("e r d -> (e r) d")).then_inc(loaded, 16)
            sp.dma_start(starts_i[:], A["starts"].rearrange("(a n) -> a n", a=1).to_broadcast([64, ADAPTERS])
                         ).then_inc(loaded, 16)
            sp.dma_start(rope[:], A["rope"].rearrange("(t p) a f -> p t a f", p=P)).then_inc(loaded, 16)
            sp.wait_ge(loaded, 16 * (LOADS + 4))

        @block.vector
        def _(dve):
            step = Steps(dve, fixed)
            dve.wait_ge(C["begun"], 16 * (BATCH + 1))
            step(nc.vector.tensor_copy(ident_b[:], C["ident"]))
            step(nc.vector.tensor_copy(mask_b[:], C["neg"]))
            step(nc.vector.memset(q_tok[:].bitcast(F32), 0.0))
            step(nc.vector.memset(vals[:], 1.0))
            row_stats(nc, step, [X[:, t] for t in range(NT)], stats, mean_var, var_eps[:], stats_ready)
            dve.wait_ge(loaded, 16 * (LOADS + 4))
            step(nc.vector.tensor_copy(starts[:], starts_i[:]))
            for b in range(BATCH):
                step(nc.vector.tensor_scalar(picked[:, 0, :], starts[:], float(b), None, ALU.is_le))
                step(nc.vector.tensor_reduce(picked[:, 1, 0:1], picked[:, 0, :], AX, ALU.add))
                step(nc.vector.tensor_scalar(picked[:, 2, 0:1], picked[:, 1, 0:1], -1.0, 0.0, ALU.add, ALU.max))
                step(nc.vector.tensor_scalar(picked[:, 3, b:b + 1], picked[:, 2, 0:1], C["adapter"][0:64, :], None,
                                             ALU.is_equal))
            for m in range(4):
                dve.wait_ge(wt_ps, m + 1)
                nc.vector.tensor_copy(w_t[:, m], ps_e[:, m // 2, m % 2, :]).then_inc(wt_sb, 1)
            for m in range(4):
                dve.wait_ge(wt_ps, 5 + m)
                nc.vector.tensor_copy(b_t[:, m], ps_e[0:64, m // 2, m % 2, 0:D]).then_inc(wt_sb, 1)
            dve.wait_ge(wt_sb, 8)
            dve.sem_inc(chunk_max, 2)
            dve.sem_inc(x_added, 1)
            dve.wait_ge(rstd_ready, 1)
            NSTEP = 3 + 2 * T + GROUPS * 3
            with dve.Fori(0, BATCH) as b:
                step = Steps(dve, dve_step, b * NSTEP)
                for m in range(4):
                    if m == 0:
                        dve.wait_ge(x_added, b * T + 1)
                    nc.vector.tensor_scalar(a_sel[:, m], a_cat[:, m], picked[:, 3, bass.ds(b, 1)], None,
                                            ALU.mult).then_inc(sel_ready, 1)
                step(nc.vector.memset(q_tok[:, :, :, 32:34].bitcast(F32), 0.0), wait=False)
                step(nc.vector.memset(k_tok[:, :, :, 34:48].bitcast(F32), 0.0), wait=False)
                step(nc.vector.memset(k_tok[:, :, :, 32:34].bitcast(F32), 1.0), wait=False)

                def norm(t):
                    if t >= 2:
                        dve.wait_ge(xt_ps, b * T + t - 1)
                    nc.vector.tensor_scalar(xn[:, t % 2], X[:, bass.ds(b * T + t, 1), :].rearrange("p a d -> p (a d)"),
                                            mean_var[:, bass.ds(b * T + t, 1), 0], rstd[:, bass.ds(b * T + t, 1)],
                                            ALU.subtract, ALU.mult
                                            ).then_inc(xn_ready, 1)

                def rotate(t):
                    dve.wait_ge(qk_ps, b * T + t + 1)
                    qk = ps_e[:, 0, 0, :]
                    cos = rope[:, t, 0:1, :].to_broadcast([P, 2 * HEADS, DH])
                    sin = rope[:, t, 1, :].rearrange("p (i two) -> p two i", two=2)
                    step(nc.vector.tensor_tensor(rope_a.rearrange("p (h d) -> p h d", d=DH),
                                                 qk.rearrange("p (h d) -> p h d", d=DH), cos, ALU.mult))
                    pair = qk.rearrange("p (h i two) -> p two h i", two=2, i=DH // 2)
                    out = rope_b.rearrange("p (h i two) -> p two h i", two=2, i=DH // 2)
                    for odd in range(2):
                        last = nc.vector.tensor_tensor(
                            out[:, odd], pair[:, 1 - odd],
                            sin[:, odd:odd + 1, :].to_broadcast([P, 2 * HEADS, DH // 2]), ALU.mult)
                        if odd == 0:
                            last.then_inc(half_turned, 1)
                    step(last)
                    dve.wait_ge(half_turned, b * T + t + 1)
                    if t >= 2:
                        dve.wait_ge(lo_ready, b * T + t - 1)
                    nc.vector.tensor_tensor(rot[:, t % 2].rearrange("p a d -> p (a d)"), rope_a, rope_b,
                                            ALU.add).then_inc(rot_ready, 1)

                def maxima(g, chunks, first):
                    for n, (i, u, c) in enumerate(chunks, first):
                        dve.wait_ge(score_ps, (b * GROUPS + g) * CHUNKS + n + 1)
                        w = min(512, (i + 1) * P - 512 * c)
                        nc.vector.tensor_reduce(peak[:, u, i, c:c + 1], ps_m[:, n % 2, 0:w], AX, ALU.max
                                                ).then_inc(chunk_max, 1)

                norm(0)
                norm(1)
                for m in range(4):
                    dve.wait_ge(wl_ps, b * 4 + m + 1)
                    nc.vector.tensor_tensor(w_eff[:, :, m, :], w_t[:, m],
                                            ps_e[:, m // 2, m % 2, :].rearrange("p (t o) -> p t o", t=DT),
                                            ALU.add).then_inc(wl_used, 1)
                for s in range(1, T + 3):
                    if s <= T:
                        rotate(s - 1)
                    if s + 1 < T:
                        norm(s + 1)
                    if s >= 3:
                        maxima(0, [x for x in rising if x[0] == s - 3],
                               sum(x[0] < s - 3 for x in rising))

                def fold(g):
                    dve.wait_ge(chunk_max, (b * GROUPS + g + 1) * CHUNKS + 2)
                    h = T // 2
                    step(nc.vector.tensor_tensor(peak[:, :, h:, 0], peak[:, :, h:, 0], peak[:, :, h:, 1], ALU.max))
                    to = q_tok[:, :, g * GROUP:(g + 1) * GROUP, :].rearrange("p t u c -> p u t c")
                    step(nc.vector.tensor_scalar(to[:, :, :, 32], peak[:, :, :, 0], -1.0, None, ALU.mult))
                    nc.vector.scalar_tensor_tensor(to[:, :, :, 33], peak[:, :, :, 0], -1.0,
                                                   to[:, :, :, 32].bitcast(F32), ALU.mult, ALU.subtract
                                                   ).then_inc(max_ready, 1)

                def collect(g):
                    dve.wait_ge(acc_t, b * GROUPS + g + 1)
                    at = ps_a[:].rearrange("p b (c u f) -> p (b c u) f", u=GROUP, f=32)
                    step(nc.vector.reciprocal(recip[:], at[:, :, 16]))
                    nc.vector.tensor_tensor(
                        heads_out[:, :, g * GROUP * DH:(g + 1) * GROUP * DH].rearrange("p t (u f) -> p t u f", f=DH),
                        at[:, :, 0:DH].rearrange("p (t u) f -> p t u f", u=GROUP),
                        recip[:].rearrange("p (t u) -> p t u", u=GROUP).unsqueeze(3).to_broadcast([P, T, GROUP, DH]),
                        ALU.mult).then_inc(normed, 1)

                def again(g):
                    for n in (0, 2):
                        dve.wait_ge(again_ps, (b * GROUPS + g) * 4 + n + 1)
                        nc.vector.tensor_copy(q_st[:, 2 * g + n // 2, 0:512], ps_m[:, 0, :]).then_inc(again_dve, 1)

                fold(0)
                again(0)
                for g in range(GROUPS):
                    if g + 1 < GROUPS:
                        maxima(g + 1, falling[:issued[GROUP]], 0)
                    if g >= 1:
                        collect(g - 1)
                    if g + 1 < GROUPS:
                        maxima(g + 1, falling[issued[GROUP]:], issued[GROUP])
                        fold(g + 1)
                        again(g + 1)
                collect(GROUPS - 1)
                for t in range(T):
                    dve.wait_ge(proj_ps, b * T + t + 1)
                    x = X[:, bass.ds(b * T + t, 1), :].rearrange("p a d -> p (a d)")
                    nc.vector.tensor_tensor(x, x, ps_e[:, t % 2, 0, 0:D], ALU.add).then_inc(x_added, 1)
                dve.wait_ge(x_added, b * T + T + 1)
                assert step.n == NSTEP, step.n

        @block.gpsimd
        def _(pool):
            pool.wait_ge(stats_ready, 1)
            inverse_root(nc, rstd[:], var_eps[:], C).then_inc(rstd_ready, 1)
            with pool.Fori(0, BATCH) as b:
                for t in range(T):
                    r = rot[:, t % 2].rearrange("p a (h d) -> p a h d", d=DH)
                    pool.wait_ge(hi_ready, b * T + t + 1)
                    q, k = q_tok[:, t], k_tok[:, t % 2]
                    nc.gpsimd.tensor_tensor(q[:, :, 48:64], r[:, 0], q[:, :, 0:16].bitcast(F32), ALU.subtract)
                    nc.gpsimd.tensor_tensor(k[:, :, 16:32], r[:, 1], k[:, :, 0:16].bitcast(F32), ALU.subtract
                                            ).then_inc(lo_ready, 1)

        @block.scalar
        def _(act):
            act.sem_inc(exp_done, 2)
            act.wait_ge(fixed, 4)
            with act.Fori(0, BATCH) as b:
                def turned(t):
                    act.wait_ge(xt_ps, b * T + t + 1)
                    if t >= 2:
                        act.wait_ge(qk_ps, b * T + t - 1)
                    nc.scalar.copy(xn_t[:, t % 2], ps_e[:, 1, t % 2, 0:D]).then_inc(xt_sb, 1)

                def high(t):
                    act.wait_ge(rot_ready, b * T + t + 1)
                    r = rot[:, t % 2].rearrange("p a (h d) -> p a h d", d=DH)
                    q = q_tok[:, t].rearrange("p h (s d) -> p h s d", d=DH)
                    k = k_tok[:, t % 2].rearrange("p h (s d) -> p h s d", d=DH)
                    twice = [P, HEADS, 2, DH]
                    nc.scalar.copy(q[:, :, 0:2], r[:, 0].unsqueeze(2).to_broadcast(twice))
                    if t >= 2:
                        act.wait_ge(stack_ps, (b * T + t - 2) * 4 + 2)
                    nc.scalar.copy(k[:, :, 0:4:3], r[:, 1].unsqueeze(2).to_broadcast(twice)).then_inc(hi_ready, 1)

                def values(t):
                    act.wait_ge(v_ps, b * T + t + 1)
                    nc.scalar.copy(vals[:, t].rearrange("p (h c) -> p h c", c=17)[:, 0:HEADS, 0:DH],
                                   ps_e[:, 0, 1, 0:D].rearrange("p (h d) -> p h d", d=DH)).then_inc(v_copied, 1)

                def stack(t, n):
                    act.wait_ge(stack_ps, (b * T + t) * 4 + n + 1)
                    to = (k_st, q_st)[n // 2][:, 4 * (n % 2):4 * (n % 2) + 4, t * P:(t + 1) * P]
                    nc.scalar.copy(to, ps_a[:, n % 2].rearrange("p (c k) -> p c k", k=P)).then_inc(stack_sb, 1)

                turned(0)
                for s in range(T + 2):
                    if s + 1 < T:
                        turned(s + 1)
                    if s >= 2:
                        stack(s - 2, 0)
                        stack(s - 2, 1)
                    if 1 <= s <= T:
                        high(s - 1)
                    if s < T:
                        values(s)
                    if s >= 2:
                        stack(s - 2, 2)
                        stack(s - 2, 3)

                def again(g, n):
                    act.wait_ge(again_ps, (b * GROUPS + g) * 4 + n + 1)
                    nc.scalar.copy(q_st[:, 2 * g + n // 2, 512:1024], ps_m[:, 1, :]).then_inc(again_act, 1)

                def sums(g):
                    act.wait_ge(pv_done, (b * GROUPS + g) * T + T)
                    nc.scalar.copy(acc, ps_a[:].rearrange("p b q -> p (b q)")).then_inc(acc_sb, 1)

                again(0, 1)
                again(0, 3)
                for S in range(GROUPS * T):
                    g, j = S // T, S % T
                    for u in range(GROUP):
                        n = S * GROUP + u
                        act.wait_ge(shifted_ps, b * GROUPS * UNITS + n + 1)
                        if S >= 2 and u == 0:
                            act.wait_ge(pv_done, b * GROUPS * T + S - 1)
                        if g >= 1 and n % UNITS == RING - 1:
                            act.wait_ge(acc_t, b * GROUPS + g)
                        nc.scalar.activation(probs[:, n % RING, j * P:],
                                             ps_e[:, n % 2].rearrange("p b q -> p (b q)")[:, j * P:],
                                             ACT.Exp, scale=DH ** -0.5).then_inc(exp_done, 1)
                        if j == 0 and u == 1 and g >= 1:
                            sums(g - 1)
                        if j == T - 1 and u % 2 == 1 and g + 1 < GROUPS:
                            again(g + 1, u)
                sums(GROUPS - 1)
                for t in range(T):
                    act.wait_ge(ot_ps, b * T + t + 1)
                    if t >= 2:
                        act.wait_ge(proj_ps, b * T + t - 1)
                    nc.scalar.copy(ho_t[:, t % 2], ps_a[:, t % 2, 0:D]).then_inc(ot_sb, 1)

        @block.tensor
        def _(pe):
            ident = C["ident"]
            pe.wait_ge(loaded, 16 * (LOADS + 4))
            pe.wait_ge(C["begun"], 16 * (BATCH + 1))
            for m in range(4):
                for d in range(DT):
                    for o in range(2):
                        last = nc.tensor.transpose(ps_e[:, m // 2, m % 2, d * D + o * P:d * D + o * P + P],
                                                   w_nat[:, m, o, d * P:(d + 1) * P], ident)
                last.then_inc(wt_ps, 1)
            for m in range(4):
                pe.wait_ge(wt_sb, m + 1)
                for o in range(2):
                    last = nc.tensor.transpose(ps_e[0:64, m // 2, m % 2, o * P:(o + 1) * P],
                                               b_nat[:, m, o].rearrange("p e r -> p (e r)"), ident)
                last.then_inc(wt_ps, 1)
            pe.wait_ge(fixed, 4)
            pe.wait_ge(wt_sb, 8)
            with pe.Fori(0, BATCH) as b:
                pe.wait_ge(x_added, b * T + 1)
                for m in range(4):
                    pe.wait_ge(sel_ready, b * 4 + m + 1)
                    for d in range(DT):
                        last = nc.tensor.matmul(ps_e[:, m // 2, m % 2, d * D:(d + 1) * D],
                                                a_sel[:, m, d * P:(d + 1) * P], b_t[:, m], start=(d == 0),
                                                stop=(d == DT - 1), skip_group_check=True)
                    last.then_inc(wl_ps, 1)
                pe.wait_ge(wl_used, b * 4 + 4)

                def turn(t):
                    pe.wait_ge(xn_ready, b * T + t + 1)
                    if t >= 2:
                        pe.wait_ge(xt_sb, b * T + t - 1)
                    for d in range(DT):
                        last = nc.tensor.transpose(ps_e[:, 1, t % 2, d * P:(d + 1) * P],
                                                   xn[:, t % 2, d * P:(d + 1) * P], ident)
                    last.then_inc(xt_ps, 1)

                def stack(t, n):
                    if n == 0:
                        pe.wait_ge(lo_ready, b * T + t + 1)
                    if t >= 1 or n >= 2:
                        pe.wait_ge(stack_sb, (b * T + t) * 4 + n - 1)
                    tok = (k_tok[:, t % 2], q_tok[:, t])[n // 2]
                    for c in range(4):
                        h = 8 * (n % 2) + 2 * c
                        last = nc.tensor.transpose(ps_a[:, n % 2, c * P:(c + 1) * P],
                                                   tok[:, h:h + 2, :].bitcast(F32).rearrange("p h c -> p (h c)"), ident)
                    last.then_inc(stack_ps, 1)

                def project_v(t):
                    pe.wait_ge(xt_sb, b * T + t + 1)
                    if t >= 1:
                        pe.wait_ge(v_copied, b * T + t)
                    for d in range(DT):
                        last = nc.tensor.matmul(ps_e[:, 0, 1, 0:D], xn_t[:, t % 2, d * P:(d + 1) * P], w_eff[:, d, 2],
                                                start=(d == 0), stop=(d == DT - 1))
                    last.then_inc(v_ps, 1)

                def project_qk(t):
                    if t >= 1:
                        pe.wait_ge(rot_ready, b * T + t)
                    for d in range(DT):
                        last = nc.tensor.matmul(ps_e[:, 0, 0, :], xn_t[:, t % 2, d * P:(d + 1) * P],
                                                w_eff[:, d, 0:2].rearrange("p m o -> p (m o)"), start=(d == 0),
                                                stop=(d == DT - 1))
                    last.then_inc(qk_ps, 1)

                def scores(g, chunks, first):
                    for n, (i, u, c) in enumerate(chunks, first):
                        h = g * GROUP + u
                        rows = slice(64 * (h % 2), 64 * (h % 2) + 64)
                        w = min(512, (i + 1) * P - 512 * c)
                        diag = c == i // HALF
                        pe.wait_ge(chunk_max, (b * GROUPS + g) * CHUNKS + n + 1)
                        last = nc.tensor.matmul(ps_m[:, n % 2, 0:w], q_st[rows, h // 2, i * P:(i + 1) * P],
                                                k_st[rows, h // 2, 512 * c:512 * c + w], start=True,
                                                stop=not diag)
                        if diag:
                            last = nc.tensor.matmul(ps_m[:, n % 2, w - P:w], ident_b[:], mask_b[:, 0], start=False,
                                                    stop=True)
                        last.then_inc(score_ps, 1)

                turn(0)
                for s in range(T + 3):
                    if s + 1 < T:
                        turn(s + 1)
                    first = [x for x in rising if x[0] == s - 3]
                    before = sum(x[0] < s - 3 for x in rising)
                    if s >= 3:
                        pe.wait_ge(stack_sb, (b * T + s - 3) * 4 + 4)
                    per = len(first) // GROUP
                    for n in range(GROUP):
                        if 2 <= s < T + 2:
                            stack(s - 2, n)
                        if n == 1 and s < T:
                            project_v(s)
                        if n >= 1:
                            scores(0, first[(n - 1) * per:n * per], before + (n - 1) * per)
                    scores(0, first[3 * per:], before + 3 * per)
                    if s < T:
                        project_qk(s)

                def again(g, n):
                    if n == 0:
                        pe.wait_ge(max_ready, b * GROUPS + g + 1)
                    if n == 2:
                        pe.wait_ge(again_dve, (b * GROUPS + g) * 2 + 1)
                    if n == 3:
                        pe.wait_ge(again_act, (b * GROUPS + g) * 2 + 1)
                    h = g * GROUP + 2 * (n // 2)
                    for k in range(4):
                        last = nc.tensor.transpose(ps_m[:, n % 2, k * P:(k + 1) * P],
                                                   q_tok[:, (n % 2) * 4 + k, h:h + 2, :].bitcast(F32).rearrange(
                                                       "p h c -> p (h c)"), ident)
                    last.then_inc(again_ps, 1)

                def shifted(g, j, u):
                    h, n = g * GROUP + u, j * GROUP + u
                    rows = slice(64 * (h % 2), 64 * (h % 2) + 64)
                    if j == 0 and u % 2 == 0:
                        pe.wait_ge(again_dve, (b * GROUPS + g) * 2 + u // 2 + 1)
                        pe.wait_ge(again_act, (b * GROUPS + g) * 2 + u // 2 + 1)
                    pe.wait_ge(exp_done, (b * GROUPS + g) * UNITS + n + 1)
                    for c in range(j // HALF, 2):
                        q0 = max(j * P, 512 * c)
                        diag = q0 == j * P
                        last = nc.tensor.matmul(ps_e[:, n % 2, c, q0 - 512 * c:512], k_st[rows, h // 2, j * P:(j + 1) * P],
                                                q_st[rows, h // 2, q0:512 * (c + 1)], start=True, stop=not diag)
                        if diag:
                            last = nc.tensor.matmul(ps_e[:, n % 2, c, q0 - 512 * c:q0 - 512 * c + P], ident_b[:],
                                                    mask_b[:, 1], start=False, stop=True)
                    last.then_inc(shifted_ps, 1)

                def weigh(S, c):
                    g, j = S // T, S % T
                    pe.wait_ge(exp_done, b * GROUPS * UNITS + (S + 1) * GROUP + 2)
                    if j == 0 and g >= 1:
                        pe.wait_ge(normed, b * GROUPS + g)
                    q0 = max(j * P, 512 * c)
                    for u in range(GROUP):
                        last = nc.tensor.matmul(ps_a[32 * u:32 * u + 32, c, q0 - 512 * c:512],
                                                vals[:, j, 17 * (g * GROUP + u):17 * (g * GROUP + u) + 32],
                                                probs[:, (S * GROUP + u) % RING, q0:512 * (c + 1)],
                                                start=(j == 0), stop=(j == 4 * c + 3), tile_position=(0, 32 * u))
                    if c == 1:
                        last.then_inc(pv_done, 1)

                def turn_acc(g):
                    pe.wait_ge(acc_sb, b * GROUPS + g + 1)
                    for t in range(T):
                        last = nc.tensor.transpose(ps_a[:, t // 4, (t % 4) * P:(t % 4 + 1) * P],
                                                   acc[:, t * P:(t + 1) * P], ident)
                    last.then_inc(acc_t, 1)

                for n in range(4):
                    again(0, n)
                for S in range(GROUPS * T):
                    g, j = S // T, S % T
                    for u in range(GROUP):
                        n = j * GROUP + u
                        shifted(g, j, u)
                        if S >= 1 and u == 1 and (S - 1) % T < HALF:
                            weigh(S - 1, 0)
                        if S >= 1 and u == (2 if j else 1):
                            weigh(S - 1, 1)
                        if g >= 1 and n == 3:
                            turn_acc(g - 1)
                        if g + 1 < GROUPS:
                            if n == FIRST:
                                pe.wait_ge(again_dve, (b * GROUPS + g) * 2 + 2)
                                pe.wait_ge(again_act, (b * GROUPS + g) * 2 + 2)
                            scores(g + 1, falling[issued[n]:issued[n + 1]], issued[n])
                            if j == T - 1:
                                again(g + 1, u)
                weigh(GROUPS * T - 1, 1)
                turn_acc(GROUPS - 1)
                pe.wait_ge(normed, b * GROUPS + GROUPS)

                def turn_out(t):
                    if t >= 2:
                        pe.wait_ge(ot_sb, b * T + t - 1)
                    for d in range(DT):
                        last = nc.tensor.transpose(ps_a[:, t % 2, d * P:(d + 1) * P], heads_out[:, t, d * P:(d + 1) * P],
                                                   ident)
                    last.then_inc(ot_ps, 1)

                turn_out(0)
                for t in range(T):
                    if t + 1 < T:
                        turn_out(t + 1)
                    pe.wait_ge(ot_sb, b * T + t + 1)
                    if t >= 2:
                        pe.wait_ge(x_added, b * T + t)
                    for d in range(DT):
                        last = nc.tensor.matmul(ps_e[:, t % 2, 0, 0:D], ho_t[:, t % 2, d * P:(d + 1) * P],
                                                w_eff[:, d, 3], start=(d == 0), stop=(d == DT - 1))
                    last.then_inc(proj_ps, 1)


def routed_ffn(nc, X, C, F, name):
    FT = FF // P
    with ExitStack() as ctx:
        def sb(n, shape, dt=F32):
            return ctx.enter_context(nc.sbuf_tensor(name + n, shape, dt))

        def sem(n):
            return C["sems"]("f_" + n)

        ps_g = ctx.enter_context(nc.psum_tensor(name + "ps_g", [P, 2, 512], F32))
        ps_u = ctx.enter_context(nc.psum_tensor(name + "ps_u", [P, 2, 512], F32))
        ps_h = ctx.enter_context(nc.psum_tensor(name + "ps_h", [P, 2, 512], F32))
        ps_x = ctx.enter_context(nc.psum_tensor(name + "ps_x", [P, 512], F32))
        ps_y = ctx.enter_context(nc.psum_tensor(name + "ps_y", [P, 512], F32))

        w_gu = sb("w_gu", [P, EXPERTS, DT, 2, FF])
        w_d = sb("w_d", [P, EXPERTS, FT, D])
        w_r = sb("w_r", [P, DT, EXPERTS])
        b_r = sb("b_r", [P, EXPERTS])
        stats = sb("stats", [P, NT, 6])
        mean_var = sb("mean_var", [P, NT, 2])
        var_eps = sb("var_eps", [P, NT])
        rstd = sb("rstd", [P, NT])
        xn = sb("xn", [P, 4, D])
        xn_t = sb("xn_t", [P, 2, 2 * D])
        logits = sb("logits", [P, NT, EXPERTS])
        best = sb("best", [P, NT])
        expd = sb("expd", [P, NT, EXPERTS])
        top_w = sb("top_w", [P, NT])
        hot = sb("hot", [P, NT, EXPERTS])
        taken = sb("taken", [P, NT])
        hot_b = sb("hot_b", [P, NT, EXPERTS], BF16)
        before_b = sb("before_b", [P, P], BF16)
        ones_b = sb("ones_b", [P, P], BF16)
        ones = sb("ones", [P, NT])
        upto = sb("upto", [P, NT, EXPERTS])
        place = sb("place", [P, NT, EXPERTS])
        over = sb("over", [P, EXPERTS, NT])
        tiles = sb("tiles", [P, EXPERTS])
        first = sb("first", [P, EXPERTS])
        slot = sb("slot", [P, NT])
        slot_i = sb("slot_i", [P, NT], U32)
        owner = sb("owner", [P, 2, SLOTS])
        owner_i = sb("owner_i", [P, SLOTS], I32)
        xe = sb("xe", [P, D])
        xe_t = sb("xe_t", [P, D])
        gate = sb("gate", [P, FF])
        hid = sb("hid", [P, FF])
        hid_t = sb("hid_t", [P, FF])
        y = sb("y", [P, D])
        y_tok = sb("y_tok", [P, 4, D])
        warm = sb("warm", [P, 1])
        warmed = sem("warmed")

        loaded, w_loaded, step_done, stats_ready, rstd_ready = (
            sem(n) for n in ("loaded", "w_loaded", "step_done", "stats_ready", "rstd_ready"))
        xn_ready, xt_ps, xt_sb, logit_ps, pair_used, shifted, exp_ready = (
            sem(n) for n in ("xn_ready", "xt_ps", "xt_sb", "logit_ps", "pair_used", "shifted", "exp_ready"))
        hot_ready, rank_ps, slot_ready, owner_ready, again_ready = (
            sem(n) for n in ("hot_ready", "rank_ps", "slot_ready", "owner_ready", "again_ready"))
        sent = [C["sems"](f"{name}sent{k}") for k in range(4)]
        fetched = [C["sems"](f"{name}fetched{k}") for k in range(4)]
        xe_loaded, xe_ps, xe_sb, gate_ps, gate_sb, up_ps, hid_ready = (
            sem(n) for n in ("xe_loaded", "xe_ps", "xe_sb", "gate_ps", "gate_sb", "up_ps", "hid_ready"))
        ht_ps, ht_lo, ht_hi, y_ps, y_sb, y_stored, added, zeroed = (
            sem(n) for n in ("ht_ps", "ht_lo", "ht_hi", "y_ps", "y_sb", "y_stored", "added", "zeroed"))

        x_slots, y_slots = F["x_slots"], F["y_slots"]
        W_LOADS = 3 * EXPERTS
        block = ctx.enter_context(nc.Block())

        @block.sync
        def _(sp):
            sp.dma_start(w_r[:], F["Wr"].rearrange("(t p) e -> p t e", p=P)).then_inc(loaded, 16)
            sp.dma_start(b_r[:], F["br"].rearrange("(a e) -> a e", a=1).to_broadcast([P, EXPERTS])).then_inc(loaded, 16)
            sp.wait_ge(zeroed, 1)
            sp.dma_start(x_slots.rearrange("(t p) d -> p t d", p=P),
                         gate[:, 0:D].unsqueeze(1).to_broadcast([P, SLOTS, D])).then_inc(zeroed, 16)
            for e in range(EXPERTS):
                for k, w in enumerate(("Wg", "Wu")):
                    sp.dma_start(w_gu[:, e, :, k], F[w][e].rearrange("(t p) f -> p t f", p=P)).then_inc(w_loaded, 16)
                sp.dma_start(w_d[:, e], F["Wd"][e].rearrange("(t p) d -> p t d", p=P)).then_inc(w_loaded, 16)
            for k in range(4):
                sp.wait_ge(sent[k], 16 * (NT // 4))
            sp.sem_inc(y_stored, 16)
            sp.dma_start(xe[:], x_slots[0:P, :]).then_inc(xe_loaded, 16)
            with sp.Fori(1, SLOTS) as j:
                sp.wait_ge(xe_ps, j)
                sp.dma_start(xe[:], x_slots[bass.ds(j * P, P), :]).then_inc(xe_loaded, 16)
            sp.wait_ge(y_stored, 16 * SLOTS + 16)

        def x_tile(t):
            return X[:, bass.ds(t, 1), :].rearrange("p a d -> p (a d)")

        @block.vector
        def _(dve):
            step = Steps(dve, step_done)
            nc.vector.memset(gate[:], 0.0).then_inc(zeroed, 1)
            step(nc.vector.memset(ones_b[:], 1.0))
            step(nc.vector.memset(ones[:], 1.0))
            step(nc.vector.tensor_copy(before_b[:], C["before"]))
            row_stats(nc, step, [X[:, t, :] for t in range(NT)], stats, mean_var, var_eps[:], stats_ready)
            dve.wait_ge(rstd_ready, 1)
            dve.wait_ge(loaded, 32)

            def norm(t):
                if t >= 4:
                    dve.wait_ge(xt_ps, t // 2 - 1)
                nc.vector.tensor_scalar(xn[:, t % 4], X[:, t, :], mean_var[:, t, 0:1], rstd[:, t:t + 1],
                                        ALU.subtract, ALU.mult).then_inc(xn_ready, 1)

            for t in range(NT):
                norm(t)
            dve.wait_ge(logit_ps, 1)
            step(nc.vector.tensor_tensor(logits[:], ps_y[:, 0:NT * EXPERTS].rearrange("p (t e) -> p t e", e=EXPERTS),
                                         b_r[:].unsqueeze(1).to_broadcast([P, NT, EXPERTS]), ALU.add))

            def all_experts(v):
                return v.unsqueeze(2).to_broadcast([P, NT, EXPERTS])

            step(nc.vector.tensor_reduce(best[:], logits[:], AX, ALU.max))
            nc.vector.tensor_tensor(logits[:], logits[:], all_experts(best[:]), ALU.subtract).then_inc(shifted, 1)
            dve.wait_ge(shifted, 1)
            step(nc.vector.tensor_scalar(hot[:], logits[:], 0.0, None, ALU.is_equal))
            step(nc.vector.tensor_copy(taken[:], hot[:, :, 0]))
            for e in range(1, EXPERTS):
                step(nc.vector.tensor_tensor(hot[:, :, e], hot[:, :, e], taken[:], ALU.is_gt))
                step(nc.vector.tensor_tensor(taken[:], hot[:, :, e], taken[:], ALU.add))
            nc.vector.tensor_copy(hot_b[:], hot[:]).then_inc(hot_ready, 1)
            dve.wait_ge(exp_ready, 1)
            step(nc.vector.tensor_reduce(best[:], expd[:], AX, ALU.add))
            step(nc.vector.reciprocal(top_w[:], best[:]))
            dve.wait_ge(rank_ps, 1)
            totals = ps_g[:, 1, 0:P].rearrange("p (t e) -> p t e", e=EXPERTS)
            for e in range(EXPERTS):
                step(nc.vector.tensor_tensor_scan(upto[:, :, e], ones[:], totals[:, :, e], 0.0, ALU.mult, ALU.add))
            step(nc.vector.tensor_tensor(place[:], upto[:], totals, ALU.subtract))
            step(nc.vector.tensor_tensor(place[:], place[:], ps_g[:, 0, 0:P].rearrange("p (t e) -> p t e", e=EXPERTS),
                                         ALU.add))
            step(nc.vector.tensor_tensor(over[:], upto[:, NT - 1, :].unsqueeze(2).to_broadcast([P, EXPERTS, NT]),
                                         C["tile_tokens"].unsqueeze(1).to_broadcast([P, EXPERTS, NT]), ALU.is_gt))
            step(nc.vector.tensor_reduce(tiles[:], over[:], AX, ALU.add))
            step(nc.vector.memset(first[:], 0.0))
            for e in range(1, EXPERTS):
                step(nc.vector.tensor_tensor(first[:, e:e + 1], first[:, e - 1:e], tiles[:, e - 1:e], ALU.add))
            for e in range(EXPERTS):
                step(nc.vector.tensor_scalar(over[:, e, 0:1], first[:, e:e + 1], float(P), None, ALU.mult))
                step(nc.vector.tensor_scalar(place[:, :, e], place[:, :, e], over[:, e, 0:1], None, ALU.add))
            step(nc.vector.tensor_tensor(place[:], place[:], hot[:], ALU.mult))
            step(nc.vector.tensor_reduce(slot[:], place[:], AX, ALU.add))
            nc.vector.tensor_copy(slot_i[:], slot[:]).then_inc(slot_ready, 1)
            step(nc.vector.tensor_scalar(owner[:, 0, :], C["slot_no"], first[:, 1:2], None, ALU.is_ge))
            for e in range(2, EXPERTS):
                step(nc.vector.tensor_scalar(owner[:, 1, :], C["slot_no"], first[:, e:e + 1], None, ALU.is_ge))
                step(nc.vector.tensor_tensor(owner[:, 0, :], owner[:, 0, :], owner[:, 1, :], ALU.add))
            nc.vector.tensor_copy(owner_i[:], owner[:, 0, :]).then_inc(owner_ready, 1)
            for t in range(NT):
                if t >= 4:
                    dve.wait_ge(sent[t % 4], 16 * (t // 4))
                nc.vector.tensor_scalar(xn[:, t % 4], X[:, t, :], mean_var[:, t, 0:1], rstd[:, t:t + 1],
                                        ALU.subtract, ALU.mult).then_inc(again_ready, 1)

            def take(j):
                dve.wait_ge(xe_ps, j + 1)
                nc.vector.tensor_copy(xe_t[:], ps_x[:, 0:D]).then_inc(xe_sb, 1)

            def combine(j):
                dve.wait_ge(up_ps, j + 1)
                dve.wait_ge(gate_sb, j + 1)
                nc.vector.tensor_tensor(hid[:], gate[:], ps_u[:].rearrange("p b f -> p (b f)"), ALU.mult
                                        ).then_inc(hid_ready, 1)

            def hidden(j):
                dve.wait_ge(ht_ps, j + 1)
                nc.vector.tensor_copy(hid_t[:, 0:512], ps_h[:, 0]).then_inc(ht_lo, 1)

            take(0)
            with dve.Fori(0, SLOTS - 1) as j:
                combine(j)
                take(j + 1)
                hidden(j)
            combine(SLOTS - 1)
            hidden(SLOTS - 1)
            for t in range(NT):
                dve.wait_ge(fetched[t % 4], 16 * (t // 4 + 1))
                nc.vector.scalar_tensor_tensor(X[:, t, :], y_tok[:, t % 4], top_w[:, t:t + 1], X[:, t, :], ALU.mult,
                                               ALU.add).then_inc(added, 1)
            dve.wait_ge(added, NT)

        @block.gpsimd
        def _(pool):
            pool.wait_ge(stats_ready, 1)
            inverse_root(nc, rstd[:], var_eps[:], C).then_inc(rstd_ready, 1)
            pool.wait_ge(zeroed, 17)
            pool.wait_ge(slot_ready, 1)
            for t in range(NT):
                pool.wait_ge(again_ready, t + 1)
                nc.gpsimd.indirect_dma_start(
                    out=x_slots, out_offset=bass.IndirectOffsetOnAxis(ap=slot_i[:, t:t + 1], axis=0),
                    in_=xn[:, t % 4], in_offset=None).then_inc(sent[t % 4], 16)
            pool.wait_ge(y_stored, 16 * SLOTS + 16)
            for t in range(NT):
                if t >= 4:
                    pool.wait_ge(added, t - 3)
                nc.gpsimd.indirect_dma_start(
                    out=y_tok[:, t % 4], out_offset=None, in_=y_slots,
                    in_offset=bass.IndirectOffsetOnAxis(ap=slot_i[:, t:t + 1], axis=0)).then_inc(fetched[t % 4], 16)
            for k in range(4):
                pool.wait_ge(fetched[k], 16 * (NT // 4))

        @block.scalar
        def _(act):
            for k in range(NT // 2):
                act.wait_ge(xt_ps, k + 1)
                if k >= 2:
                    act.wait_ge(pair_used, k - 1)
                nc.scalar.copy(xn_t[:, k % 2], ps_u[:, k % 2]).then_inc(xt_sb, 1)
            act.wait_ge(shifted, 1)
            nc.scalar.activation(expd[:], logits[:], ACT.Exp).then_inc(exp_ready, 1)

            def activate(j):
                act.wait_ge(gate_ps, j + 1)
                nc.scalar.activation(gate[:], ps_g[:].rearrange("p b f -> p (b f)"), ACT.Silu).then_inc(gate_sb, 1)

            def hidden(j):
                act.wait_ge(ht_ps, j + 1)
                nc.scalar.copy(hid_t[:, 512:1024], ps_h[:, 1]).then_inc(ht_hi, 1)

            def result(j):
                act.wait_ge(y_ps, j + 1)
                act.wait_ge(y_stored, j * 16 + 16)
                nc.scalar.copy(y[:], ps_y[:, 0:D]).then_inc(y_sb, 1)
                act.wait_ge(y_sb, j + 1)
                act.dma_start(y_slots[bass.ds(j * P, P), :], y[:]).then_inc(y_stored, 16)

            activate(0)
            hidden(0)
            with act.Fori(1, SLOTS) as j:
                nc.scalar.activation(warm[:], ones[:, 0:1], ACT.Silu).then_inc(warmed, 1)
                act.wait_ge(warmed, j)
                activate(j)
                result(j - 1)
                hidden(j)
            result(SLOTS - 1)

        @block.tensor
        def _(pe):
            ident = C["ident"]

            def turn_pair(k):
                pe.wait_ge(xn_ready, 2 * k + 2)
                if k >= 2:
                    pe.wait_ge(xt_sb, k - 1)
                for n in range(2 * DT):
                    last = nc.tensor.transpose(ps_u[:, k % 2, n * P:(n + 1) * P],
                                               xn[:, 2 * (k % 2) + n // DT, (n % DT) * P:(n % DT + 1) * P], ident)
                last.then_inc(xt_ps, 1)

            def route(k):
                pe.wait_ge(xt_sb, k + 1)
                for n in range(2 * DT):
                    t, d = 2 * k + n // DT, n % DT
                    last = nc.tensor.matmul(ps_y[:, t * EXPERTS:(t + 1) * EXPERTS], xn_t[:, k % 2, n * P:(n + 1) * P],
                                            w_r[:, d], start=(d == 0), stop=(d == DT - 1))
                last.then_inc(logit_ps if k == NT // 2 - 1 else pair_used, 1)

            turn_pair(0)
            for k in range(NT // 2):
                if k + 1 < NT // 2:
                    turn_pair(k + 1)
                route(k)
            pe.wait_ge(hot_ready, 1)
            oh = hot_b[:].rearrange("p t e -> p (t e)")
            nc.tensor.matmul(ps_g[:, 0, 0:P], before_b[:], oh, start=True, stop=True)
            nc.tensor.matmul(ps_g[:, 1, 0:P], ones_b[:], oh, start=True, stop=True).then_inc(rank_ps, 1)
            pe.wait_ge(owner_ready, 1)
            pe.wait_ge(w_loaded, 16 * W_LOADS)

            def turn(j):
                pe.wait_ge(xe_loaded, j * 16 + 16)
                for d in range(DT):
                    last = nc.tensor.transpose(ps_x[:, d * P:(d + 1) * P], xe[:, d * P:(d + 1) * P], ident)
                last.then_inc(xe_ps, 1)

            def up(j, e):
                pe.wait_ge(xe_sb, j + 1)
                for k, ps, done in ((0, ps_g, gate_ps), (1, ps_u, up_ps)):
                    for c in range(FF // 512):
                        for d in range(DT):
                            last = nc.tensor.matmul(
                                ps[:, c], xe_t[:, d * P:(d + 1) * P],
                                w_gu[:, bass.ds(e, 1), d, k, c * 512:(c + 1) * 512].rearrange("p a f -> p (a f)"),
                                start=(d == 0), stop=(d == DT - 1))
                    last.then_inc(done, 1)

            def down(j, e):
                pe.wait_ge(ht_lo, j + 1)
                pe.wait_ge(ht_hi, j + 1)
                for f in range(FT):
                    last = nc.tensor.matmul(ps_y[:, 0:D], hid_t[:, f * P:(f + 1) * P],
                                            w_d[:, bass.ds(e, 1), f].rearrange("p a d -> p (a d)"), start=(f == 0),
                                            stop=(f == FT - 1))
                last.then_inc(y_ps, 1)

            def turn_hidden(j):
                pe.wait_ge(hid_ready, j + 1)
                for f in range(FT):
                    last = nc.tensor.transpose(ps_h[:, f // 4, (f % 4) * P:(f % 4 + 1) * P], hid[:, f * P:(f + 1) * P],
                                               ident)
                last.then_inc(ht_ps, 1)

            def expert_of(j):
                return pe.value_load(owner_i[0:1, bass.ds(j, 1)], min_val=0, max_val=EXPERTS - 1)

            turn(0)
            up(0, expert_of(0))
            turn(1)
            turn_hidden(0)
            with pe.Fori(1, SLOTS - 1) as j:
                up(j, expert_of(j))
                down(j - 1, expert_of(j - 1))
                turn(j + 1)
                turn_hidden(j)
            up(SLOTS - 1, expert_of(SLOTS - 1))
            down(SLOTS - 2, expert_of(SLOTS - 2))
            turn_hidden(SLOTS - 1)
            down(SLOTS - 1, expert_of(SLOTS - 1))
            pe.wait_ge(y_sb, SLOTS)



def mamba(nc, X, C, M):
    ZT = INNER // P
    with ExitStack() as ctx:
        def sb(n, shape, dt=F32):
            return ctx.enter_context(nc.sbuf_tensor("m_" + n, shape, dt))

        def sem(n):
            return C["sems"]("m_" + n)

        def ps(n, banks=1):
            return ctx.enter_context(nc.psum_tensor("m_ps_" + n, [P, banks, 512], F32))

        ps_r, ps_t, ps_b, ps_y, ps_o, ps_s, ps_z = ps("r", 2), ps("t"), ps("b"), ps("y"), ps("o"), ps("s"), ps("z")

        w_in = sb("w_in", [P, DT, IN_PROJ])
        w_out = sb("w_out", [P, ZT, D])
        norm_w = sb("norm_w", [P, ZT])
        conv_w = sb("conv_w", [P, CT, TAPS])
        conv_b = sb("conv_b", [P, CT])
        dt_bias = sb("dt_bias", [P, MHEADS])
        a_neg = sb("a_neg", [P, 2, MHEADS])
        skip = sb("skip", [P, MHEADS])
        ident_b = sb("ident_b", [P, P], BF16)
        neg_b = sb("neg_b", [P, P], BF16)
        ones = sb("ones", [P, P])
        stats = sb("stats", [P, T, 6])
        mean_var = sb("mean_var", [P, T, 2])
        var_eps = sb("var_eps", [P, T])
        rstd = sb("rstd", [P, T])
        xn = sb("xn", [P, 2, D])
        xn_t = sb("xn_t", [P, DT, SEQ])
        pre = sb("pre", [P, 2, SEQ + TAPS - 1])
        conv = sb("conv", [P, 2, SEQ])
        xbc = sb("xbc", [P, CT, SEQ])
        z_act = sb("z_act", [P, T, INNER])
        dtv = sb("dtv", [P, 6, T, MHEADS])
        dt = sb("dt", [P, T, MHEADS])
        dta = sb("dta", [P, T, MHEADS])
        acs = sb("acs", [P, 2, T, MHEADS])
        neg_acs = sb("neg_acs", [P, T, MHEADS])
        e_acs = sb("e_acs", [P, T, MHEADS])
        e_rest = sb("e_rest", [P, T, MHEADS])
        e_all = sb("e_all", [P, T, MHEADS])
        decay = sb("decay", [P, MHEADS, P])
        mix = sb("mix", [P, MHEADS, P])
        b_tok = sb("b_tok", [P, P])
        xdt = sb("xdt", [P, MHEADS, HDIM])
        xskip = sb("xskip", [P, MHEADS, HDIM])
        xds = sb("xds", [P, MHEADS, HDIM])
        state = sb("state", [P, MHEADS, HDIM])
        y = sb("y", [P, 2, MHEADS, HDIM])
        y_t = sb("y_t", [P, INNER])
        square = sb("square", [P, INNER])
        sum_sq = sb("sum_sq", [P, 1])
        mean_sq = sb("mean_sq", [P, 1])
        rms = sb("rms", [P, 1])

        loaded, fixed, step_done, act_fixed, stats_ready, rstd_ready = (
            sem(n) for n in ("loaded", "fixed", "step_done", "act_fixed", "stats_ready", "rstd_ready"))
        xn_ready, xn_added, xt_ps, xt_sb, conv_ps, pre_ready, conv_ready, xbc_ready = (
            sem(n) for n in ("xn_ready", "xn_added", "xt_ps", "xt_sb", "conv_ps", "pre_ready", "conv_ready", "xbc_ready"))
        z_ps, z_ready, dt_ps, dt_step, dt_exp, dta_ready, sums_ps, sums_ready, exps_ready = (
            sem(n) for n in ("z_ps", "z_ready", "dt_ps", "dt_step", "dt_exp", "dta_ready", "sums_ps", "sums_ready",
                             "exps_ready"))
        turned_ps, gram_ps, decay_ps, b_ready, decay_ready, mix_ready, xdt_ready, xds_ready = (
            sem(n) for n in ("turned_ps", "gram_ps", "decay_ps", "b_ready", "decay_ready", "mix_ready", "xdt_ready",
                             "xds_ready"))
        diag_ps, off_ps, state_ps, state_ready, y_sum, gate_step, y_ready, sq_ready, mean_ready, rms_ready = (
            sem(n) for n in ("diag_ps", "off_ps", "state_ps", "state_ready", "y_sum", "gate_step", "y_ready",
                             "sq_ready", "mean_ready", "rms_ready"))
        yt_ps, yt_sb, out_ps, x_added = (sem(n) for n in ("yt_ps", "yt_sb", "out_ps", "x_added"))

        block = ctx.enter_context(nc.Block())

        def spread(v):
            return v.rearrange("(a h) -> a h", a=1).to_broadcast([P, MHEADS])

        @block.sync
        def _(sp):
            sp.dma_start(w_in[:], M["w_in"].rearrange("(t p) e -> p t e", p=P)).then_inc(loaded, 16)
            sp.dma_start(w_out[:], M["w_out"].rearrange("(t p) d -> p t d", p=P)).then_inc(loaded, 16)
            with nc.allow_non_contiguous_dma(reason="a few hundred words of parameters"):
                sp.dma_start(norm_w[:], M["norm_w"].rearrange("(t p) -> p t", p=P)).then_inc(loaded, 16)
                sp.dma_start(conv_b[:], M["conv_b"].rearrange("(t p) -> p t", p=P)).then_inc(loaded, 16)
                sp.dma_start(conv_w[:], M["conv_w"].rearrange("(t p) k -> p t k", p=P)).then_inc(loaded, 16)
            sp.dma_start(dt_bias[:], spread(M["dt_bias"])).then_inc(loaded, 16)
            sp.dma_start(a_neg[:, 0], spread(M["A_log"])).then_inc(loaded, 16)
            sp.dma_start(skip[:], spread(M["D"])).then_inc(loaded, 16)
            sp.wait_ge(loaded, 16 * 8)

        def heads(v):
            return v.unsqueeze(2).to_broadcast([P, MHEADS, HDIM])

        def by_head(v):
            return v.rearrange("p (h f) -> p h f", h=MHEADS)

        def x_tile(b, t):
            return X[:, bass.ds(b * T + t, 1), :].rearrange("p a d -> p (a d)")

        ORDER = [4, 5, 0, 1, 2, 3]

        @block.vector
        def _(dve):
            dve.wait_ge(loaded, 16 * 8)
            step = Steps(dve, fixed)
            step(nc.vector.tensor_copy(ident_b[:], C["ident"]))
            step(nc.vector.tensor_copy(neg_b[:], C["neg"][:, 1]))
            step(nc.vector.memset(ones[:], 1.0))
            step(nc.vector.memset(pre[:], 0.0))
            for k in range(ZT):
                step(nc.vector.tensor_scalar(w_out[:, k], w_out[:, k], norm_w[:, k:k + 1], None, ALU.mult))
            dve.wait_ge(act_fixed, 1)
            step(nc.vector.tensor_scalar(a_neg[:, 1], a_neg[:, 1], -1.0, None, ALU.mult))
            dve.sem_inc(x_added, 1)
            dve.sem_inc(y_sum, 1)
            NSTEP = 2 * T + 1 + CT * (TAPS - 1) + 7 + 2 + T * 2
            with dve.Fori(0, BATCH) as b:
                step = Steps(dve, step_done, b * NSTEP)
                row_stats(nc, step, [x_tile(b, t) for t in range(T)], stats, mean_var, var_eps[:], stats_ready)
                dve.wait_ge(rstd_ready, b + 1)
                for t in range(T):
                    if t >= 2:
                        dve.wait_ge(xt_ps, b * T + t - 1)
                        dve.wait_ge(xn_added, b * T + t - 1)
                    nc.vector.tensor_scalar(xn[:, t % 2], x_tile(b, t), mean_var[:, t, 0:1], rstd[:, t:t + 1],
                                            ALU.subtract, ALU.mult).then_inc(xn_ready, 1)
                for n, c in enumerate(ORDER):
                    dve.wait_ge(pre_ready, b * 2 * CT + 2 * n + 2)
                    if n >= 2:
                        dve.wait_ge(xbc_ready, b * CT + n - 1)
                    x, a = pre[:, n % 2], conv[:, n % 2]
                    step(nc.vector.tensor_scalar(a, x[:, 3:3 + SEQ], conv_w[:, c, 3:4], conv_b[:, c:c + 1], ALU.mult,
                                                 ALU.add))
                    for k in (2, 1):
                        step(nc.vector.scalar_tensor_tensor(a, x[:, k:k + SEQ], conv_w[:, c, k:k + 1], a, ALU.mult,
                                                            ALU.add))
                    nc.vector.scalar_tensor_tensor(a, x[:, 0:SEQ], conv_w[:, c, 0:1], a, ALU.mult, ALU.add
                                                   ).then_inc(conv_ready, 1)
                v, e, u, r, q = (dtv[:, k] for k in range(5))

                def flat(w):
                    return w.rearrange("p t h -> p (t h)")

                dve.wait_ge(dt_ps, b + 1)
                step(nc.vector.tensor_tensor(v, ps_b[:, 0, 0:T * MHEADS].rearrange("p (t h) -> p t h", h=MHEADS),
                                             dt_bias[:].unsqueeze(1).to_broadcast([P, T, MHEADS]), ALU.add))
                nc.vector.scalar_tensor_tensor(flat(e), flat(v), -1.0, flat(v), ALU.mult, ALU.max).then_inc(dt_step, 1)
                dve.wait_ge(dt_exp, b * 2 + 1)
                nc.vector.tensor_scalar(u, e, 1.0, None, ALU.add).then_inc(dt_step, 1)
                dve.wait_ge(dt_step, b * 2 + 2)
                step(nc.vector.tensor_scalar(r, u, -1.0, None, ALU.add))
                step(nc.vector.tensor_tensor(r, e, r, ALU.subtract))
                step(nc.vector.reciprocal(q, u))
                step(nc.vector.tensor_tensor(r, r, q, ALU.mult))
                dve.wait_ge(dt_exp, b * 2 + 2)
                step(nc.vector.tensor_tensor(r, r, dtv[:, 5], ALU.add))
                step(nc.vector.scalar_tensor_tensor(flat(dt[:]), flat(v), 0.0, flat(r), ALU.max, ALU.add))
                nc.vector.tensor_tensor(dta[:], dt[:], a_neg[:, 1].unsqueeze(1).to_broadcast([P, T, MHEADS]), ALU.mult
                                        ).then_inc(dta_ready, 1)
                dve.wait_ge(sums_ps, b + 1)
                two = ps_t[:, 0, 0:2 * T * MHEADS].rearrange("p (a t h) -> p a t h", a=2, t=T)
                step(nc.vector.tensor_copy(acs[:, 0], two[:, 0]))
                step(nc.vector.tensor_scalar(neg_acs[:], acs[:, 0], -1.0, None, ALU.mult))
                nc.vector.tensor_tensor(acs[:, 1], two[:, 1], acs[:, 0], ALU.subtract).then_inc(sums_ready, 1)
                nc.vector.memset(state[:], 0.0).then_inc(state_ready, 1)

                def front(t):
                    N = b * T + t
                    dve.wait_ge(turned_ps, N + 1)
                    nc.vector.tensor_tensor(xdt[:], by_head(ps_t[:, 0]), heads(dt[:, t]), ALU.mult
                                            ).then_inc(xdt_ready, 1)
                    nc.vector.tensor_tensor(xskip[:], by_head(ps_t[:, 0]), heads(skip[:]), ALU.mult
                                            ).then_inc(xdt_ready, 1)
                    dve.wait_ge(gram_ps, N + 1)
                    dve.wait_ge(decay_ready, N + 1)
                    nc.vector.tensor_tensor(mix[:], decay[:],
                                            ps_b[:, 0, 0:P].unsqueeze(1).to_broadcast([P, MHEADS, P]), ALU.mult
                                            ).then_inc(mix_ready, 1)

                def middle(t):
                    N = b * T + t
                    dve.wait_ge(off_ps, N + 1)
                    step(nc.vector.tensor_tensor(state[:], state[:], heads(e_all[:, t]), ALU.mult))
                    dve.wait_ge(state_ps, N + 1)
                    nc.vector.tensor_tensor(state[:], state[:], by_head(ps_s[:, 0]), ALU.add).then_inc(state_ready, 1)
                    if t >= 2:
                        dve.wait_ge(y_ready, N - 1)
                    step(nc.vector.tensor_tensor(y[:, t % 2], by_head(ps_o[:, 0]), heads(e_acs[:, t]), ALU.mult))
                    dve.wait_ge(diag_ps, N + 1)
                    nc.vector.tensor_tensor(y[:, t % 2], y[:, t % 2], by_head(ps_y[:, 0]), ALU.add).then_inc(y_sum, 1)

                def mean(t):
                    N = b * T + t
                    dve.wait_ge(sq_ready, N + 1)
                    nc.vector.tensor_scalar(mean_sq[:], sum_sq[:], 1.0 / INNER, LN_EPS, ALU.mult, ALU.add
                                            ).then_inc(mean_ready, 1)

                def last(t):
                    N = b * T + t
                    dve.wait_ge(out_ps, N + 1)
                    dve.wait_ge(rms_ready, N + 1)
                    dve.wait_ge(xn_added, N + 1)
                    nc.vector.scalar_tensor_tensor(x_tile(b, t), ps_z[:, 0, 0:D], rms[:], x_tile(b, t), ALU.mult,
                                                   ALU.add).then_inc(x_added, 1)

                dve.wait_ge(exps_ready, b + 1)
                dve.wait_ge(state_ready, b * (T + 1) + 1)
                front(0)
                for t in range(T):
                    middle(t)
                    if t + 1 < T:
                        dve.wait_ge(state_ps, b * T + t + 1)
                        dve.wait_ge(gate_step, b * T + t + 1)
                        front(t + 1)
                    mean(t)
                    last(t)
                dve.wait_ge(x_added, b * T + T + 1)
                assert step.n == NSTEP, (step.n, NSTEP)

        @block.gpsimd
        def _(pool):
            with pool.Fori(0, BATCH) as b:
                pool.wait_ge(stats_ready, b + 1)
                inverse_root(nc, rstd[:], var_eps[:], C).then_inc(rstd_ready, 1)
                for t in range(T):
                    pool.wait_ge(xn_ready, b * T + t + 1)
                    nc.gpsimd.tensor_tensor(x_tile(b, t), x_tile(b, t), xn[:, t % 2], ALU.add).then_inc(xn_added, 1)

                def weigh(t):
                    pool.wait_ge(xdt_ready, 2 * (b * T + t) + 1)
                    if t >= 1:
                        pool.wait_ge(state_ps, b * T + t)
                    nc.gpsimd.tensor_tensor(xds[:], xdt[:], heads(e_rest[:, t]), ALU.mult).then_inc(xds_ready, 1)

                pool.wait_ge(exps_ready, b + 1)
                pool.wait_ge(z_ready, b * T + T)
                weigh(0)
                for t in range(T):
                    N = b * T + t
                    pool.wait_ge(y_sum, N + 2)
                    pool.wait_ge(xdt_ready, 2 * N + 2)
                    nc.gpsimd.tensor_tensor(y[:, t % 2], y[:, t % 2], xskip[:], ALU.add).then_inc(gate_step, 1)
                    pool.wait_ge(gate_step, N + 1)
                    nc.gpsimd.tensor_tensor(y[:, t % 2], y[:, t % 2], by_head(z_act[:, t]), ALU.mult).then_inc(y_ready, 1)
                    if t + 1 < T:
                        weigh(t + 1)
                    pool.wait_ge(mean_ready, N + 1)
                    if t >= 1:
                        pool.wait_ge(x_added, N + 1)
                    inverse_root(nc, rms[:], mean_sq[:], C).then_inc(rms_ready, 1)

        @block.scalar
        def _(act):
            act.wait_ge(loaded, 16 * 8)
            nc.scalar.activation(a_neg[:, 1], a_neg[:, 0], ACT.Exp).then_inc(act_fixed, 1)
            act.sem_inc(xt_sb, 1)
            act.wait_ge(fixed, 4)
            with act.Fori(0, BATCH) as b:
                for t in range(T):
                    act.wait_ge(xt_ps, b * T + t + 1)
                    nc.scalar.copy(xn_t[:, :, t * P:(t + 1) * P], ps_z[:, 0, 0:D].rearrange("p (d k) -> p d k", d=DT)
                                   ).then_inc(xt_sb, 1)
                for n, c in enumerate(ORDER):
                    for k, bank in enumerate((ps_y, ps_o)):
                        act.wait_ge(conv_ps, b * 2 * CT + 2 * n + k + 1)
                        if n >= 2 and k == 0:
                            act.wait_ge(conv_ready, b * CT + n - 1)
                        nc.scalar.copy(pre[:, n % 2, 3 + 512 * k:3 + 512 * (k + 1)], bank[:, 0]).then_inc(pre_ready, 1)
                    if n >= 1:
                        act.wait_ge(conv_ready, b * CT + n)
                        nc.scalar.activation(xbc[:, ORDER[n - 1]], conv[:, (n - 1) % 2], ACT.Silu).then_inc(xbc_ready, 1)
                act.wait_ge(conv_ready, b * CT + CT)
                nc.scalar.activation(xbc[:, ORDER[-1]], conv[:, (CT - 1) % 2], ACT.Silu).then_inc(xbc_ready, 1)
                for t in range(T):
                    act.wait_ge(z_ps, b * T + t + 1)
                    nc.scalar.activation(z_act[:, t], ps_r[:, t % 2], ACT.Silu).then_inc(z_ready, 1)
                act.wait_ge(dt_step, b * 2 + 1)
                nc.scalar.activation(dtv[:, 1], dtv[:, 1], ACT.Exp, scale=-1.0).then_inc(dt_exp, 1)
                act.wait_ge(dt_step, b * 2 + 2)
                nc.scalar.activation(dtv[:, 5], dtv[:, 2], ACT.Ln).then_inc(dt_exp, 1)
                act.wait_ge(sums_ready, b + 1)
                nc.scalar.activation(e_acs[:], acs[:, 0], ACT.Exp)
                nc.scalar.activation(e_rest[:], acs[:, 1], ACT.Exp)
                nc.scalar.activation(e_all[:].rearrange("p t h -> p (t h)"), ps_t[:, 0, T * MHEADS:2 * T * MHEADS],
                                     ACT.Exp).then_inc(exps_ready, 1)

                def front(t):
                    N = b * T + t
                    act.wait_ge(turned_ps, N + 1)
                    if t >= 1:
                        act.wait_ge(state_ps, N)
                    nc.scalar.copy(b_tok[:], ps_b[:, 0, P:2 * P]).then_inc(b_ready, 1)
                    act.wait_ge(decay_ps, N + 1)
                    if t >= 1:
                        act.wait_ge(mix_ready, N)
                    for h in range(MHEADS):
                        last = nc.scalar.activation(decay[:, h], ps_r[:, h // 4, (h % 4) * P:(h % 4 + 1) * P], ACT.Exp,
                                                    bias=neg_acs[:, t, h:h + 1])
                    last.then_inc(decay_ready, 1)

                front(0)
                for t in range(T):
                    N = b * T + t
                    if t + 1 < T:
                        front(t + 1)
                    act.wait_ge(y_ready, N + 1)
                    if t >= 1:
                        act.wait_ge(mean_ready, N)
                    nc.scalar.activation(square[:], y[:, t % 2].rearrange("p h f -> p (h f)"), ACT.Square,
                                         accum_out=sum_sq[:]).then_inc(sq_ready, 1)
                    act.wait_ge(yt_ps, N + 1)
                    if t >= 1:
                        act.wait_ge(out_ps, N)
                    nc.scalar.copy(y_t[:], ps_y[:, 0]).then_inc(yt_sb, 1)

        @block.tensor
        def _(pe):
            ident = C["ident"]
            pe.wait_ge(loaded, 16 * 8)
            pe.wait_ge(fixed, 4 + ZT + 1)
            with pe.Fori(0, BATCH) as b:
                pe.wait_ge(x_added, b * T + 1)
                for t in range(T):
                    pe.wait_ge(xn_ready, b * T + t + 1)
                    pe.wait_ge(xt_sb, b * T + t + 1)
                    for d in range(DT):
                        last = nc.tensor.transpose(ps_z[:, 0, d * P:(d + 1) * P], xn[:, t % 2, d * P:(d + 1) * P], ident)
                    last.then_inc(xt_ps, 1)
                pe.wait_ge(xt_sb, b * T + T + 1)
                for n, c in enumerate(ORDER):
                    for k, bank in enumerate((ps_y, ps_o)):
                        if n >= 1:
                            pe.wait_ge(pre_ready, b * 2 * CT + 2 * n + k - 1)
                        for d in range(DT):
                            last = nc.tensor.matmul(bank[:, 0], w_in[:, d, INNER + c * P:INNER + (c + 1) * P],
                                                    xn_t[:, d, 512 * k:512 * (k + 1)], start=(d == 0),
                                                    stop=(d == DT - 1))
                        last.then_inc(conv_ps, 1)
                for t in range(T):
                    if t >= 2:
                        pe.wait_ge(z_ready, b * T + t - 1)
                    for d in range(DT):
                        last = nc.tensor.matmul(ps_r[:, t % 2], xn_t[:, d, t * P:(t + 1) * P], w_in[:, d, 0:INNER],
                                                start=(d == 0), stop=(d == DT - 1))
                    last.then_inc(z_ps, 1)
                for t in range(T):
                    for d in range(DT):
                        last = nc.tensor.matmul(ps_b[:, 0, t * MHEADS:(t + 1) * MHEADS], xn_t[:, d, t * P:(t + 1) * P],
                                                w_in[:, d, INNER + CONV:], start=(d == 0), stop=(d == DT - 1))
                last.then_inc(dt_ps, 1)
                pe.wait_ge(dta_ready, b + 1)
                flat = dta[:].rearrange("p t h -> p (t h)")
                nc.tensor.matmul(ps_t[:, 0, 0:T * MHEADS], C["upto"], flat, start=True, stop=True)
                nc.tensor.matmul(ps_t[:, 0, T * MHEADS:2 * T * MHEADS], ones[:], flat, start=True, stop=True
                                 ).then_inc(sums_ps, 1)
                pe.wait_ge(exps_ready, b + 1)
                pe.wait_ge(z_ready, b * T + T)
                pe.wait_ge(xbc_ready, b * CT + CT)

                def front(t):
                    N, s = b * T + t, slice(t * P, (t + 1) * P)
                    if t >= 1:
                        pe.wait_ge(xdt_ready, 2 * N)
                        pe.wait_ge(b_ready, N)
                        pe.wait_ge(mix_ready, N)
                    for k in range(ZT):
                        nc.tensor.transpose(ps_t[:, 0, k * P:(k + 1) * P], xbc[:, k, s], ident)
                    nc.tensor.transpose(ps_b[:, 0, P:2 * P], xbc[:, 4, s], ident).then_inc(turned_ps, 1)
                    for h in range(MHEADS):
                        nc.tensor.matmul(ps_r[:, h // 4, (h % 4) * P:(h % 4 + 1) * P],
                                         dta[:, t, h:h + 1].to_broadcast([P, P]), C["upto"], start=(h % 4 == 0),
                                         stop=False, skip_group_check=True)
                    for k in range(2):
                        last = nc.tensor.matmul(ps_r[:, k].rearrange("p (h l) -> p h l", l=P), ident_b[:],
                                                neg_b[:].unsqueeze(1).to_broadcast([P, 4, P]), start=False, stop=True,
                                                skip_group_check=True)
                    last.then_inc(decay_ps, 1)
                    pe.wait_ge(b_ready, N + 1)
                    nc.tensor.matmul(ps_b[:, 0, 0:P], xbc[:, 4, s], xbc[:, 5, s], start=True, stop=True
                                     ).then_inc(gram_ps, 1)

                front(0)
                for t in range(T):
                    N, s = b * T + t, slice(t * P, (t + 1) * P)
                    pe.wait_ge(y_sum, N + 1)
                    pe.wait_ge(state_ready, b * (T + 1) + t + 1)
                    nc.tensor.matmul(ps_o[:, 0], xbc[:, 5, s], state[:].rearrange("p h f -> p (h f)"), start=True,
                                     stop=True).then_inc(off_ps, 1)
                    pe.wait_ge(mix_ready, N + 1)
                    if t >= 1:
                        pe.wait_ge(yt_sb, N)
                    for h in range(MHEADS):
                        last = nc.tensor.matmul(ps_y[:, 0, h * HDIM:(h + 1) * HDIM], mix[:, h], xdt[:, h],
                                                start=(h == 0), stop=True, skip_group_check=True)
                    last.then_inc(diag_ps, 1)
                    pe.wait_ge(xds_ready, N + 1)
                    nc.tensor.matmul(ps_s[:, 0], b_tok[:], xds[:].rearrange("p h f -> p (h f)"), start=True, stop=True
                                     ).then_inc(state_ps, 1)
                    if t + 1 < T:
                        front(t + 1)
                    pe.wait_ge(y_ready, N + 1)
                    flat_y = y[:, t % 2].rearrange("p h f -> p (h f)")
                    for k in range(ZT):
                        last = nc.tensor.transpose(ps_y[:, 0, k * P:(k + 1) * P], flat_y[:, k * P:(k + 1) * P], ident)
                    last.then_inc(yt_ps, 1)
                    pe.wait_ge(yt_sb, N + 1)
                    pe.wait_ge(x_added, N + 1)
                    for k in range(ZT):
                        last = nc.tensor.matmul(ps_z[:, 0, 0:D], y_t[:, k * P:(k + 1) * P], w_out[:, k], start=(k == 0),
                                                stop=(k == ZT - 1))
                    last.then_inc(out_ps, 1)



def constants():
    i = np.arange(P)
    inv = (10000.0 ** (-np.arange(0, DH, 2) / DH)).astype(np.float32)
    ang = (np.arange(SEQ, dtype=np.float32)[:, None] * inv[None, :]).astype(np.float32)
    cos, sin = np.cos(ang), np.sin(ang)
    rope = np.stack([np.repeat(cos, 2, 1), np.stack([-sin, sin], -1).reshape(SEQ, DH)], 1).astype(np.float32)
    neg = np.stack([np.where(i[None, :] > i[:, None], MASKED, 0.0), np.where(i[None, :] < i[:, None], MASKED, 0.0)], 1)
    table = np.zeros((P, CONSTS), np.float32)
    table[:, 0:P] = np.eye(P)
    table[:, P:3 * P] = neg.reshape(P, 2 * P)
    table[:, 3 * P:4 * P] = (i[:, None] < i[None, :])
    table[:, 4 * P:5 * P] = (i[:, None] <= i[None, :])
    table[:, 5 * P] = i // RANK
    table[:, 5 * P + 1:5 * P + 1 + SLOTS] = np.arange(SLOTS)
    table[:, 5 * P + 1 + SLOTS:5 * P + 1 + SLOTS + NT] = P * np.arange(NT)
    table[:, CONSTS - 1] = -0.5
    return {"const_table": table, "const_rope": rope}


CONSTS = 5 * P + 1 + SLOTS + NT + 1


def program(nc, I, out, phases):
    with ExitStack() as ctx:
        X = ctx.enter_context(nc.sbuf_tensor("x_res", [P, NT, D], F32))
        table = ctx.enter_context(nc.sbuf_tensor("table", [P, CONSTS], F32))
        C = {
            "ident": table[:, 0:P],
            "neg": table[:, P:3 * P].rearrange("p (a k) -> p a k", a=2),
            "before": table[:, 3 * P:4 * P],
            "upto": table[:, 4 * P:5 * P],
            "minus_half": table[:, CONSTS - 1:CONSTS],
            "adapter": table[:, 5 * P:5 * P + 1],
            "slot_no": table[:, 5 * P + 1:5 * P + 1 + SLOTS],
            "tile_tokens": table[:, 5 * P + 1 + SLOTS:CONSTS - 1],
        }
        C["sems"] = Semaphores(nc, ctx)
        C["begun"] = begun = ctx.enter_context(nc.semaphore("begun"))
        with nc.Block() as block:
            @block.sync
            def _(sp):
                sp.dma_start(table[:], I["const_table"]).then_inc(begun, 16)
                x = I["L0_attn_a_x"].rearrange("b (t p) d -> p (b t) d", p=P)
                for b in range(BATCH):
                    sp.dma_start(X[:, b * T:(b + 1) * T], x[:, b * T:(b + 1) * T]).then_inc(begun, 16)
        for phase in phases:
            phase(nc, X, C, I)
        stored = ctx.enter_context(nc.semaphore("stored"))
        with nc.Block() as block:
            @block.sync
            def _(sp):
                y = out.rearrange("b (t p) d -> p (b t) d", p=P)
                for b in range(BATCH):
                    sp.dma_start(y[:, b * T:(b + 1) * T], X[:, b * T:(b + 1) * T]).then_inc(stored, 16)
                sp.wait_ge(stored, 16 * BATCH)


def phase_attention(nc, X, C, I):
    A = {k: I["L0_attn_a_" + k] for k in ("Wq", "Wk", "Wv", "Wo", "Aq", "Ak", "Av", "Ao", "Bq", "Bk", "Bv", "Bo")}
    A["starts"], A["rope"] = I["L0_attn_a_lora_start_indices"], I["const_rope"]
    attention(nc, X, C, A)


def phase_ffn(which):
    def phase(nc, X, C, I):
        C["sems"].clear("f_")
        F = {k: I["L0_ffn_" + k] for k in ("Wr", "br", "Wg", "Wu", "Wd")}
        F["x_slots"] = nc.dram_tensor(which + "x_slots", (SLOTS * P, D), F32, kind="Internal").ap()
        F["y_slots"] = nc.dram_tensor(which + "y_slots", (SLOTS * P, D), F32, kind="Internal").ap()
        routed_ffn(nc, X, C, F, which)
    return phase


def phase_mamba(nc, X, C, I):
    mamba(nc, X, C, {k: I["L0_attn_b_" + k]
                     for k in ("w_in", "conv_w", "conv_b", "dt_bias", "A_log", "D", "norm_w", "w_out")})


PHASES = [phase_attention, phase_ffn("g1_"), phase_mamba, phase_ffn("g2_")]


def kernel(**inputs):
    import concourse.bacc as bacc
    from concourse.bass_utils import run_bass_kernel_spmd

    nc = bacc.Bacc("TRN2", target_bir_lowering=False, num_devices=1)
    arrays = {k: np.ascontiguousarray(v) for k, v in {**inputs, **constants()}.items()}
    I = {k: nc.dram_tensor(k, a.shape, mybir.dt.from_np(a.dtype), kind="ExternalInput").ap()
         for k, a in arrays.items()}
    out = nc.dram_tensor("out", (BATCH, SEQ, D), F32, kind="ExternalOutput").ap()
    program(nc, I, out, PHASES)
    return run_bass_kernel_spmd(nc, [arrays], core_ids=[0]).results[0]["out"]
```

```python
from contextlib import ExitStack

import numpy as np

import concourse.bass as bass
from concourse import mybir

F32 = mybir.dt.float32
F32R = mybir.dt.float32r
BF16 = mybir.dt.bfloat16
I32 = mybir.dt.int32
U32 = mybir.dt.uint32
ALU = mybir.AluOpType
ACT = mybir.ActivationFunctionType
AX = mybir.AxisListType.X

P = 128
BATCH, SEQ, D = 4, 1024, 256
DT = D // P
T = SEQ // P
NT = BATCH * T
HEADS, DH = 16, 16
GROUP = 4
GROUPS = HEADS // GROUP
ADAPTERS, RANK = 4, 16
EXPERTS, FF = 4, 1024
SLOTS = NT + EXPERTS - 1
LN_EPS = 1e-5
MASKED = -1e30
STATE, INNER, CONV, TAPS, MHEADS, HDIM = 128, 512, 768, 4, 8, 64
CT = CONV // P
IN_PROJ = 2 * INNER + 2 * STATE + MHEADS


class Semaphores:

    def __init__(self, nc, ctx):
        self.nc, self.ctx, self.held = nc, ctx, {}

    def __call__(self, name):
        if name not in self.held:
            self.held[name] = self.ctx.enter_context(self.nc.semaphore(name))
        return self.held[name]

    def clear(self, prefix):
        with self.nc.Block() as block:
            @block.sync
            def _(sp):
                for name, held in self.held.items():
                    if name.startswith(prefix):
                        sp.sem_clear(held)


class Steps:

    def __init__(self, eng, sem, base=0):
        self.eng, self.sem, self.base, self.n = eng, sem, base, 0

    def __call__(self, ins, wait=True):
        ins.then_inc(self.sem, 1)
        self.n += 1
        if wait:
            self.eng.wait_ge(self.sem, self.base + self.n)


def row_stats(nc, step, tiles, stats, mean_var, var_eps, done):
    for t, x in enumerate(tiles):
        step(nc.vector.bn_stats(stats[:, t], x), wait=t + 1 == len(tiles))
    step(nc.vector.memset(var_eps, 0.0), wait=False)
    for t in range(NT):
        step(nc.vector.bn_aggr(mean_var[:, t], stats[:, t]), wait=t + 1 == NT)
    nc.vector.tensor_scalar(var_eps, mean_var[:, :, 1], LN_EPS, None, ALU.add).then_inc(done, 1)


def inverse_root(nc, out, x, C):
    return nc.gpsimd.tensor_tensor(out, x, C["minus_half"].to_broadcast(list(out.shape)), ALU.pow)


def attention(nc, X, C, A):
    STACK = 64
    PAIRS = HEADS // 2
    RING = 8
    UNITS = T * GROUP
    HALF = T // 2
    rising = [(i, u, c) for i in range(T) for u in range(GROUP) for c in range(1 + i // HALF)]
    falling = [(i, u, c) for i in reversed(range(T)) for u in range(GROUP) for c in range(1 + i // HALF)]
    CHUNKS = len(rising)
    WARM_UP = 12
    def pieces(j):
        if j == 0:
            return [], [(0, HALF)], [(HALF, T)], []
        cuts = [j + (T - j) * k // 3 for k in range(4)] if j < T - 1 else [j, T, T, T]
        parts = [[]]
        for a, b in zip(cuts, cuts[1:]):
            halves = [(a, min(b, HALF)), (max(a, HALF), b)]
            parts.append([h for h in halves if h[0] < h[1]])
        return parts

    FIRST, LAST, SLACK = 1, 7 * GROUP - 1, 100
    issued, pe_at, act_at, chunk_end = [0] * (FIRST + 1), 0., [0., 0.], [0., 0.]
    for n in range(FIRST, UNITS):
        j, u, wide = n // GROUP, n % GROUP, P * (T - n // GROUP)
        weighed = sum(b - a for a, b in pieces((j - 1) % T)[u])
        pe_at = max(pe_at, act_at[-2]) + wide * 0.42 + 110
        act_at.append(max(act_at[-1], pe_at + 80) + wide * 0.84 + 50)
        pe_at += weighed * P * 1.67 + 60
        if n == 3:
            pe_at += 900
            chunk_end[-1] += 900
            act_at[-1] += 900
        k = issued[-1]
        while k < CHUNKS and (n >= LAST or chunk_end[-2] - pe_at < SLACK):
            w = min(512, (falling[k][0] + 1) * P - 512 * falling[k][2])
            pe_at = max(pe_at, chunk_end[-2]) + w * 0.42 + 60
            chunk_end.append(max(chunk_end[-1], pe_at + 60) + w * 1.04 + 66)
            k += 1
        issued.append(k)
    with ExitStack() as ctx:
        def sb(name, shape, dt=F32):
            return ctx.enter_context(nc.sbuf_tensor("a_" + name, shape, dt))

        def sem(name):
            return C["sems"]("a_" + name)

        ps_e = ctx.enter_context(nc.psum_tensor("a_ps_e", [P, 2, 2, 512], F32))
        ps_m = ctx.enter_context(nc.psum_tensor("a_ps_m", [P, 2, 512], F32))
        ps_a = ctx.enter_context(nc.psum_tensor("a_ps_a", [P, 2, 512], F32))

        probs = sb("probs", [P, RING, SEQ])
        spare = probs[:].rearrange("p r q -> p (r q)")
        w_nat = spare[:, 0:2048].rearrange("p (m t d) -> p m t d", m=4, t=2)
        b_nat = spare[:, 2048:2560].rearrange("p (m t e r) -> p m t e r", m=4, t=2, e=ADAPTERS)
        k_tok = spare[:, 3072:5120].bitcast(F32R).rearrange("p (a h c) -> p a h c", a=2, h=HEADS)
        rot = spare[:, 5120:6144].rearrange("p (a b d) -> p a b d", a=2, b=2)
        rope_a, rope_b = spare[:, 6144:6656], spare[:, 6656:7168]
        xn = spare[:, 7168:7680].rearrange("p (a d) -> p a d", a=2)
        xn_t = spare[:, 7680:8192].rearrange("p (a d) -> p a d", a=2)
        acc = probs[:, RING - 1, :]
        a_cat = sb("a_cat", [64, 4, D])
        w_t = sb("w_t", [P, 4, DT, D])
        b_t = sb("b_t", [64, 4, D])
        w_eff = sb("w_eff", [P, DT, 4, D])
        starts_i = sb("starts_i", [64, ADAPTERS], I32)
        starts = sb("starts", [64, ADAPTERS])
        picked = sb("picked", [64, 4, BATCH + 1])
        ident_b = sb("ident_b", [P, P], BF16)
        mask_b = sb("mask_b", [P, 2, P], BF16)
        rope = sb("rope", [P, T, 2, DH])
        mean_var = sb("mean_var", [P, NT, 2])
        var_eps = sb("var_eps", [P, NT])
        rstd = sb("rstd", [P, NT])
        q_tok = sb("q_tok", [P, T, HEADS, STACK], F32R)
        q_st = sb("q_st", [P, PAIRS, SEQ], F32R)
        k_st = sb("k_st", [P, PAIRS, SEQ], F32R)
        vals = sb("vals", [P, T, (HEADS + 1) * 17])
        peak = sb("peak", [P, GROUP, T, 2])
        recip = sb("recip", [P, T * GROUP])
        heads_out = sb("heads_out", [P, T, D])
        ho_t = spare[:, 0:512].rearrange("p (a d) -> p a d", a=2)
        stats = heads_out[:, 0, 0:NT * 6].rearrange("p (t s) -> p t s", s=6)
        a_sel = spare[0:64, 2048:3072].rearrange("p (m d) -> p m d", m=4)

        loaded, fixed = sem("loaded"), sem("fixed")
        dve_step, wt_ps, wt_sb, sel_ready, wl_ps, wl_used = (
            sem(n) for n in ("dve_step", "wt_ps", "wt_sb", "sel_ready", "wl_ps", "wl_used"))
        xn_ready, xt_ps, xt_sb, qk_ps, rot_ready, v_copied = (
            sem(n) for n in ("xn_ready", "xt_ps", "xt_sb", "qk_ps", "rot_ready", "v_copied"))
        hi_ready, lo_ready, stack_ps, stack_sb, v_ps, again_dve = (
            sem(n) for n in ("hi_ready", "lo_ready", "stack_ps", "stack_sb", "v_ps", "again_dve"))
        score_ps, chunk_max, max_ready, again_ps, again_act = (
            sem(n) for n in ("score_ps", "chunk_max", "max_ready", "again_ps", "again_act"))
        shifted_ps, exp_done, pv_done, acc_sb, acc_t, normed = (
            sem(n) for n in ("shifted_ps", "exp_done", "pv_done", "acc_sb", "acc_t", "normed"))
        stats_ready, rstd_ready, stats_step = sem("stats_ready"), sem("rstd_ready"), sem("stats_step")
        ot_ps, ot_sb, proj_ps, x_added, half_turned = (
            sem(n) for n in ("ot_ps", "ot_sb", "proj_ps", "x_added", "half_turned"))

        LOADS = 4 * 3 + 2

        def qk_bank(t):
            return ps_e[:, t % 2, t % 2, :]

        block = ctx.enter_context(nc.Block())

        @block.sync
        def _(sp):
            for m, name in enumerate("qkvo"):
                sp.dma_start(w_nat[:, m], A["W" + name].rearrange("(t p) d -> p t d", p=P)).then_inc(loaded, 16)
                for t in range(2):
                    sp.dma_start(b_nat[:, m, t], A["B" + name][:, t * P:(t + 1) * P, :].rearrange("e p r -> p e r")
                                 ).then_inc(loaded, 16)
                sp.dma_start(a_cat[:, m], A["A" + name].rearrange("e r d -> (e r) d")).then_inc(loaded, 16)
            sp.dma_start(starts_i[:], A["starts"].rearrange("(a n) -> a n", a=1).to_broadcast([64, ADAPTERS])
                         ).then_inc(loaded, 16)
            sp.dma_start(rope[:], A["rope"].rearrange("(t p) a f -> p t a f", p=P)).then_inc(loaded, 16)
            C["load_x"](sp)
            sp.wait_ge(loaded, 16 * (LOADS + 4))

        @block.vector
        def _(dve):
            step = Steps(dve, fixed)
            step(nc.vector.tensor_copy(ident_b[:], C["ident"]))
            step(nc.vector.tensor_copy(mask_b[:], C["neg"]))
            step(nc.vector.memset(q_tok[:].bitcast(F32), 0.0))
            step(nc.vector.memset(vals[:], 1.0))
            dve.wait_ge(loaded, 16 * (LOADS + 4))
            step(nc.vector.tensor_copy(starts[:], starts_i[:]))
            step(nc.vector.memset(picked[:], 0.0))
            for b in range(BATCH):
                step(nc.vector.tensor_scalar(picked[:, 0, 0:ADAPTERS], starts[:], float(b), None, ALU.is_le))
                step(nc.vector.tensor_reduce(picked[:, 1, 0:1], picked[:, 0, 0:ADAPTERS], AX, ALU.add))
                step(nc.vector.tensor_scalar(picked[:, 2, 0:1], picked[:, 1, 0:1], -1.0, 0.0, ALU.add, ALU.max))
                step(nc.vector.tensor_scalar(picked[:, 3, b:b + 1], picked[:, 2, 0:1], C["adapter"][0:64, :], None,
                                             ALU.is_equal))
            for m in range(4):
                dve.wait_ge(wt_ps, m + 1)
                nc.vector.tensor_copy(w_t[:, m], ps_e[:, m // 2, m % 2, :]).then_inc(wt_sb, 1)
            for m in range(4):
                dve.wait_ge(wt_ps, 5 + m)
                nc.vector.tensor_copy(b_t[:, m], ps_e[0:64, m // 2, m % 2, 0:D]).then_inc(wt_sb, 1)
            dve.wait_ge(wt_sb, 8)
            dve.sem_inc(chunk_max, 2)
            dve.sem_inc(x_added, 1)
            dve.wait_ge(C["begun"], 16 * (BATCH + 1))
            row_stats(nc, Steps(dve, stats_step), [X[:, t] for t in range(NT)], stats, mean_var, var_eps[:],
                      stats_ready)
            dve.wait_ge(rstd_ready, 1)

            def choose(b):
                for m in range(4):
                    nc.vector.tensor_scalar(a_sel[:, m], a_cat[:, m], picked[:, 3, bass.ds(b, 1)], None,
                                            ALU.mult).then_inc(sel_ready, 1)

            def merge(b, m):
                dve.wait_ge(wl_ps, b * 4 + m + 1)
                nc.vector.tensor_tensor(w_eff[:, :, m, :], w_t[:, m], ps_m[:, m % 2].rearrange("p (t o) -> p t o", t=DT),
                                        ALU.add).then_inc(wl_used, 1)

            def clear(step):
                step(nc.vector.memset(q_tok[:, :, :, 32:34].bitcast(F32), 0.0), wait=False)
                step(nc.vector.memset(k_tok[:, :, :, 34:48].bitcast(F32), 0.0), wait=False)
                step(nc.vector.memset(k_tok[:, :, :, 32:34].bitcast(F32), 1.0), wait=False)

            choose(0)
            clear(step)
            for m in range(4):
                merge(0, m)
            NSTEP = 3 + 2 * T + GROUPS * 3
            with dve.Fori(0, BATCH) as b:
                step = Steps(dve, dve_step, b * NSTEP)

                def norm(t):
                    if t >= 2:
                        dve.wait_ge(xt_ps, b * T + t - 1)
                    nc.vector.tensor_scalar(xn[:, t % 2], X[:, bass.ds(b * T + t, 1), :].rearrange("p a d -> p (a d)"),
                                            mean_var[:, bass.ds(b * T + t, 1), 0], rstd[:, bass.ds(b * T + t, 1)],
                                            ALU.subtract, ALU.mult
                                            ).then_inc(xn_ready, 1)

                def rotate(t):
                    dve.wait_ge(qk_ps, b * T + t + 1)
                    if t >= 1:
                        dve.wait_ge(rot_ready, b * T + t)
                    qk = qk_bank(t)
                    cos = rope[:, t, 0:1, :].to_broadcast([P, 2 * HEADS, DH])
                    sin = rope[:, t, 1, :].rearrange("p (i two) -> p two i", two=2)
                    step(nc.vector.tensor_tensor(rope_a.rearrange("p (h d) -> p h d", d=DH),
                                                 qk.rearrange("p (h d) -> p h d", d=DH), cos, ALU.mult))
                    pair = qk.rearrange("p (h i two) -> p two h i", two=2, i=DH // 2)
                    out = rope_b.rearrange("p (h i two) -> p two h i", two=2, i=DH // 2)
                    for odd in range(2):
                        last = nc.vector.tensor_tensor(
                            out[:, odd], pair[:, 1 - odd],
                            sin[:, odd:odd + 1, :].to_broadcast([P, 2 * HEADS, DH // 2]), ALU.mult)
                        if odd == 0:
                            last.then_inc(half_turned, 1)
                    step(last)
                    dve.wait_ge(half_turned, b * T + t + 1)
                    if t >= 2:
                        dve.wait_ge(lo_ready, b * T + t - 1)
                    nc.vector.tensor_tensor(rot[:, t % 2].rearrange("p a d -> p (a d)"), rope_a, rope_b,
                                            ALU.add).then_inc(rot_ready, 1)

                def maxima(g, chunks, first):
                    for n, (i, u, c) in enumerate(chunks, first):
                        dve.wait_ge(score_ps, (b * GROUPS + g) * CHUNKS + n + 1)
                        w = min(512, (i + 1) * P - 512 * c)
                        nc.vector.tensor_reduce(peak[:, u, i, c:c + 1], ps_m[:, n % 2, 0:w], AX, ALU.max
                                                ).then_inc(chunk_max, 1)

                norm(0)
                norm(1)
                for s in range(T + 3):
                    if s + 2 < T:
                        norm(s + 2)
                    if 1 <= s <= T:
                        rotate(s - 1)
                    if s >= 3:
                        maxima(0, [x for x in rising if x[0] == s - 3],
                               sum(x[0] < s - 3 for x in rising))

                def fold(g):
                    dve.wait_ge(chunk_max, (b * GROUPS + g + 1) * CHUNKS + 2)
                    h = T // 2
                    step(nc.vector.tensor_tensor(peak[:, :, h:, 0], peak[:, :, h:, 0], peak[:, :, h:, 1], ALU.max))
                    to = q_tok[:, :, g * GROUP:(g + 1) * GROUP, :].rearrange("p t u c -> p u t c")
                    step(nc.vector.tensor_scalar(to[:, :, :, 32], peak[:, :, :, 0], -1.0, None, ALU.mult))
                    nc.vector.scalar_tensor_tensor(to[:, :, :, 33], peak[:, :, :, 0], -1.0,
                                                   to[:, :, :, 32].bitcast(F32), ALU.mult, ALU.subtract
                                                   ).then_inc(max_ready, 1)

                def collect(g):
                    dve.wait_ge(acc_t, b * GROUPS + g + 1)
                    at = ps_a[:].rearrange("p b (c u f) -> p (b c u) f", u=GROUP, f=32)
                    step(nc.vector.reciprocal(recip[:], at[:, :, 16]))
                    nc.vector.tensor_tensor(
                        heads_out[:, :, g * GROUP * DH:(g + 1) * GROUP * DH].rearrange("p t (u f) -> p t u f", f=DH),
                        at[:, :, 0:DH].rearrange("p (t u) f -> p t u f", u=GROUP),
                        recip[:].rearrange("p (t u) -> p t u", u=GROUP).unsqueeze(3).to_broadcast([P, T, GROUP, DH]),
                        ALU.mult).then_inc(normed, 1)

                def again(g):
                    for n in (0, 2):
                        dve.wait_ge(again_ps, (b * GROUPS + g) * 4 + n + 1)
                        nc.vector.tensor_copy(q_st[:, 2 * g + n // 2, 0:512], ps_m[:, 0, :]).then_inc(again_dve, 1)

                fold(0)
                again(0)
                for g in range(GROUPS):
                    if g + 1 < GROUPS:
                        maxima(g + 1, falling[:issued[GROUP]], 0)
                    if g >= 1:
                        collect(g - 1)
                    if g + 1 < GROUPS:
                        maxima(g + 1, falling[issued[GROUP]:], issued[GROUP])
                        fold(g + 1)
                        again(g + 1)
                dve.wait_ge(pv_done, b * GROUPS * T + GROUPS * T)
                choose(b + 1)
                clear(step)
                collect(GROUPS - 1)
                merge(b + 1, 0)
                merge(b + 1, 1)
                for t in range(T):
                    if t == 2:
                        merge(b + 1, 2)
                    dve.wait_ge(proj_ps, b * T + t + 1)
                    x = X[:, bass.ds(b * T + t, 1), :].rearrange("p a d -> p (a d)")
                    nc.vector.tensor_tensor(x, x, ps_e[:, t % 2, 0, 0:D], ALU.add).then_inc(x_added, 1)
                merge(b + 1, 3)
                dve.wait_ge(x_added, b * T + T + 1)
                assert step.n == NSTEP, step.n

        @block.gpsimd
        def _(pool):
            pool.wait_ge(stats_ready, 1)
            inverse_root(nc, rstd[:], var_eps[:], C).then_inc(rstd_ready, 1)
            with pool.Fori(0, BATCH) as b:
                for t in range(T):
                    r = rot[:, t % 2].rearrange("p a (h d) -> p a h d", d=DH)
                    pool.wait_ge(hi_ready, b * T + t + 1)
                    q, k = q_tok[:, t], k_tok[:, t % 2]
                    nc.gpsimd.tensor_tensor(q[:, :, 48:64], r[:, 0], q[:, :, 0:16].bitcast(F32), ALU.subtract)
                    nc.gpsimd.tensor_tensor(k[:, :, 16:32], r[:, 1], k[:, :, 0:16].bitcast(F32), ALU.subtract
                                            ).then_inc(lo_ready, 1)

        @block.scalar
        def _(act):
            act.sem_inc(exp_done, 2)
            act.wait_ge(fixed, 4)
            with act.Fori(0, BATCH) as b:
                def turned(t):
                    act.wait_ge(xt_ps, b * T + t + 1)
                    if t >= 2:
                        act.wait_ge(qk_ps, b * T + t - 1)
                    nc.scalar.copy(xn_t[:, t % 2], ps_e[:, 1, 0, 0:D]).then_inc(xt_sb, 1)

                def high(t):
                    act.wait_ge(rot_ready, b * T + t + 1)
                    r = rot[:, t % 2].rearrange("p a (h d) -> p a h d", d=DH)
                    q = q_tok[:, t].rearrange("p h (s d) -> p h s d", d=DH)
                    k = k_tok[:, t % 2].rearrange("p h (s d) -> p h s d", d=DH)
                    twice = [P, HEADS, 2, DH]
                    nc.scalar.copy(q[:, :, 0:2], r[:, 0].unsqueeze(2).to_broadcast(twice))
                    if t >= 2:
                        act.wait_ge(stack_ps, (b * T + t - 2) * 4 + 2)
                    nc.scalar.copy(k[:, :, 0:4:3], r[:, 1].unsqueeze(2).to_broadcast(twice)).then_inc(hi_ready, 1)

                def values(t):
                    act.wait_ge(v_ps, b * T + t + 1)
                    nc.scalar.copy(vals[:, t].rearrange("p (h c) -> p h c", c=17)[:, 0:HEADS, 0:DH],
                                   ps_e[:, 0, 1, 0:D].rearrange("p (h d) -> p h d", d=DH)).then_inc(v_copied, 1)

                def stack(t, n):
                    act.wait_ge(stack_ps, (b * T + t) * 4 + n + 1)
                    to = (k_st, q_st)[n // 2][:, 4 * (n % 2):4 * (n % 2) + 4, t * P:(t + 1) * P]
                    nc.scalar.copy(to, ps_a[:, n % 2].rearrange("p (c k) -> p c k", k=P)).then_inc(stack_sb, 1)

                turned(0)
                for s in range(T + 2):
                    if s + 1 < T:
                        turned(s + 1)
                    if s >= 2:
                        stack(s - 2, 0)
                        stack(s - 2, 1)
                    if 1 <= s <= T:
                        high(s - 1)
                    if s < T:
                        values(s)
                    if s >= 2:
                        stack(s - 2, 2)
                        stack(s - 2, 3)

                def again(g, n):
                    act.wait_ge(again_ps, (b * GROUPS + g) * 4 + n + 1)
                    nc.scalar.copy(q_st[:, 2 * g + n // 2, 512:1024], ps_m[:, 1, :]).then_inc(again_act, 1)

                def sums(g):
                    act.wait_ge(pv_done, (b * GROUPS + g) * T + T)
                    nc.scalar.copy(acc, ps_a[:].rearrange("p b q -> p (b q)")).then_inc(acc_sb, 1)

                again(0, 1)
                again(0, 3)
                for S in range(GROUPS * T):
                    g, j = S // T, S % T
                    for u in range(GROUP):
                        n = S * GROUP + u
                        act.wait_ge(shifted_ps, b * GROUPS * UNITS + n + 1)
                        if S >= 2 and u == 0:
                            act.wait_ge(pv_done, b * GROUPS * T + S - 1)
                        if g >= 1 and n % UNITS == RING - 1:
                            act.wait_ge(acc_t, b * GROUPS + g)
                        nc.scalar.activation(probs[:, n % RING, j * P:],
                                             ps_e[:, n % 2].rearrange("p b q -> p (b q)")[:, j * P:],
                                             ACT.Exp, scale=DH ** -0.5).then_inc(exp_done, 1)
                        if j == 0 and u == 1 and g >= 1:
                            sums(g - 1)
                        if j == T - 1 and u % 2 == 1 and g + 1 < GROUPS:
                            again(g + 1, u)
                sums(GROUPS - 1)
                for t in range(T):
                    act.wait_ge(ot_ps, b * T + t + 1)
                    if t >= 2:
                        act.wait_ge(proj_ps, b * T + t - 1)
                    nc.scalar.copy(ho_t[:, t % 2], ps_a[:, t % 2, 0:D]).then_inc(ot_sb, 1)

        @block.tensor
        def _(pe):
            ident = C["ident"]
            pe.wait_ge(loaded, 16 * (LOADS + 4))
            for m in range(4):
                for d in range(DT):
                    for o in range(2):
                        last = nc.tensor.transpose(ps_e[:, m // 2, m % 2, d * D + o * P:d * D + o * P + P],
                                                   w_nat[:, m, o, d * P:(d + 1) * P], ident)
                last.then_inc(wt_ps, 1)
            for m in range(4):
                pe.wait_ge(wt_sb, m + 1)
                for o in range(2):
                    last = nc.tensor.transpose(ps_e[0:64, m // 2, m % 2, o * P:(o + 1) * P],
                                               b_nat[:, m, o].rearrange("p e r -> p (e r)"), ident)
                last.then_inc(wt_ps, 1)
            pe.wait_ge(fixed, 4)
            pe.wait_ge(wt_sb, 8)

            def low_rank(b, m):
                pe.wait_ge(sel_ready, b * 4 + m + 1)
                if m >= 2:
                    pe.wait_ge(wl_used, b * 4 + m - 1)
                for d in range(DT):
                    last = nc.tensor.matmul(ps_m[:, m % 2, d * D:(d + 1) * D], a_sel[:, m, d * P:(d + 1) * P],
                                            b_t[:, m], start=(d == 0), stop=(d == DT - 1), skip_group_check=True)
                last.then_inc(wl_ps, 1)

            for m in range(4):
                low_rank(0, m)
            with pe.Fori(0, BATCH) as b:
                pe.wait_ge(x_added, b * T + 1)
                pe.wait_ge(wl_used, b * 4 + 4)

                def turn(t):
                    pe.wait_ge(xn_ready, b * T + t + 1)
                    if t >= 1:
                        pe.wait_ge(xt_sb, b * T + t)
                    for d in range(DT):
                        last = nc.tensor.transpose(ps_e[:, 1, 0, d * P:(d + 1) * P],
                                                   xn[:, t % 2, d * P:(d + 1) * P], ident)
                    last.then_inc(xt_ps, 1)

                def stack(t, n):
                    if n == 0:
                        pe.wait_ge(lo_ready, b * T + t + 1)
                    if t >= 1 or n >= 2:
                        pe.wait_ge(stack_sb, (b * T + t) * 4 + n - 1)
                    tok = (k_tok[:, t % 2], q_tok[:, t])[n // 2]
                    for c in range(4):
                        h = 8 * (n % 2) + 2 * c
                        last = nc.tensor.transpose(ps_a[:, n % 2, c * P:(c + 1) * P],
                                                   tok[:, h:h + 2, :].bitcast(F32).rearrange("p h c -> p (h c)"), ident)
                    last.then_inc(stack_ps, 1)

                def project_v(t):
                    pe.wait_ge(xt_sb, b * T + t + 1)
                    if t >= 1:
                        pe.wait_ge(v_copied, b * T + t)
                    for d in range(DT):
                        last = nc.tensor.matmul(ps_e[:, 0, 1, 0:D], xn_t[:, t % 2, d * P:(d + 1) * P], w_eff[:, d, 2],
                                                start=(d == 0), stop=(d == DT - 1))
                    last.then_inc(v_ps, 1)

                def project_qk(t):
                    if t >= 2:
                        pe.wait_ge(rot_ready, b * T + t - 1)
                    for d in range(DT):
                        last = nc.tensor.matmul(qk_bank(t), xn_t[:, t % 2, d * P:(d + 1) * P],
                                                w_eff[:, d, 0:2].rearrange("p m o -> p (m o)"), start=(d == 0),
                                                stop=(d == DT - 1))
                    last.then_inc(qk_ps, 1)

                def scores(g, chunks, first):
                    for n, (i, u, c) in enumerate(chunks, first):
                        h = g * GROUP + u
                        rows = slice(64 * (h % 2), 64 * (h % 2) + 64)
                        w = min(512, (i + 1) * P - 512 * c)
                        diag = c == i // HALF
                        pe.wait_ge(chunk_max, (b * GROUPS + g) * CHUNKS + n + 1)
                        last = nc.tensor.matmul(ps_m[:, n % 2, 0:w], q_st[rows, h // 2, i * P:(i + 1) * P],
                                                k_st[rows, h // 2, 512 * c:512 * c + w], start=True,
                                                stop=not diag)
                        if diag:
                            last = nc.tensor.matmul(ps_m[:, n % 2, w - P:w], ident_b[:], mask_b[:, 0], start=False,
                                                    stop=True)
                        last.then_inc(score_ps, 1)

                turn(0)
                for s in range(T + 3):
                    if s + 1 < T:
                        turn(s + 1)
                    first = [x for x in rising if x[0] == s - 3]
                    before = sum(x[0] < s - 3 for x in rising)
                    if s >= 3:
                        pe.wait_ge(stack_sb, (b * T + s - 3) * 4 + 4)
                    per = len(first) // GROUP
                    for n in range(GROUP):
                        if 2 <= s < T + 2:
                            stack(s - 2, n)
                        if n == 1 and s < T:
                            project_v(s)
                        if n >= 1:
                            scores(0, first[(n - 1) * per:n * per], before + (n - 1) * per)
                    scores(0, first[3 * per:], before + 3 * per)
                    if s < T:
                        project_qk(s)

                def again(g, n):
                    if n == 0:
                        pe.wait_ge(max_ready, b * GROUPS + g + 1)
                    if n == 2:
                        pe.wait_ge(again_dve, (b * GROUPS + g) * 2 + 1)
                    if n == 3:
                        pe.wait_ge(again_act, (b * GROUPS + g) * 2 + 1)
                    h = g * GROUP + 2 * (n // 2)
                    for k in range(4):
                        last = nc.tensor.transpose(ps_m[:, n % 2, k * P:(k + 1) * P],
                                                   q_tok[:, (n % 2) * 4 + k, h:h + 2, :].bitcast(F32).rearrange(
                                                       "p h c -> p (h c)"), ident)
                    last.then_inc(again_ps, 1)

                def shifted(g, j, u):
                    h, n = g * GROUP + u, j * GROUP + u
                    rows = slice(64 * (h % 2), 64 * (h % 2) + 64)
                    if j == 0 and u % 2 == 0:
                        pe.wait_ge(again_dve, (b * GROUPS + g) * 2 + u // 2 + 1)
                        pe.wait_ge(again_act, (b * GROUPS + g) * 2 + u // 2 + 1)
                    pe.wait_ge(exp_done, (b * GROUPS + g) * UNITS + n + 1)
                    for c in range(j // HALF, 2):
                        q0 = max(j * P, 512 * c)
                        diag = q0 == j * P
                        last = nc.tensor.matmul(ps_e[:, n % 2, c, q0 - 512 * c:512], k_st[rows, h // 2, j * P:(j + 1) * P],
                                                q_st[rows, h // 2, q0:512 * (c + 1)], start=True, stop=not diag)
                        if diag:
                            last = nc.tensor.matmul(ps_e[:, n % 2, c, q0 - 512 * c:q0 - 512 * c + P], ident_b[:],
                                                    mask_b[:, 1], start=False, stop=True)
                    last.then_inc(shifted_ps, 1)

                def weigh(S, parts, last):
                    g, j = S // T, S % T
                    pe.wait_ge(exp_done, b * GROUPS * UNITS + (S + 1) * GROUP + 2)
                    if j == 0 and g >= 1:
                        pe.wait_ge(normed, b * GROUPS + g)
                    for i0, i1 in parts:
                        c = i0 // HALF
                        for u in range(GROUP):
                            done = nc.tensor.matmul(ps_a[32 * u:32 * u + 32, c, i0 * P - 512 * c:i1 * P - 512 * c],
                                                    vals[:, j, 17 * (g * GROUP + u):17 * (g * GROUP + u) + 32],
                                                    probs[:, (S * GROUP + u) % RING, i0 * P:i1 * P],
                                                    start=(j == 0), stop=(j == HALF * c + HALF - 1),
                                                    tile_position=(0, 32 * u))
                    if last:
                        done.then_inc(pv_done, 1)

                def turn_acc(g):
                    pe.wait_ge(acc_sb, b * GROUPS + g + 1)
                    for t in range(T):
                        last = nc.tensor.transpose(ps_a[:, t // 4, (t % 4) * P:(t % 4 + 1) * P],
                                                   acc[:, t * P:(t + 1) * P], ident)
                    last.then_inc(acc_t, 1)

                pe.wait_ge(rot_ready, b * T + T)
                for _ in range(WARM_UP):
                    nc.tensor.matmul(ps_e[:, 0, 0, :].rearrange("p (h l) -> p h l", l=P), ident_b[:],
                                     mask_b[:, 0].unsqueeze(1).to_broadcast([P, 4, P]), start=True, stop=True)
                for n in range(4):
                    again(0, n)
                for S in range(GROUPS * T):
                    g, j = S // T, S % T
                    for u in range(GROUP):
                        n = j * GROUP + u
                        shifted(g, j, u)
                        if S >= 1:
                            parts = pieces((S - 1) % T)
                            if parts[u]:
                                weigh(S - 1, parts[u], not any(parts[u + 1:]))
                        if g >= 1 and n == 3:
                            turn_acc(g - 1)
                        if g + 1 < GROUPS:
                            if n == FIRST:
                                pe.wait_ge(again_dve, (b * GROUPS + g) * 2 + 2)
                                pe.wait_ge(again_act, (b * GROUPS + g) * 2 + 2)
                            scores(g + 1, falling[issued[n]:issued[n + 1]], issued[n])
                            if j == T - 1:
                                again(g + 1, u)
                weigh(GROUPS * T - 1, [(T - 1, T)], True)
                turn_acc(GROUPS - 1)
                low_rank(b + 1, 0)
                low_rank(b + 1, 1)
                pe.wait_ge(normed, b * GROUPS + GROUPS)

                def turn_out(t):
                    if t >= 2:
                        pe.wait_ge(ot_sb, b * T + t - 1)
                    for d in range(DT):
                        last = nc.tensor.transpose(ps_a[:, t % 2, d * P:(d + 1) * P], heads_out[:, t, d * P:(d + 1) * P],
                                                   ident)
                    last.then_inc(ot_ps, 1)

                turn_out(0)
                for t in range(T):
                    if t + 1 < T:
                        turn_out(t + 1)
                    pe.wait_ge(ot_sb, b * T + t + 1)
                    if t >= 2:
                        pe.wait_ge(x_added, b * T + t)
                    if t in (2, 4):
                        low_rank(b + 1, 1 + t // 2)
                    for d in range(DT):
                        last = nc.tensor.matmul(ps_e[:, t % 2, 0, 0:D], ho_t[:, t % 2, d * P:(d + 1) * P],
                                                w_eff[:, d, 3], start=(d == 0), stop=(d == DT - 1))
                    last.then_inc(proj_ps, 1)


def routed_ffn(nc, X, C, F, name):
    FT = FF // P
    SPLIT = 3 * 512
    with ExitStack() as ctx:
        def sb(n, shape, dt=F32):
            return ctx.enter_context(nc.sbuf_tensor(name + n, shape, dt))

        def sem(n):
            return C["sems"]("f_" + n)

        ps_g = ctx.enter_context(nc.psum_tensor(name + "ps_g", [P, 2, 512], F32))
        ps_u = ctx.enter_context(nc.psum_tensor(name + "ps_u", [P, 2, 512], F32))
        ps_h = ctx.enter_context(nc.psum_tensor(name + "ps_h", [P, 2, 512], F32))
        ps_x = ctx.enter_context(nc.psum_tensor(name + "ps_x", [P, 512], F32))
        ps_y = ctx.enter_context(nc.psum_tensor(name + "ps_y", [P, 512], F32))

        w_gu = sb("w_gu", [P, EXPERTS, DT, 2, FF])
        w_hi = sb("w_hi", [P, EXPERTS, DT, SPLIT], F32R)
        w_d = sb("w_d", [P, EXPERTS, FT, D])
        w_r = sb("w_r", [P, DT, EXPERTS])
        b_r = sb("b_r", [P, EXPERTS])
        mean_var = sb("mean_var", [P, NT, 2])
        var_eps = sb("var_eps", [P, NT])
        rstd = sb("rstd", [P, NT])
        logits = sb("logits", [P, NT, EXPERTS])
        best = sb("best", [P, NT])
        expd = sb("expd", [P, NT, EXPERTS])
        top_w = sb("top_w", [P, NT])
        hot = sb("hot", [P, NT, EXPERTS])
        taken = sb("taken", [P, NT])
        hot_b = sb("hot_b", [P, NT, EXPERTS], BF16)
        before_b = sb("before_b", [P, P], BF16)
        ones_b = sb("ones_b", [P, P], BF16)
        ones = sb("ones", [P, NT])
        upto = sb("upto", [P, NT, EXPERTS])
        place = sb("place", [P, NT, EXPERTS])
        over = sb("over", [P, EXPERTS, NT])
        tiles = sb("tiles", [P, EXPERTS])
        first = sb("first", [P, EXPERTS])
        slot = sb("slot", [P, NT])
        slot_i = sb("slot_i", [P, NT], U32)
        owner = sb("owner", [P, 2, SLOTS])
        owner_i = sb("owner_i", [P, SLOTS], I32)
        xe = sb("xe", [P, D])
        xe_t = sb("xe_t", [P, D])
        xe_hi = sb("xe_hi", [P, D], F32R)
        xe_lo = sb("xe_lo", [P, D], F32R)
        gate = sb("gate", [P, FF])
        hid = sb("hid", [P, FF])
        hid_t = sb("hid_t", [P, FF])
        y = sb("y", [P, D])
        xn = hid[:].rearrange("p (a d) -> p a d", a=4)
        xn_t = hid_t[:].rearrange("p (a d) -> p a d", a=2)
        y_tok = gate[:].rearrange("p (a d) -> p a d", a=4)
        warm = sb("warm", [P, 1])
        warmed = sem("warmed")

        loaded, w_loaded, step_done, stats_ready, rstd_ready = (
            sem(n) for n in ("loaded", "w_loaded", "step_done", "stats_ready", "rstd_ready"))
        xn_ready, xt_ps, xt_sb, logit_ps, pair_used, shifted, exp_ready = (
            sem(n) for n in ("xn_ready", "xt_ps", "xt_sb", "logit_ps", "pair_used", "shifted", "exp_ready"))
        hot_ready, rank_ps, slot_ready, owner_ready, again_ready = (
            sem(n) for n in ("hot_ready", "rank_ps", "slot_ready", "owner_ready", "again_ready"))
        sent = [C["sems"](f"{name}sent{k}") for k in range(4)]
        fetched = [C["sems"](f"{name}fetched{k}") for k in range(4)]
        xe_loaded, xe_ps, xe_sb, gate_ps, gate_sb, up_ps, hid_ready = (
            sem(n) for n in ("xe_loaded", "xe_ps", "xe_sb", "gate_ps", "gate_sb", "up_ps", "hid_ready"))
        ht_ps, ht_lo, ht_hi, y_ps, y_sb, y_stored, added, zeroed = (
            sem(n) for n in ("ht_ps", "ht_lo", "ht_hi", "y_ps", "y_sb", "y_stored", "added", "zeroed"))

        hi_ready, split, xe_split, xe_copied, next_stats = (
            sem(n) for n in ("hi_ready", "split", "xe_split", "xe_copied", "next_stats"))

        def split_columns(e):
            return w_gu[:, e].rearrange("p t k f -> p t (k f)")[:, :, 0:SPLIT]

        x_slots, y_slots = F["x_slots"], F["y_slots"]
        W_LOADS = 3 * EXPERTS
        block = ctx.enter_context(nc.Block())

        @block.sync
        def _(sp):
            sp.dma_start(w_r[:], F["Wr"].rearrange("(t p) e -> p t e", p=P)).then_inc(loaded, 16)
            sp.dma_start(b_r[:], F["br"].rearrange("(a e) -> a e", a=1).to_broadcast([P, EXPERTS])).then_inc(loaded, 16)
            sp.wait_ge(zeroed, 1)
            sp.dma_start(x_slots.rearrange("(t p) d -> p t d", p=P),
                         y[:].unsqueeze(1).to_broadcast([P, SLOTS, D])).then_inc(zeroed, 16)
            for e in range(EXPERTS):
                for k, w in enumerate(("Wg", "Wu")):
                    sp.dma_start(w_gu[:, e, :, k], F[w][e].rearrange("(t p) f -> p t f", p=P)).then_inc(w_loaded, 16)
                sp.dma_start(w_d[:, e], F["Wd"][e].rearrange("(t p) d -> p t d", p=P)).then_inc(w_loaded, 16)
            for k in range(4):
                sp.wait_ge(sent[k], 16 * (NT // 4))
            sp.sem_inc(y_stored, 16)
            sp.dma_start(xe[:], x_slots[0:P, :]).then_inc(xe_loaded, 16)
            with sp.Fori(1, SLOTS) as j:
                sp.wait_ge(xe_ps, j)
                sp.dma_start(xe[:], x_slots[bass.ds(j * P, P), :]).then_inc(xe_loaded, 16)
            sp.wait_ge(y_stored, 16 * SLOTS + 16)

        @block.vector
        def _(dve):
            step = Steps(dve, step_done)
            nc.vector.memset(y[:], 0.0).then_inc(zeroed, 1)
            step(nc.vector.memset(ones_b[:], 1.0))
            step(nc.vector.memset(ones[:], 1.0))
            step(nc.vector.tensor_copy(before_b[:], C["before"]))
            row_stats(nc, step, [X[:, t, :] for t in range(NT)], C["stats"], mean_var, var_eps[:], stats_ready)
            dve.wait_ge(rstd_ready, 1)
            dve.wait_ge(loaded, 32)

            def norm(t):
                if t >= 4:
                    dve.wait_ge(xt_ps, t // 2 - 1)
                nc.vector.tensor_scalar(xn[:, t % 4], X[:, t, :], mean_var[:, t, 0:1], rstd[:, t:t + 1],
                                        ALU.subtract, ALU.mult).then_inc(xn_ready, 1)

            for t in range(NT):
                norm(t)
            dve.wait_ge(logit_ps, 1)
            step(nc.vector.tensor_tensor(logits[:], ps_y[:, 0:NT * EXPERTS].rearrange("p (t e) -> p t e", e=EXPERTS),
                                         b_r[:].unsqueeze(1).to_broadcast([P, NT, EXPERTS]), ALU.add))

            def all_experts(v):
                return v.unsqueeze(2).to_broadcast([P, NT, EXPERTS])

            step(nc.vector.tensor_reduce(best[:], logits[:], AX, ALU.max))
            nc.vector.tensor_tensor(logits[:], logits[:], all_experts(best[:]), ALU.subtract).then_inc(shifted, 1)
            dve.wait_ge(shifted, 1)
            step(nc.vector.tensor_scalar(hot[:], logits[:], 0.0, None, ALU.is_equal))
            step(nc.vector.tensor_copy(taken[:], hot[:, :, 0]))
            for e in range(1, EXPERTS):
                step(nc.vector.tensor_tensor(hot[:, :, e], hot[:, :, e], taken[:], ALU.is_gt))
                step(nc.vector.tensor_tensor(taken[:], hot[:, :, e], taken[:], ALU.add))
            nc.vector.tensor_copy(hot_b[:], hot[:]).then_inc(hot_ready, 1)
            dve.wait_ge(exp_ready, 1)
            step(nc.vector.tensor_reduce(best[:], expd[:], AX, ALU.add))
            step(nc.vector.reciprocal(top_w[:], best[:]))
            dve.wait_ge(rank_ps, 1)
            totals = ps_g[:, 1, 0:P].rearrange("p (t e) -> p t e", e=EXPERTS)
            for e in range(EXPERTS):
                step(nc.vector.tensor_tensor_scan(upto[:, :, e], ones[:], totals[:, :, e], 0.0, ALU.mult, ALU.add))
            step(nc.vector.tensor_tensor(place[:], upto[:], totals, ALU.subtract))
            step(nc.vector.tensor_tensor(place[:], place[:], ps_g[:, 0, 0:P].rearrange("p (t e) -> p t e", e=EXPERTS),
                                         ALU.add))
            step(nc.vector.tensor_tensor(over[:], upto[:, NT - 1, :].unsqueeze(2).to_broadcast([P, EXPERTS, NT]),
                                         C["tile_tokens"].unsqueeze(1).to_broadcast([P, EXPERTS, NT]), ALU.is_gt))
            step(nc.vector.tensor_reduce(tiles[:], over[:], AX, ALU.add))
            step(nc.vector.memset(first[:], 0.0))
            for e in range(1, EXPERTS):
                step(nc.vector.tensor_tensor(first[:, e:e + 1], first[:, e - 1:e], tiles[:, e - 1:e], ALU.add))
            for e in range(EXPERTS):
                step(nc.vector.tensor_scalar(over[:, e, 0:1], first[:, e:e + 1], float(P), None, ALU.mult))
                step(nc.vector.tensor_scalar(place[:, :, e], place[:, :, e], over[:, e, 0:1], None, ALU.add))
            step(nc.vector.tensor_tensor(place[:], place[:], hot[:], ALU.mult))
            step(nc.vector.tensor_reduce(slot[:], place[:], AX, ALU.add))
            nc.vector.tensor_copy(slot_i[:], slot[:]).then_inc(slot_ready, 1)
            step(nc.vector.tensor_scalar(owner[:, 0, :], C["slot_no"], first[:, 1:2], None, ALU.is_ge))
            for e in range(2, EXPERTS):
                step(nc.vector.tensor_scalar(owner[:, 1, :], C["slot_no"], first[:, e:e + 1], None, ALU.is_ge))
                step(nc.vector.tensor_tensor(owner[:, 0, :], owner[:, 0, :], owner[:, 1, :], ALU.add))
            nc.vector.tensor_copy(owner_i[:], owner[:, 0, :]).then_inc(owner_ready, 1)
            for t in range(NT):
                if t >= 4:
                    dve.wait_ge(sent[t % 4], 16 * (t // 4))
                nc.vector.tensor_scalar(xn[:, t % 4], X[:, t, :], mean_var[:, t, 0:1], rstd[:, t:t + 1],
                                        ALU.subtract, ALU.mult).then_inc(again_ready, 1)
                if t % 4 == 3:
                    e, d = t // 8, t // 4 % 2
                    dve.wait_ge(hi_ready, e + 1)
                    nc.vector.tensor_tensor(split_columns(e)[:, d].bitcast(F32R), split_columns(e)[:, d],
                                            w_hi[:, e, d].bitcast(F32), ALU.subtract).then_inc(split, 1)

            def take(j):
                dve.wait_ge(xe_ps, j + 1)
                nc.vector.tensor_copy(xe_hi[:], ps_x[:, 0:D]).then_inc(xe_sb, 1)
                dve.wait_ge(xe_sb, j + 1)
                nc.vector.tensor_tensor(xe_lo[:], ps_x[:, 0:D], xe_hi[:].bitcast(F32), ALU.subtract
                                        ).then_inc(xe_split, 1)

            def combine(j):
                dve.wait_ge(up_ps, j + 1)
                dve.wait_ge(gate_sb, j + 1)
                nc.vector.tensor_tensor(hid[:], gate[:], ps_u[:].rearrange("p b f -> p (b f)"), ALU.mult
                                        ).then_inc(hid_ready, 1)

            def hidden(j):
                dve.wait_ge(ht_ps, j + 1)
                nc.vector.tensor_copy(hid_t[:, 0:512], ps_h[:, 0]).then_inc(ht_lo, 1)

            take(0)
            with dve.Fori(0, SLOTS - 1) as j:
                combine(j)
                take(j + 1)
                hidden(j)
            combine(SLOTS - 1)
            hidden(SLOTS - 1)
            for t in range(NT):
                dve.wait_ge(fetched[t % 4], 16 * (t // 4 + 1))
                nc.vector.scalar_tensor_tensor(X[:, t, :], y_tok[:, t % 4], top_w[:, t:t + 1], X[:, t, :], ALU.mult,
                                               ALU.add).then_inc(added, 1)
                dve.wait_ge(added, t + 1)
                nc.vector.bn_stats(C["stats"][:, t], X[:, t, :]).then_inc(next_stats, 1)
            dve.wait_ge(next_stats, NT)

        @block.gpsimd
        def _(pool):
            pool.wait_ge(stats_ready, 1)
            inverse_root(nc, rstd[:], var_eps[:], C).then_inc(rstd_ready, 1)
            pool.wait_ge(zeroed, 17)
            pool.wait_ge(slot_ready, 1)
            for t in range(NT):
                pool.wait_ge(again_ready, t + 1)
                nc.gpsimd.indirect_dma_start(
                    out=x_slots, out_offset=bass.IndirectOffsetOnAxis(ap=slot_i[:, t:t + 1], axis=0),
                    in_=xn[:, t % 4], in_offset=None).then_inc(sent[t % 4], 16)
            pool.wait_ge(y_stored, 16 * SLOTS + 16)
            for t in range(NT):
                if t >= 4:
                    pool.wait_ge(added, t - 3)
                nc.gpsimd.indirect_dma_start(
                    out=y_tok[:, t % 4], out_offset=None, in_=y_slots,
                    in_offset=bass.IndirectOffsetOnAxis(ap=slot_i[:, t:t + 1], axis=0)).then_inc(fetched[t % 4], 16)
            for k in range(4):
                pool.wait_ge(fetched[k], 16 * (NT // 4))

        @block.scalar
        def _(act):
            for k in range(NT // 2):
                act.wait_ge(xt_ps, k + 1)
                if k >= 2:
                    act.wait_ge(pair_used, k - 1)
                nc.scalar.copy(xn_t[:, k % 2], ps_u[:, k % 2]).then_inc(xt_sb, 1)
            act.wait_ge(shifted, 1)
            nc.scalar.activation(expd[:], logits[:], ACT.Exp).then_inc(exp_ready, 1)

            for e in range(EXPERTS):
                act.wait_ge(w_loaded, 16 * W_LOADS)
                nc.scalar.copy(w_hi[:, e], split_columns(e)).then_inc(hi_ready, 1)

            def take(j):
                act.wait_ge(xe_split, j + 1)
                nc.scalar.copy(xe_t[:], ps_x[:, 0:D]).then_inc(xe_copied, 1)

            def activate(j):
                act.wait_ge(gate_ps, j + 1)
                nc.scalar.activation(gate[:], ps_g[:].rearrange("p b f -> p (b f)"), ACT.Silu).then_inc(gate_sb, 1)

            def hidden(j):
                act.wait_ge(ht_ps, j + 1)
                nc.scalar.copy(hid_t[:, 512:1024], ps_h[:, 1]).then_inc(ht_hi, 1)

            def result(j):
                act.wait_ge(y_ps, j + 1)
                act.wait_ge(y_stored, j * 16 + 16)
                nc.scalar.copy(y[:], ps_y[:, 0:D]).then_inc(y_sb, 1)
                act.wait_ge(y_sb, j + 1)
                act.dma_start(y_slots[bass.ds(j * P, P), :], y[:]).then_inc(y_stored, 16)

            take(0)
            activate(0)
            take(1)
            hidden(0)
            with act.Fori(1, SLOTS - 1) as j:
                nc.scalar.activation(warm[:], ones[:, 0:1], ACT.Silu).then_inc(warmed, 1)
                act.wait_ge(warmed, j)
                activate(j)
                result(j - 1)
                take(j + 1)
                hidden(j)
            nc.scalar.activation(warm[:], ones[:, 0:1], ACT.Silu).then_inc(warmed, 1)
            activate(SLOTS - 1)
            result(SLOTS - 2)
            hidden(SLOTS - 1)
            result(SLOTS - 1)

        @block.tensor
        def _(pe):
            ident = C["ident"]

            def turn_pair(k):
                pe.wait_ge(xn_ready, 2 * k + 2)
                if k >= 2:
                    pe.wait_ge(xt_sb, k - 1)
                for n in range(2 * DT):
                    last = nc.tensor.transpose(ps_u[:, k % 2, n * P:(n + 1) * P],
                                               xn[:, 2 * (k % 2) + n // DT, (n % DT) * P:(n % DT + 1) * P], ident)
                last.then_inc(xt_ps, 1)

            def route(k):
                pe.wait_ge(xt_sb, k + 1)
                for n in range(2 * DT):
                    t, d = 2 * k + n // DT, n % DT
                    last = nc.tensor.matmul(ps_y[:, t * EXPERTS:(t + 1) * EXPERTS], xn_t[:, k % 2, n * P:(n + 1) * P],
                                            w_r[:, d], start=(d == 0), stop=(d == DT - 1))
                last.then_inc(logit_ps if k == NT // 2 - 1 else pair_used, 1)

            turn_pair(0)
            for k in range(NT // 2):
                if k + 1 < NT // 2:
                    turn_pair(k + 1)
                route(k)
            pe.wait_ge(hot_ready, 1)
            oh = hot_b[:].rearrange("p t e -> p (t e)")
            nc.tensor.matmul(ps_g[:, 0, 0:P], before_b[:], oh, start=True, stop=True)
            nc.tensor.matmul(ps_g[:, 1, 0:P], ones_b[:], oh, start=True, stop=True).then_inc(rank_ps, 1)
            pe.wait_ge(owner_ready, 1)
            pe.wait_ge(w_loaded, 16 * W_LOADS)
            pe.wait_ge(split, EXPERTS * DT)

            def turn(j, turned_before=True):
                pe.wait_ge(xe_loaded, j * 16 + 16)
                if turned_before:
                    pe.wait_ge(xe_copied, j)
                for d in range(DT):
                    last = nc.tensor.transpose(ps_x[:, d * P:(d + 1) * P], xe[:, d * P:(d + 1) * P], ident)
                last.then_inc(xe_ps, 1)

            def up(j, e):
                pe.wait_ge(xe_sb, j + 1)
                for k, ps, done in ((0, ps_g, gate_ps), (1, ps_u, up_ps)):
                    for c in range(FF // 512):
                        col = k * FF + c * 512
                        native = w_gu[:, bass.ds(e, 1), :, k, c * 512:(c + 1) * 512]
                        if col < SPLIT:
                            high = w_hi[:, bass.ds(e, 1), :, col:col + 512]
                            terms = [(xe_hi, high), (xe_hi, native.bitcast(F32R)), (xe_lo, high)]
                        else:
                            pe.wait_ge(xe_copied, j + 1)
                            terms = [(xe_t, native)]
                        for n, (x, w) in enumerate(terms):
                            if x is xe_lo and col == 0:
                                pe.wait_ge(xe_split, j + 1)
                            for d in range(DT):
                                last = nc.tensor.matmul(ps[:, c], x[:, d * P:(d + 1) * P],
                                                        w[:, :, d].rearrange("p a f -> p (a f)"),
                                                        start=(n == d == 0), stop=(n == len(terms) - 1 and d == DT - 1))
                    last.then_inc(done, 1)

            def down(j, e):
                pe.wait_ge(ht_lo, j + 1)
                pe.wait_ge(ht_hi, j + 1)
                for f in range(FT):
                    last = nc.tensor.matmul(ps_y[:, 0:D], hid_t[:, f * P:(f + 1) * P],
                                            w_d[:, bass.ds(e, 1), f].rearrange("p a d -> p (a d)"), start=(f == 0),
                                            stop=(f == FT - 1))
                last.then_inc(y_ps, 1)

            def turn_hidden(j):
                pe.wait_ge(hid_ready, j + 1)
                for f in range(FT):
                    last = nc.tensor.transpose(ps_h[:, f // 4, (f % 4) * P:(f % 4 + 1) * P], hid[:, f * P:(f + 1) * P],
                                               ident)
                last.then_inc(ht_ps, 1)

            def expert_of(j):
                return pe.value_load(owner_i[0:1, bass.ds(j, 1)], min_val=0, max_val=EXPERTS - 1)

            turn(0, False)
            up(0, expert_of(0))
            turn(1)
            turn_hidden(0)
            with pe.Fori(1, SLOTS - 1) as j:
                up(j, expert_of(j))
                down(j - 1, expert_of(j - 1))
                turn(j + 1)
                turn_hidden(j)
            up(SLOTS - 1, expert_of(SLOTS - 1))
            down(SLOTS - 2, expert_of(SLOTS - 2))
            turn_hidden(SLOTS - 1)
            down(SLOTS - 1, expert_of(SLOTS - 1))
            pe.wait_ge(y_sb, SLOTS)



def mamba(nc, X, C, M):
    ZT = INNER // P
    with ExitStack() as ctx:
        def sb(n, shape, dt=F32):
            return ctx.enter_context(nc.sbuf_tensor("m_" + n, shape, dt))

        def sem(n):
            return C["sems"]("m_" + n)

        def ps(n, banks=1):
            return ctx.enter_context(nc.psum_tensor("m_ps_" + n, [P, banks, 512], F32))

        ps_r, ps_t, ps_b, ps_y, ps_o, ps_s, ps_z = ps("r", 2), ps("t"), ps("b"), ps("y"), ps("o"), ps("s"), ps("z")

        w_in = sb("w_in", [P, DT, IN_PROJ])
        w_out = sb("w_out", [P, ZT, D])
        norm_w = sb("norm_w", [P, ZT])
        conv_w = sb("conv_w", [P, CT, TAPS])
        conv_b = sb("conv_b", [P, CT])
        dt_bias = sb("dt_bias", [P, MHEADS])
        a_neg = sb("a_neg", [P, 2, MHEADS])
        skip = sb("skip", [P, MHEADS])
        ident_b = sb("ident_b", [P, P], BF16)
        neg_b = sb("neg_b", [P, P], BF16)
        ones = sb("ones", [P, P])
        mean_var = sb("mean_var", [P, NT, 2])
        var_eps = sb("var_eps", [P, NT])
        rstd = sb("rstd", [P, NT])
        xn = sb("xn", [P, 2, D])
        xn_t = sb("xn_t", [P, DT, SEQ])
        pre = sb("pre", [P, 2, SEQ + TAPS - 1])
        conv = sb("conv", [P, 2, SEQ])
        xbc = sb("xbc", [P, CT, SEQ])
        z_act = sb("z_act", [P, T, INNER])
        dtv = sb("dtv", [P, 6, T, MHEADS])
        dt = sb("dt", [P, T, MHEADS])
        dta = sb("dta", [P, T, MHEADS])
        acs = sb("acs", [P, 2, T, MHEADS])
        neg_acs = sb("neg_acs", [P, T, MHEADS])
        e_acs = sb("e_acs", [P, T, MHEADS])
        e_rest = sb("e_rest", [P, T, MHEADS])
        e_all = sb("e_all", [P, T, MHEADS])
        decay = sb("decay", [P, MHEADS, P])
        mix = sb("mix", [P, MHEADS, P])
        b_tok = sb("b_tok", [P, P])
        xdt = sb("xdt", [P, MHEADS, HDIM])
        xskip = sb("xskip", [P, 2, MHEADS, HDIM])
        xds = sb("xds", [P, MHEADS, HDIM])
        state = sb("state", [P, MHEADS, HDIM])
        y = sb("y", [P, 2, MHEADS, HDIM])
        y_t = sb("y_t", [P, INNER])
        square = sb("square", [P, INNER])
        sum_sq = sb("sum_sq", [P, 1])
        mean_sq = sb("mean_sq", [P, 1])
        rms = sb("rms", [P, 1])

        loaded, fixed, step_done, act_fixed, stats_ready, rstd_ready, stats_step = (
            sem(n) for n in ("loaded", "fixed", "step_done", "act_fixed", "stats_ready", "rstd_ready", "stats_step"))
        xn_ready, xn_added, xt_ps, xt_sb, conv_ps, pre_ready, conv_ready, xbc_ready = (
            sem(n) for n in ("xn_ready", "xn_added", "xt_ps", "xt_sb", "conv_ps", "pre_ready", "conv_ready", "xbc_ready"))
        z_ps, z_ready, dt_ps, dt_step, dt_exp, dta_ready, sums_ps, sums_ready, exps_ready = (
            sem(n) for n in ("z_ps", "z_ready", "dt_ps", "dt_step", "dt_exp", "dta_ready", "sums_ps", "sums_ready",
                             "exps_ready"))
        turned_ps, gram_ps, decay_ps, b_ready, decay_ready, mix_ready, xdt_ready, xds_ready = (
            sem(n) for n in ("turned_ps", "gram_ps", "decay_ps", "b_ready", "decay_ready", "mix_ready", "xdt_ready",
                             "xds_ready"))
        diag_ps, off_ps, state_ps, state_ready, y_sum, gate_step, y_ready, sq_ready, mean_ready, rms_ready = (
            sem(n) for n in ("diag_ps", "off_ps", "state_ps", "state_ready", "y_sum", "gate_step", "y_ready",
                             "sq_ready", "mean_ready", "rms_ready"))
        yt_ps, yt_sb, out_ps, x_added, off_used = (sem(n) for n in ("yt_ps", "yt_sb", "out_ps", "x_added", "off_used"))

        block = ctx.enter_context(nc.Block())

        def spread(v):
            return v.rearrange("(a h) -> a h", a=1).to_broadcast([P, MHEADS])

        @block.sync
        def _(sp):
            sp.dma_start(w_in[:], M["w_in"].rearrange("(t p) e -> p t e", p=P)).then_inc(loaded, 16)
            sp.dma_start(w_out[:], M["w_out"].rearrange("(t p) d -> p t d", p=P)).then_inc(loaded, 16)
            with nc.allow_non_contiguous_dma(reason="a few hundred words of parameters"):
                sp.dma_start(norm_w[:], M["norm_w"].rearrange("(t p) -> p t", p=P)).then_inc(loaded, 16)
                sp.dma_start(conv_b[:], M["conv_b"].rearrange("(t p) -> p t", p=P)).then_inc(loaded, 16)
                sp.dma_start(conv_w[:], M["conv_w"].rearrange("(t p) k -> p t k", p=P)).then_inc(loaded, 16)
            sp.dma_start(dt_bias[:], spread(M["dt_bias"])).then_inc(loaded, 16)
            sp.dma_start(a_neg[:, 0], spread(M["A_log"])).then_inc(loaded, 16)
            sp.dma_start(skip[:], spread(M["D"])).then_inc(loaded, 16)
            sp.wait_ge(loaded, 16 * 8)

        def heads(v):
            return v.unsqueeze(2).to_broadcast([P, MHEADS, HDIM])

        def by_head(v):
            return v.rearrange("p (h f) -> p h f", h=MHEADS)

        def x_tile(b, t):
            return X[:, bass.ds(b * T + t, 1), :].rearrange("p a d -> p (a d)")

        ORDER = [4, 5, 0, 1, 2, 3]
        Z_TILES = [(0,), (1,), (2,), (3, 4), (5,), (6, 7)]

        @block.vector
        def _(dve):
            row_stats(nc, Steps(dve, stats_step), [], C["stats"], mean_var, var_eps[:], stats_ready)
            dve.wait_ge(loaded, 16 * 8)
            step = Steps(dve, fixed)
            step(nc.vector.tensor_copy(ident_b[:], C["ident"]))
            step(nc.vector.tensor_copy(neg_b[:], C["neg"][:, 1]))
            step(nc.vector.memset(ones[:], 1.0))
            step(nc.vector.memset(pre[:], 0.0))
            for k in range(ZT):
                step(nc.vector.tensor_scalar(w_out[:, k], w_out[:, k], norm_w[:, k:k + 1], None, ALU.mult))
            dve.wait_ge(act_fixed, 1)
            step(nc.vector.tensor_scalar(a_neg[:, 1], a_neg[:, 1], -1.0, None, ALU.mult))
            dve.sem_inc(x_added, 1)
            dve.wait_ge(rstd_ready, 1)
            NSTEP = CT * (TAPS - 2) + 7 + 2 + T
            with dve.Fori(0, BATCH) as b:
                step = Steps(dve, step_done, b * NSTEP)
                for t in range(T):
                    if t >= 2:
                        dve.wait_ge(xt_ps, b * T + t - 1)
                        dve.wait_ge(xn_added, b * T + t - 1)
                    nc.vector.tensor_scalar(xn[:, t % 2], x_tile(b, t), mean_var[:, bass.ds(b * T + t, 1), 0],
                                            rstd[:, bass.ds(b * T + t, 1)], ALU.subtract, ALU.mult
                                            ).then_inc(xn_ready, 1)

                def taps(n):
                    c = ORDER[n]
                    dve.wait_ge(pre_ready, b * 2 * CT + 2 * n + 2)
                    x, a = pre[:, n % 2], conv[:, n % 2]
                    for k in (2, 1):
                        step(nc.vector.scalar_tensor_tensor(a, x[:, k:k + SEQ], conv_w[:, c, k:k + 1], a, ALU.mult,
                                                            ALU.add))
                    nc.vector.scalar_tensor_tensor(a, x[:, 0:SEQ], conv_w[:, c, 0:1], a, ALU.mult, ALU.add
                                                   ).then_inc(conv_ready, 1)

                v, e, u, r, q = (dtv[:, k] for k in range(5))

                def flat(w):
                    return w.rearrange("p t h -> p (t h)")

                dve.wait_ge(dt_ps, b + 1)
                step(nc.vector.tensor_tensor(v, ps_b[:, 0, 0:T * MHEADS].rearrange("p (t h) -> p t h", h=MHEADS),
                                             dt_bias[:].unsqueeze(1).to_broadcast([P, T, MHEADS]), ALU.add))
                nc.vector.scalar_tensor_tensor(flat(e), flat(v), -1.0, flat(v), ALU.mult, ALU.max).then_inc(dt_step, 1)
                dve.wait_ge(dt_exp, b * 2 + 1)
                nc.vector.tensor_scalar(u, e, 1.0, None, ALU.add).then_inc(dt_step, 1)
                dve.wait_ge(dt_step, b * 2 + 2)
                step(nc.vector.tensor_scalar(r, u, -1.0, None, ALU.add))
                step(nc.vector.tensor_tensor(r, e, r, ALU.subtract))
                step(nc.vector.reciprocal(q, u))
                step(nc.vector.tensor_tensor(r, r, q, ALU.mult))
                dve.wait_ge(dt_exp, b * 2 + 2)
                step(nc.vector.tensor_tensor(r, r, dtv[:, 5], ALU.add))
                step(nc.vector.scalar_tensor_tensor(flat(dt[:]), flat(v), 0.0, flat(r), ALU.max, ALU.add))
                nc.vector.tensor_tensor(dta[:], dt[:], a_neg[:, 1].unsqueeze(1).to_broadcast([P, T, MHEADS]), ALU.mult
                                        ).then_inc(dta_ready, 1)
                taps(0)
                dve.wait_ge(sums_ps, b + 1)
                two = ps_t[:, 0, 0:2 * T * MHEADS].rearrange("p (a t h) -> p a t h", a=2, t=T)
                step(nc.vector.tensor_copy(acs[:, 0], two[:, 0]))
                step(nc.vector.tensor_scalar(neg_acs[:], acs[:, 0], -1.0, None, ALU.mult))
                nc.vector.tensor_tensor(acs[:, 1], two[:, 1], acs[:, 0], ALU.subtract).then_inc(sums_ready, 1)
                nc.vector.memset(state[:], 0.0).then_inc(state_ready, 1)
                for n in range(1, CT):
                    taps(n)

                def front(t):
                    N = b * T + t
                    dve.wait_ge(turned_ps, N + 1)
                    nc.vector.tensor_tensor(xdt[:], by_head(ps_t[:, 0]), heads(dt[:, t]), ALU.mult
                                            ).then_inc(xdt_ready, 1)
                    if t >= 2:
                        dve.wait_ge(gate_step, N - 1)
                    nc.vector.tensor_tensor(xskip[:, t % 2], by_head(ps_t[:, 0]), heads(skip[:]), ALU.mult
                                            ).then_inc(xdt_ready, 1)
                    dve.wait_ge(gram_ps, N + 1)
                    for k in range(2):
                        dve.wait_ge(decay_ready, 2 * N + k + 1)
                        nc.vector.tensor_tensor(mix[:, 4 * k:4 * k + 4], decay[:, 4 * k:4 * k + 4],
                                                ps_b[:, 0, 0:P].unsqueeze(1).to_broadcast([P, 4, P]), ALU.mult
                                                ).then_inc(mix_ready, 1)

                def middle(t):
                    N = b * T + t
                    dve.wait_ge(off_ps, N + 1)
                    if t >= 2:
                        dve.wait_ge(yt_ps, N - 1)
                        dve.wait_ge(sq_ready, N - 1)
                    nc.vector.tensor_tensor(y[:, t % 2], by_head(ps_o[:, 0]), heads(e_acs[:, t]), ALU.mult
                                            ).then_inc(off_used, 1)
                    step(nc.vector.tensor_tensor(state[:], state[:], heads(e_all[:, t]), ALU.mult))
                    dve.wait_ge(state_ps, N + 1)
                    nc.vector.tensor_tensor(state[:], state[:], by_head(ps_s[:, 0]), ALU.add).then_inc(state_ready, 1)
                    dve.wait_ge(off_used, N + 1)
                    dve.wait_ge(diag_ps, N + 1)
                    nc.vector.tensor_tensor(y[:, t % 2], y[:, t % 2], by_head(ps_y[:, 0]), ALU.add).then_inc(y_sum, 1)

                def mean(t):
                    N = b * T + t
                    dve.wait_ge(sq_ready, N + 1)
                    nc.vector.tensor_scalar(mean_sq[:], sum_sq[:], 1.0 / INNER, LN_EPS, ALU.mult, ALU.add
                                            ).then_inc(mean_ready, 1)

                def last(t):
                    N = b * T + t
                    dve.wait_ge(out_ps, N + 1)
                    dve.wait_ge(rms_ready, N + 1)
                    dve.wait_ge(xn_added, N + 1)
                    nc.vector.scalar_tensor_tensor(x_tile(b, t), ps_z[:, 0, 0:D], rms[:], x_tile(b, t), ALU.mult,
                                                   ALU.add).then_inc(x_added, 1)

                dve.wait_ge(exps_ready, b + 1)
                dve.wait_ge(state_ready, b * (T + 1) + 1)
                front(0)
                for t in range(T):
                    middle(t)
                    if t >= 1:
                        mean(t - 1)
                    if t + 1 < T:
                        front(t + 1)
                    if t >= 1:
                        last(t - 1)
                mean(T - 1)
                last(T - 1)
                dve.wait_ge(x_added, b * T + T + 1)
                assert step.n == NSTEP, (step.n, NSTEP)

        @block.gpsimd
        def _(pool):
            pool.wait_ge(stats_ready, 1)
            inverse_root(nc, rstd[:], var_eps[:], C).then_inc(rstd_ready, 1)
            with pool.Fori(0, BATCH) as b:
                for t in range(T):
                    pool.wait_ge(xn_ready, b * T + t + 1)
                    nc.gpsimd.tensor_tensor(x_tile(b, t), x_tile(b, t), xn[:, t % 2], ALU.add).then_inc(xn_added, 1)

                def weigh(t):
                    pool.wait_ge(xdt_ready, 2 * (b * T + t) + 1)
                    if t >= 1:
                        pool.wait_ge(state_ps, b * T + t)
                    nc.gpsimd.tensor_tensor(xds[:], xdt[:], heads(e_rest[:, t]), ALU.mult).then_inc(xds_ready, 1)

                def root(t):
                    N = b * T + t
                    pool.wait_ge(mean_ready, N + 1)
                    if t >= 1:
                        pool.wait_ge(x_added, N + 1)
                    inverse_root(nc, rms[:], mean_sq[:], C).then_inc(rms_ready, 1)

                pool.wait_ge(exps_ready, b + 1)
                pool.wait_ge(z_ready, b * T + T)
                weigh(0)
                for t in range(T):
                    N = b * T + t
                    if t >= 1:
                        root(t - 1)
                    pool.wait_ge(y_sum, N + 1)
                    pool.wait_ge(xdt_ready, 2 * N + 2)
                    nc.gpsimd.tensor_tensor(y[:, t % 2], y[:, t % 2], xskip[:, t % 2], ALU.add).then_inc(gate_step, 1)
                    pool.wait_ge(gate_step, N + 1)
                    nc.gpsimd.tensor_tensor(y[:, t % 2], y[:, t % 2], by_head(z_act[:, t]), ALU.mult).then_inc(y_ready, 1)
                    if t + 1 < T:
                        weigh(t + 1)
                root(T - 1)

        @block.scalar
        def _(act):
            act.wait_ge(loaded, 16 * 8)
            nc.scalar.activation(a_neg[:, 1], a_neg[:, 0], ACT.Exp).then_inc(act_fixed, 1)
            act.wait_ge(fixed, 4)
            with act.Fori(0, BATCH) as b:
                for t in range(T):
                    act.wait_ge(xt_ps, b * T + t + 1)
                    nc.scalar.copy(xn_t[:, :, t * P:(t + 1) * P],
                                   (ps_z, ps_s)[t % 2][:, 0, 0:D].rearrange("p (d k) -> p d k", d=DT)
                                   ).then_inc(xt_sb, 1)
                act.wait_ge(dt_step, b * 2 + 1)
                nc.scalar.activation(dtv[:, 1], dtv[:, 1], ACT.Exp, scale=-1.0).then_inc(dt_exp, 1)
                act.wait_ge(dt_step, b * 2 + 2)
                nc.scalar.activation(dtv[:, 5], dtv[:, 2], ACT.Ln).then_inc(dt_exp, 1)

                def channels(n):
                    c = ORDER[n]
                    for k, bank in enumerate((ps_y, ps_o)):
                        act.wait_ge(conv_ps, b * 2 * CT + 2 * n + k + 1)
                        if n >= 2 and k == 0:
                            act.wait_ge(conv_ready, b * CT + n - 1)
                            act.wait_ge(xbc_ready, b * CT + n - 1)
                        nc.scalar.copy(pre[:, n % 2, 3 + 512 * k:3 + 512 * (k + 1)], bank[:, 0])
                        nc.scalar.activation(conv[:, n % 2, 512 * k:512 * (k + 1)], bank[:, 0], ACT.Identity,
                                             scale=conv_w[:, c, 3:4], bias=conv_b[:, c:c + 1]).then_inc(pre_ready, 1)

                def channels_act(n):
                    act.wait_ge(conv_ready, b * CT + n + 1)
                    nc.scalar.activation(xbc[:, ORDER[n]], conv[:, n % 2], ACT.Silu).then_inc(xbc_ready, 1)

                def gates(t):
                    act.wait_ge(z_ps, b * T + t + 1)
                    nc.scalar.activation(z_act[:, t], ps_r[:, t % 2], ACT.Silu).then_inc(z_ready, 1)

                channels(0)
                channels(1)
                act.wait_ge(sums_ready, b + 1)
                nc.scalar.activation(e_acs[:], acs[:, 0], ACT.Exp)
                nc.scalar.activation(e_rest[:], acs[:, 1], ACT.Exp)
                nc.scalar.activation(e_all[:].rearrange("p t h -> p (t h)"), ps_t[:, 0, T * MHEADS:2 * T * MHEADS],
                                     ACT.Exp).then_inc(exps_ready, 1)
                for n in range(CT):
                    if n >= 2:
                        channels(n)
                    if n >= 1:
                        channels_act(n - 1)
                    for t in Z_TILES[n]:
                        if t >= 1:
                            gates(t - 1)
                channels_act(CT - 1)
                gates(T - 1)

                def front(t):
                    N = b * T + t
                    for k in range(2):
                        act.wait_ge(decay_ps, 2 * N + k + 1)
                        if t >= 1:
                            act.wait_ge(mix_ready, 2 * N + k - 1)
                        for h in range(4 * k, 4 * k + 4):
                            last = nc.scalar.activation(decay[:, h], ps_r[:, k, (h % 4) * P:(h % 4 + 1) * P], ACT.Exp,
                                                        bias=neg_acs[:, t, h:h + 1])
                        last.then_inc(decay_ready, 1)

                def keys(t):
                    N = b * T + t
                    act.wait_ge(turned_ps, N + 1)
                    if t >= 1:
                        act.wait_ge(state_ps, N)
                    nc.scalar.copy(b_tok[:], ps_b[:, 0, P:2 * P]).then_inc(b_ready, 1)

                def squares(t):
                    N = b * T + t
                    act.wait_ge(y_ready, N + 1)
                    if t >= 1:
                        act.wait_ge(mean_ready, N)
                    nc.scalar.activation(square[:], y[:, t % 2].rearrange("p h f -> p (h f)"), ACT.Square,
                                         accum_out=sum_sq[:]).then_inc(sq_ready, 1)

                def turned(t):
                    N = b * T + t
                    act.wait_ge(yt_ps, N + 1)
                    if t >= 1:
                        act.wait_ge(out_ps, N)
                    nc.scalar.copy(y_t[:], ps_y[:, 0]).then_inc(yt_sb, 1)

                keys(0)
                front(0)
                for t in range(T):
                    if t + 1 < T:
                        keys(t + 1)
                    if t >= 1:
                        squares(t - 1)
                        turned(t - 1)
                    if t + 1 < T:
                        front(t + 1)
                squares(T - 1)
                turned(T - 1)

        @block.tensor
        def _(pe):
            ident = C["ident"]
            pe.wait_ge(loaded, 16 * 8)
            pe.wait_ge(fixed, 4 + ZT + 1)
            with pe.Fori(0, BATCH) as b:
                pe.wait_ge(x_added, b * T + 1)
                for t in range(T):
                    pe.wait_ge(xn_ready, b * T + t + 1)
                    if t >= 2:
                        pe.wait_ge(xt_sb, b * T + t - 1)
                    for d in range(DT):
                        last = nc.tensor.transpose((ps_z, ps_s)[t % 2][:, 0, d * P:(d + 1) * P],
                                                   xn[:, t % 2, d * P:(d + 1) * P], ident)
                    last.then_inc(xt_ps, 1)
                pe.wait_ge(xt_sb, b * T + T)
                for t in range(T):
                    for d in range(DT):
                        last = nc.tensor.matmul(ps_b[:, 0, t * MHEADS:(t + 1) * MHEADS], xn_t[:, d, t * P:(t + 1) * P],
                                                w_in[:, d, INNER + CONV:], start=(d == 0), stop=(d == DT - 1))
                last.then_inc(dt_ps, 1)
                for n, c in enumerate(ORDER):
                    for k, bank in enumerate((ps_y, ps_o)):
                        if n >= 1:
                            pe.wait_ge(pre_ready, b * 2 * CT + 2 * n + k - 1)
                        for d in range(DT):
                            last = nc.tensor.matmul(bank[:, 0], w_in[:, d, INNER + c * P:INNER + (c + 1) * P],
                                                    xn_t[:, d, 512 * k:512 * (k + 1)], start=(d == 0),
                                                    stop=(d == DT - 1))
                        last.then_inc(conv_ps, 1)
                    for t in Z_TILES[n]:
                        if t >= 2:
                            pe.wait_ge(z_ready, b * T + t - 1)
                        for d in range(DT):
                            last = nc.tensor.matmul(ps_r[:, t % 2], xn_t[:, d, t * P:(t + 1) * P], w_in[:, d, 0:INNER],
                                                    start=(d == 0), stop=(d == DT - 1))
                        last.then_inc(z_ps, 1)
                    if n == 0:
                        pe.wait_ge(dta_ready, b + 1)
                        flat = dta[:].rearrange("p t h -> p (t h)")
                        nc.tensor.matmul(ps_t[:, 0, 0:T * MHEADS], C["upto"], flat, start=True, stop=True)
                        nc.tensor.matmul(ps_t[:, 0, T * MHEADS:2 * T * MHEADS], ones[:], flat, start=True, stop=True
                                         ).then_inc(sums_ps, 1)
                pe.wait_ge(exps_ready, b + 1)
                pe.wait_ge(z_ready, b * T + T)
                pe.wait_ge(xbc_ready, b * CT + CT)

                def tokens(t):
                    N, s = b * T + t, slice(t * P, (t + 1) * P)
                    if t >= 1:
                        pe.wait_ge(xdt_ready, 2 * N)
                        pe.wait_ge(mix_ready, 2 * N)
                    for k in range(ZT):
                        nc.tensor.transpose(ps_t[:, 0, k * P:(k + 1) * P], xbc[:, k, s], ident)
                    nc.tensor.transpose(ps_b[:, 0, P:2 * P], xbc[:, 4, s], ident).then_inc(turned_ps, 1)

                def gram(t):
                    N, s = b * T + t, slice(t * P, (t + 1) * P)
                    pe.wait_ge(b_ready, N + 1)
                    nc.tensor.matmul(ps_b[:, 0, 0:P], xbc[:, 4, s], xbc[:, 5, s], start=True, stop=True
                                     ).then_inc(gram_ps, 1)

                def decays(t):
                    N = b * T + t
                    for k in range(2):
                        if t >= 1:
                            pe.wait_ge(decay_ready, 2 * N + k - 1)
                        for h in range(4 * k, 4 * k + 4):
                            nc.tensor.matmul(ps_r[:, k, (h % 4) * P:(h % 4 + 1) * P],
                                             dta[:, t, h:h + 1].to_broadcast([P, P]), C["upto"], start=(h % 4 == 0),
                                             stop=False, skip_group_check=True)
                        nc.tensor.matmul(ps_r[:, k].rearrange("p (h l) -> p h l", l=P), ident_b[:],
                                         neg_b[:].unsqueeze(1).to_broadcast([P, 4, P]), start=False, stop=True,
                                         skip_group_check=True).then_inc(decay_ps, 1)

                def off(t):
                    N, s = b * T + t, slice(t * P, (t + 1) * P)
                    if t >= 1:
                        pe.wait_ge(off_used, N)
                    pe.wait_ge(state_ready, b * (T + 1) + t + 1)
                    nc.tensor.matmul(ps_o[:, 0], xbc[:, 5, s], state[:].rearrange("p h f -> p (h f)"), start=True,
                                     stop=True).then_inc(off_ps, 1)

                def turn_y(t):
                    N = b * T + t
                    pe.wait_ge(y_ready, N + 1)
                    pe.wait_ge(y_sum, b * T + min(t + 2, T))
                    flat_y = y[:, t % 2].rearrange("p h f -> p (h f)")
                    for k in range(ZT):
                        last = nc.tensor.transpose(ps_y[:, 0, k * P:(k + 1) * P], flat_y[:, k * P:(k + 1) * P], ident)
                    last.then_inc(yt_ps, 1)

                def output(t):
                    N = b * T + t
                    pe.wait_ge(yt_sb, N + 1)
                    pe.wait_ge(x_added, N + 1)
                    for k in range(ZT):
                        last = nc.tensor.matmul(ps_z[:, 0, 0:D], y_t[:, k * P:(k + 1) * P], w_out[:, k], start=(k == 0),
                                                stop=(k == ZT - 1))
                    last.then_inc(out_ps, 1)

                tokens(0)
                gram(0)
                decays(0)
                off(0)
                for t in range(T):
                    N = b * T + t
                    pe.wait_ge(xds_ready, N + 1)
                    nc.tensor.matmul(ps_s[:, 0], b_tok[:], xds[:].rearrange("p h f -> p (h f)"), start=True, stop=True
                                     ).then_inc(state_ps, 1)
                    if t >= 2:
                        pe.wait_ge(yt_sb, N - 1)
                    for h in range(MHEADS):
                        if h % 4 == 0:
                            pe.wait_ge(mix_ready, 2 * N + h // 4 + 1)
                        last = nc.tensor.matmul(ps_y[:, 0, h * HDIM:(h + 1) * HDIM], mix[:, h], xdt[:, h],
                                                start=(h == 0), stop=True, skip_group_check=True)
                    last.then_inc(diag_ps, 1)
                    if t + 1 < T:
                        tokens(t + 1)
                        off(t + 1)
                        gram(t + 1)
                    if t >= 1:
                        turn_y(t - 1)
                    if t + 1 < T:
                        decays(t + 1)
                    if t >= 1:
                        output(t - 1)
                turn_y(T - 1)
                output(T - 1)


def constants():
    i = np.arange(P)
    inv = (10000.0 ** (-np.arange(0, DH, 2) / DH)).astype(np.float32)
    ang = (np.arange(SEQ, dtype=np.float32)[:, None] * inv[None, :]).astype(np.float32)
    cos, sin = np.cos(ang), np.sin(ang)
    rope = np.stack([np.repeat(cos, 2, 1), np.stack([-sin, sin], -1).reshape(SEQ, DH)], 1).astype(np.float32)
    neg = np.stack([np.where(i[None, :] > i[:, None], MASKED, 0.0), np.where(i[None, :] < i[:, None], MASKED, 0.0)], 1)
    table = np.zeros((P, CONSTS), np.float32)
    table[:, 0:P] = np.eye(P)
    table[:, P:3 * P] = neg.reshape(P, 2 * P)
    table[:, 3 * P:4 * P] = (i[:, None] < i[None, :])
    table[:, 4 * P:5 * P] = (i[:, None] <= i[None, :])
    table[:, 5 * P] = i // RANK
    table[:, 5 * P + 1:5 * P + 1 + SLOTS] = np.arange(SLOTS)
    table[:, 5 * P + 1 + SLOTS:5 * P + 1 + SLOTS + NT] = P * np.arange(NT)
    table[:, CONSTS - 1] = -0.5
    return {"const_table": table, "const_rope": rope}


CONSTS = 5 * P + 1 + SLOTS + NT + 1


def program(nc, I, out, phases):
    with ExitStack() as ctx:
        X = ctx.enter_context(nc.sbuf_tensor("x_res", [P, NT, D], F32))
        table = ctx.enter_context(nc.sbuf_tensor("table", [P, CONSTS], F32))
        C = {
            "ident": table[:, 0:P],
            "neg": table[:, P:3 * P].rearrange("p (a k) -> p a k", a=2),
            "before": table[:, 3 * P:4 * P],
            "upto": table[:, 4 * P:5 * P],
            "minus_half": table[:, CONSTS - 1:CONSTS],
            "adapter": table[:, 5 * P:5 * P + 1],
            "slot_no": table[:, 5 * P + 1:5 * P + 1 + SLOTS],
            "tile_tokens": table[:, 5 * P + 1 + SLOTS:CONSTS - 1],
        }
        C["stats"] = ctx.enter_context(nc.sbuf_tensor("row_statistics", [P, NT, 6], F32))
        C["sems"] = Semaphores(nc, ctx)
        C["begun"] = begun = ctx.enter_context(nc.semaphore("begun"))

        def load_x(sp):
            x = I["L0_attn_a_x"].rearrange("b (t p) d -> p (b t) d", p=P)
            for b in range(BATCH):
                sp.dma_start(X[:, b * T:(b + 1) * T], x[:, b * T:(b + 1) * T]).then_inc(begun, 16)

        C["load_x"] = load_x
        with nc.Block() as block:
            @block.sync
            def _(sp):
                sp.dma_start(table[:], I["const_table"]).then_inc(begun, 16)
                sp.wait_ge(begun, 16)
        for phase in phases:
            phase(nc, X, C, I)
        stored = ctx.enter_context(nc.semaphore("stored"))
        with nc.Block() as block:
            @block.sync
            def _(sp):
                y = out.rearrange("b (t p) d -> p (b t) d", p=P)
                for b in range(BATCH):
                    sp.dma_start(y[:, b * T:(b + 1) * T], X[:, b * T:(b + 1) * T]).then_inc(stored, 16)
                sp.wait_ge(stored, 16 * BATCH)


def phase_attention(nc, X, C, I):
    A = {k: I["L0_attn_a_" + k] for k in ("Wq", "Wk", "Wv", "Wo", "Aq", "Ak", "Av", "Ao", "Bq", "Bk", "Bv", "Bo")}
    A["starts"], A["rope"] = I["L0_attn_a_lora_start_indices"], I["const_rope"]
    attention(nc, X, C, A)


def phase_ffn(which):
    def phase(nc, X, C, I):
        C["sems"].clear("f_")
        F = {k: I["L0_ffn_" + k] for k in ("Wr", "br", "Wg", "Wu", "Wd")}
        F["x_slots"] = nc.dram_tensor(which + "x_slots", (SLOTS * P, D), F32, kind="Internal").ap()
        F["y_slots"] = nc.dram_tensor(which + "y_slots", (SLOTS * P, D), F32, kind="Internal").ap()
        routed_ffn(nc, X, C, F, which)
    return phase


def phase_mamba(nc, X, C, I):
    mamba(nc, X, C, {k: I["L0_attn_b_" + k]
                     for k in ("w_in", "conv_w", "conv_b", "dt_bias", "A_log", "D", "norm_w", "w_out")})


PHASES = [phase_attention, phase_ffn("g1_"), phase_mamba, phase_ffn("g2_")]


def kernel(**inputs):
    import concourse.bacc as bacc
    from concourse.bass_utils import run_bass_kernel_spmd

    nc = bacc.Bacc("TRN2", target_bir_lowering=False, num_devices=1)
    arrays = {k: np.ascontiguousarray(v) for k, v in {**inputs, **constants()}.items()}
    I = {k: nc.dram_tensor(k, a.shape, mybir.dt.from_np(a.dtype), kind="ExternalInput").ap()
         for k, a in arrays.items()}
    out = nc.dram_tensor("out", (BATCH, SEQ, D), F32, kind="ExternalOutput").ap()
    program(nc, I, out, PHASES)
    return run_bass_kernel_spmd(nc, [arrays], core_ids=[0]).results[0]["out"]
```
